# Optimizing a Trainium2 kernel written in Bass

```python
import numpy as np
import jax
import jax.numpy as jnp

def _softmax(x, axis=-1):
    return jax.nn.softmax(x, axis=axis)

def _gelu(x):
    return jax.nn.gelu(x, approximate=True)

def _silu(x):
    return jax.nn.silu(x)

def _sigmoid(x):
    return jax.nn.sigmoid(x)

def _layernorm(x, axis=-1, eps=1e-05):
    m = jnp.mean(x, axis=axis, keepdims=True)
    v = jnp.var(x, axis=axis, keepdims=True)
    return (x - m) / jnp.sqrt(v + eps)

def _scatter_add(tgt, idx, src, axis=0):
    return tgt.at[idx].add(src)

def _segment_sum(src, seg, n):
    return jax.ops.segment_sum(src, seg, n)
kernel_name = 'mk_sandwich_d1_jaxref_r4_da796e'

def setup_inputs(seed: int=0):
    np.random.seed(seed)
    _w = jnp.asarray

    def _L0_attn_setup():
        import jax, jax.numpy as jnp
        import numpy as np
        N_HEAD = 16
        N_EMBED = 512
        N_BLOCK = 512
        THETA = 10000.0

        def _rope_cos_sin(n_head, head_dim):
            freqs = THETA ** (-(jnp.arange(0, head_dim, 2, dtype=jnp.float32) / head_dim))
            t = jnp.arange(n_head, dtype=jnp.float32)
            ang = jnp.outer(t, freqs)
            return (jnp.cos(ang)[None, :, None, :], jnp.sin(ang)[None, :, None, :])

        def _apply_rope(x, cos, sin):
            B, H, T, hd = x.shape
            xp = x.reshape(B, H, T, hd // 2, 2)
            a, b = (xp[..., 0], xp[..., 1])
            out = jnp.stack([a * cos - b * sin, a * sin + b * cos], axis=-1)
            return out.reshape(B, H, T, hd)
        key = jax.random.key(seed)
        ks = jax.random.split(key, 5)
        E = N_EMBED
        x = jax.random.normal(ks[0], (2, 512, E), dtype=jnp.float32)
        s = 1.0 / np.sqrt(E)
        w_attn = jax.random.normal(ks[1], (E, 3 * E), dtype=jnp.float32) * s
        b_attn = jnp.zeros((3 * E,), dtype=jnp.float32)
        w_proj = jax.random.normal(ks[2], (E, E), dtype=jnp.float32) * s
        b_proj = jnp.zeros((E,), dtype=jnp.float32)
        return {'x': x, 'w_attn': w_attn, 'b_attn': b_attn, 'w_proj': w_proj, 'b_proj': b_proj}
    _L0_attn_in = _L0_attn_setup()

    def _L0_ffn_setup():
        import jax, jax.numpy as jnp
        import numpy as np
        EPS = 1e-06
        Q_B = 128.0

        def layer_norm(x):
            mean = jnp.mean(x, axis=-1, keepdims=True)
            var = jnp.var(x, axis=-1, keepdims=True)
            return (x - mean) / jnp.sqrt(var + EPS)

        def absmax_quant(x):
            gamma = jnp.max(jnp.abs(x), axis=-1, keepdims=True)
            x_hat = jnp.clip(x * Q_B / gamma, -Q_B + EPS, Q_B - EPS)
            return x_hat * gamma / Q_B

        def ternarize_weights(w):
            gamma = jnp.mean(jnp.abs(w))
            return jnp.sign(jnp.round(w / (gamma + EPS))) * gamma

        def bitlinear(x, w):
            xn = layer_norm(x)
            x_hat = xn + jax.lax.stop_gradient(absmax_quant(xn) - xn)
            w_hat = w + jax.lax.stop_gradient(ternarize_weights(w) - w)
            return jnp.einsum('bsd,od->bso', x_hat, w_hat)
        key = jax.random.key(seed)
        k1, k2, k3 = jax.random.split(key, 3)
        B, S, D = (4, 512, 512)
        x = jax.random.normal(k1, (B, S, D), dtype=jnp.float32)
        w_fc = jax.random.normal(k2, (4 * D, D), dtype=jnp.float32) / np.sqrt(D)
        w_proj = jax.random.normal(k3, (D, 4 * D), dtype=jnp.float32) / np.sqrt(4 * D)
        return {'x': x, 'w_fc': w_fc, 'w_proj': w_proj}
    _L0_ffn_in = _L0_ffn_setup()
    _d = {'L0_attn_x': _L0_attn_in['x'], 'L0_attn_w_attn': _L0_attn_in['w_attn'], 'L0_attn_b_attn': _L0_attn_in['b_attn'], 'L0_attn_w_proj': _L0_attn_in['w_proj'], 'L0_attn_b_proj': _L0_attn_in['b_proj'], 'L0_ffn_w_fc': _L0_ffn_in['w_fc'], 'L0_ffn_w_proj': _L0_ffn_in['w_proj']}
    _x0 = _d['L0_attn_x']
    _d['L0_attn_x'] = jax.random.normal(jax.random.fold_in(jax.random.key(seed), 1), (8, 512, 512), dtype=_x0.dtype)
    del _x0
    return _d

def reference(L0_attn_x, L0_attn_w_attn, L0_attn_b_attn, L0_attn_w_proj, L0_attn_b_proj, L0_ffn_w_fc, L0_ffn_w_proj):

    def _L0_attn_ref(x, w_attn, b_attn, w_proj, b_proj):
        import jax, jax.numpy as jnp
        import numpy as np
        N_HEAD = 16
        N_EMBED = 512
        N_BLOCK = 512
        THETA = 10000.0

        def _rope_cos_sin(n_head, head_dim):
            freqs = THETA ** (-(jnp.arange(0, head_dim, 2, dtype=jnp.float32) / head_dim))
            t = jnp.arange(n_head, dtype=jnp.float32)
            ang = jnp.outer(t, freqs)
            return (jnp.cos(ang)[None, :, None, :], jnp.sin(ang)[None, :, None, :])

        def _apply_rope(x, cos, sin):
            B, H, T, hd = x.shape
            xp = x.reshape(B, H, T, hd // 2, 2)
            a, b = (xp[..., 0], xp[..., 1])
            out = jnp.stack([a * cos - b * sin, a * sin + b * cos], axis=-1)
            return out.reshape(B, H, T, hd)
        B, T, E = x.shape
        H = N_HEAD
        hd = E // H
        qkv = x @ w_attn + b_attn
        q, k, v = jnp.split(qkv, 3, axis=-1)
        q = q.reshape(B, T, H, hd).transpose(0, 2, 1, 3)
        k = k.reshape(B, T, H, hd).transpose(0, 2, 1, 3)
        v = v.reshape(B, T, H, hd).transpose(0, 2, 1, 3)
        cos, sin = _rope_cos_sin(H, hd)
        q = _apply_rope(q, cos, sin)
        k = _apply_rope(k, cos, sin)
        scores = jnp.einsum('bhtd,bhsd->bhts', q, k)
        causal = jnp.tril(jnp.ones((T, T), dtype=bool))
        scores = jnp.where(causal[None, None], scores, jnp.float32(-jnp.inf))
        attn = jax.nn.softmax(scores, axis=-1) * E ** (-0.5)
        o = jnp.einsum('bhts,bhsd->bhtd', attn, v)
        o = o.transpose(0, 2, 1, 3).reshape(B, T, E)
        return o @ w_proj + b_proj

    def _L0_ffn_ref(x, w_fc, w_proj):
        import jax, jax.numpy as jnp
        import numpy as np
        EPS = 1e-06
        Q_B = 128.0

        def layer_norm(x):
            mean = jnp.mean(x, axis=-1, keepdims=True)
            var = jnp.var(x, axis=-1, keepdims=True)
            return (x - mean) / jnp.sqrt(var + EPS)

        def absmax_quant(x):
            gamma = jnp.max(jnp.abs(x), axis=-1, keepdims=True)
            x_hat = jnp.clip(x * Q_B / gamma, -Q_B + EPS, Q_B - EPS)
            return x_hat * gamma / Q_B

        def ternarize_weights(w):
            gamma = jnp.mean(jnp.abs(w))
            return jnp.sign(jnp.round(w / (gamma + EPS))) * gamma

        def bitlinear(x, w):
            xn = layer_norm(x)
            x_hat = xn + jax.lax.stop_gradient(absmax_quant(xn) - xn)
            w_hat = w + jax.lax.stop_gradient(ternarize_weights(w) - w)
            return jnp.einsum('bsd,od->bso', x_hat, w_hat)
        h = bitlinear(x, w_fc)
        h = jax.nn.gelu(h, approximate=False)
        return bitlinear(h, w_proj)
    x = L0_attn_x
    x = x + _layernorm(_L0_attn_ref(_layernorm(x, axis=-1), L0_attn_w_attn, L0_attn_b_attn, L0_attn_w_proj, L0_attn_b_proj), axis=-1)
    x = x + _layernorm(_L0_ffn_ref(_layernorm(x, axis=-1), L0_ffn_w_fc, L0_ffn_w_proj), axis=-1)
    return x

_drawn_inputs = setup_inputs


def setup_inputs(seed=0):
    import zlib

    import numpy as np

    out = dict(_drawn_inputs(seed))
    spreads = {'L0_attn_b_attn': (0.0, 0.1), 'L0_attn_b_proj': (0.0, 0.1)}
    factors = {}
    for name, (base, spread) in spreads.items():
        noise = np.random.default_rng([zlib.crc32(name.encode()), seed]).standard_normal(out[name].shape)
        drawn = base * np.exp(spread * noise) if base else spread * noise
        out[name] = jnp.asarray(drawn.astype(out[name].dtype))
    for name, factor in factors.items():
        out[name] = (out[name] * factor).astype(out[name].dtype)
    return out
```

```python
import numpy as np
from contextlib import ExitStack

import concourse.bass as bass
from concourse import mybir

BATCHES, T, E, HEADS = 8, 512, 512, 16
HD = E // HEADS
F = 4 * E
PARTS = 128
TB = T // PARTS
EC = E // PARTS
FC = F // PARTS
VW = 2 * HD + 1
THETA = 10000.0

W_UP = 16.0
S_UP = W_UP * W_UP
ROW_UP = 2.0 ** 15
P_LIFT = 12 * float(np.log(2.0))
BIAS_UP = 16.0
ATTN_SCALE = float(E) ** -0.5
PROJ_K = ATTN_SCALE / S_UP
EPS_LN, EPS_BIT = 1e-5, 1e-6
NEG = -1.0e30

QK_AT = {1: (0, 0), 2: (0, 1), 3: (1, 0), 4: (1, 1), 7: (2, 0), 8: (2, 1), 11: (3, 0), 12: (3, 1)}
DOWN_AT = {0: [(1, 0)], 5: [(1, 1), (1, 2)], 6: [(1, 3)], 9: [(2, 0), (2, 1)], 10: [(2, 2), (2, 3)],
           13: [(3, 0), (3, 1)], 14: [(3, 2), (3, 3)]}
FINAL_AT = {6: 1, 10: 2, 14: 3}
FINISH_AT = {1: 0, 7: 1, 11: 2, 15: 3}
W2_FROM = 8
CONSTS = 13


def general_plan(prev, here, nxt, setup):
    uses = []
    for u in range(FC):
        uses += [("up", u)] if prev else []
        uses += [("fc", u)] if setup else []
    uses += [("shift", 0)] if here else []
    uses += [("xT", tb) for tb in range(TB)] if nxt else []
    if nxt and not here:
        uses += [("v", tb) for tb in range(TB)]
    for h in range(HEADS):
        uses += [("qk", QK_AT[h])] if nxt and h in QK_AT else []
        uses += [("w2", 2 * (h - W2_FROM)), ("w2", 2 * (h - W2_FROM) + 1)] if setup and h >= W2_FROM else []
    if here:
        for name, n in (("v", 0), ("oT", 0), ("oT", 1), ("proj", 0), ("oT", 2), ("proj", 1), ("oT", 3),
                        ("proj", 2), ("proj", 3), ("v", 1), ("x2T", 0), ("v", 2), ("x2T", 1), ("v", 3),
                        ("x2T", 2), ("x2T", 3)):
            if name != "v" or nxt:
                uses.append((name, n))
    return {name: k for k, name in enumerate(uses)}


N_FIRST = len(general_plan(False, False, True, False))
N_SETUP = len(general_plan(False, True, True, True))
N_USUAL = len(general_plan(True, True, True, False))
N_NO_NEXT = len(general_plan(True, True, False, False))


def general_base(j):
    if isinstance(j, int) and j <= 0:
        return 0 if j < 0 else N_FIRST
    if isinstance(j, int) and j == BATCHES:
        return N_FIRST + N_SETUP + N_USUAL * (BATCHES - 2) + N_NO_NEXT
    return N_USUAL * j + (N_FIRST + N_SETUP - N_USUAL)


def general_bank(j, k):
    at = general_base(j) if isinstance(j, int) else N_FIRST + N_SETUP
    return (at + k) % 3


assert N_USUAL % 3 == 0


def need(eng, semaphore, count):
    if not isinstance(count, int) or count > 0:
        eng.wait_ge(semaphore, count)


def build(nc, x, w_attn, b_attn, w_proj, b_proj, w_fc, w_down, rope, out):
    f32, f16, bf16 = mybir.dt.float32, mybir.dt.float16, mybir.dt.bfloat16
    ALU = mybir.AluOpType
    ACT = mybir.ActivationFunctionType
    AX = mybir.AxisListType
    HI, LO = 0, 1

    x_v = x.rearrange("(r p) e -> p r e", p=PARTS)
    out_v = out.rearrange("(r p) e -> r p e", p=PARTS)

    with ExitStack() as ctx:
        def sb(name, shape, dt):
            return ctx.enter_context(nc.sbuf_tensor(name, shape, dt))

        def sem(name):
            return ctx.enter_context(nc.semaphore(name))

        wa = sb("wa", [PARTS, 2, EC, 3 * E], f16)
        wp = sb("wp", [PARTS, 2, EC, E], f16)
        t1T = sb("t1T", [PARTS, EC, F], f16)
        t2T = sb("t2T", [PARTS, FC, E], f16)
        c_sum = sb("c_sum", [PARTS, E], f32)
        qk_bias = sb("qk_bias", [PARTS, 2 * EC], f32)
        v_bias = sb("v_bias", [PARTS, E], f16)
        p_bias = sb("p_bias", [PARTS, E], f16)
        lift = sb("lift", [PARTS, PARTS], f16)
        ones16 = sb("ones16", [PARTS, PARTS], f16)
        ones32 = sb("ones32", [PARTS, PARTS], f32)
        ident32 = sb("ident32", [PARTS, PARTS], f32)
        ident16 = sb("ident16", [PARTS, PARTS], f16)
        identb = sb("identb", [PARTS, PARTS], bf16)
        mask_b = sb("mask_b", [PARTS, PARTS], bf16)
        mask_rows = sb("mask_rows", [PARTS, T], f32)
        mhalf = sb("mhalf", [PARTS, TB], f32)
        qk = sb("qk", [PARTS, 2, HEADS, T], f16)
        v_sb = sb("v_sb", [PARTS, TB, HEADS, VW], f16)
        qkn = sb("qkn", [PARTS, 2, 4, T], f16)
        hT = sb("hT", [PARTS, 2, FC, T], f16)
        xT = sb("xT", [PARTS, 2, EC, T], f16)
        x2T = sb("x2T", [PARTS, 2, EC, T], f16)
        xo = sb("xo", [PARTS, TB, E], f32)
        xn = sb("xn", [PARTS, 2, E], f32)
        x1 = sb("x1", [PARTS, TB, E], f32)
        probs = sb("probs", [PARTS, 2, 2, 1280], f16)
        z = sb("z", [PARTS, E], f32)
        oA = sb("oA", [PARTS, TB, HD], f32)
        r_sum = sb("r_sum", [PARTS, TB], f32)
        t16 = sb("t16", [PARTS, 2, E], f16)
        below = sb("below", [PARTS, 2, E], f16)
        mx = sb("mx", [PARTS, PARTS], f32)
        m_f = sb("m_f", [HEADS * TB, PARTS], f32)
        m_half = sb("m_half", [HEADS * TB, 2, PARTS], f16)
        bn = sb("bn", [PARTS, 4, TB, 6], f32)
        mv = sb("mv", [PARTS, 4, TB, 2], f32)
        veps = sb("veps", [PARTS, 4, TB], f32)
        negm = sb("negm", [PARTS, 4, TB], f32)
        rstd = sb("rstd", [PARTS, 4, TB], f32)
        shift = sb("shift", [PARTS, 4, TB], f32)
        h_negm = sb("h_negm", [PARTS, TB], f32)
        h_msq = sb("h_msq", [PARTS, TB], f32)
        h_var = sb("h_var", [PARTS, TB], f32)
        e_fin = sb("e_fin", [PARTS, TB], f32)
        gs = sb("gs", [PARTS, FC], f32)
        gt = sb("gt", [PARTS, 2], f32)
        gam = sb("gam", [PARTS, 2], f32)
        theta = sb("theta", [PARTS, 2, 2], f32)
        g_sq = sb("g_sq", [PARTS, 2], f32)
        c_fin = sb("c_fin", [PARTS, 1], f32)
        LX, LP, L1, LF = range(4)
        stage = hT[:, :, :, :].rearrange("p a c t -> p (a c t)").bitcast(f32)
        wa_in = stage[:, 0:EC * 3 * E].rearrange("p (c n) -> p c n", c=EC)
        y_sb = stage[:, 0:2 * E].rearrange("p (r e) -> p r e", r=2)
        xres = stage[:, 2 * E:6 * E].rearrange("p (b e) -> p b e", b=TB)
        oT = hT[:, 1, 8:12, :].rearrange("p c t -> p (c t)").rearrange(
            "p (r a c t) -> p r a c t", r=2, a=2, c=EC)
        temp = qk[:, :, :, :].rearrange("p a h t -> p (a h t)").bitcast(f32)
        rot1 = temp[:, 0:2048].rearrange("p (r n) -> p r n", r=2)
        rot2 = temp[:, 2048:4096].rearrange("p (r n) -> p r n", r=2)
        b_row, b_r1, b_r2 = (temp[0:1, 4096 + 1024 * i:5120 + 1024 * i] for i in range(3))
        vb_in, pb_in = temp[:, 7168:7680], temp[:, 7680:8192]
        rope_sb = probs[:, 0, :, :].rearrange("p a n -> p (a n)").bitcast(f32)[:, 0:2 * E]
        acc = probs[:, 1, :, :].rearrange("p a n -> p (a n)").bitcast(f32)[:, 0:T]
        m_stage = z[:, 0:PARTS]
        acc_add = probs[:, 1, :, :].rearrange("p a n -> p (a n)").bitcast(f32)[:, T:2 * T]
        score = [ctx.enter_context(nc.psum_tensor(f"score{i}", [PARTS, 512], f32)) for i in range(3)]
        gen = [ctx.enter_context(nc.psum_tensor(f"gen{i}", [PARTS, 512], f32)) for i in range(3)]
        pv = ctx.enter_context(nc.psum_tensor("pv", [PARTS, 512], f32))
        down = ctx.enter_context(nc.psum_tensor("down", [PARTS, 512], f32))
        H_SUM, H_SQ = 264, 268

        x_in, xres_in = sem("x_in"), sem("xres_in")
        wv_in, wp_in, rope_in, rows_in = sem("wv_in"), sem("wp_in"), sem("rope_in"), sem("rows_in")
        wqk_in = [sem(f"wqk_in{c}") for c in range(EC)]
        wfc_in, wdown_in = sem("wfc_in"), sem("wdown_in")
        stacked = [sem(f"stacked{g}") for g in range(4)]
        shift_rows = sem("shift_rows")
        stored = sem("stored")
        consts, rows_zero, ident_copy, k_rows = (
            sem(n) for n in ("consts", "rows_zero", "ident_copy", "k_rows"))
        wv_hi, wp_hi, rot_cross, rot_step, rot_done, wqk_hi = (
            sem(n) for n in ("wv_hi", "wp_hi", "rot_cross", "rot_step", "rot_done", "wqk_hi"))
        w_ready, bias_step, bias_cols, g_step, g_total, tern_half, tern_ready = (
            sem(n) for n in ("w_ready", "bias_step", "bias_cols", "g_step", "g_total", "tern_half", "tern_ready"))
        c_full, c_ready = sem("c_full"), sem("c_ready")
        g_full, g_drained = sem("g_full"), sem("g_drained")
        s_full, s_drained = sem("s_full"), sem("s_drained")
        pv_full, pv_drained = sem("pv_full"), sem("pv_drained")
        down_full, down_drained = sem("down_full"), sem("down_drained")
        hsum_full, hsq_full = sem("hsum_full"), sem("hsq_full")
        xn_ready, xT_hi, v_hi, qk_hi, h_full, exp_full = (
            sem(n) for n in ("xn_ready", "xT_hi", "v_hi", "qk_hi", "h_full", "exp_full"))
        oT_hi, y_copied, xb_ready, xn2_ready, x2T_hi, fin_ready = (
            sem(n) for n in ("oT_hi", "y_copied", "xb_ready", "xn2_ready", "x2T_hi", "fin_ready"))
        m_neg, m_hi, o_sums, o_recip, o_ready, x1_ready = (
            sem(n) for n in ("m_neg", "m_hi", "o_sums", "o_recip", "o_ready", "x1_ready"))
        bn_done = [sem(f"bn_done{i}") for i in range(4)]
        mv_done = [sem(f"mv_done{i}") for i in range(4)]
        ln_terms = [sem(f"ln_terms{i}") for i in range(4)]
        h_step, h_terms = sem("h_step"), sem("h_terms")
        ln_pow = [sem(f"ln_pow{i}") for i in range(4)]
        ln_ready = [sem(f"ln_ready{i}") for i in range(4)]
        sq_step, out_ready = sem("sq_step"), sem("out_ready")

        def bank16(bank):
            return bank[:, :].bitcast(f16)[:, 0:512]

        def block_at(s, tb):
            if s == tb:
                return PARTS * s
            return 512 + (PARTS * (tb - 1) if s == 0 else 384 if s == 2 else 512 + PARTS * (tb - 2))

        SCORE_W = (512, 512, 256)
        usual = (True, True, True, False)
        first = [(-1, False, False, True, False), (0, False, True, True, True), (1, *usual)]
        last = [(BATCHES - 1, True, True, False, False), (BATCHES, True, False, False, False)]

        def run(eng, iteration):
            for j, *what in first:
                iteration(j, *what)
            with eng.Fori(2, BATCHES - 1) as j:
                iteration(j, *usual)
            for j, *what in last:
                iteration(j, *what)

        block = ctx.enter_context(nc.Block())

        @block.sync
        def _(sp):
            sp.dma_start(xo[:, :, :], x_v[:, 0:TB, :]).then_inc(x_in, 16)
            wa_v = w_attn.rearrange("(c p) n -> p c n", p=PARTS)
            sp.dma_start(rope_sb.unsqueeze(1), rope.partition_broadcast(PARTS)).then_inc(rope_in, 16)
            for c in range(EC):
                sp.dma_start(wa_in[:, c, 0:2 * E], wa_v[:, c, 0:2 * E]).then_inc(wqk_in[c], 16)
                if c == 1:
                    sp.dma_start(wa_in[:, :, 2 * E:3 * E], wa_v[:, :, 2 * E:3 * E]).then_inc(wv_in, 16)
            sp.wait_ge(rows_zero, 1)
            for p in (0, 32):
                sp.dma_start(vb_in[p:p + 1, :], b_attn[:, 2 * E:3 * E]).then_inc(rows_in, 16)
                sp.dma_start(pb_in[p:p + 1, :], b_proj[:, :]).then_inc(rows_in, 16)
            sp.dma_start(b_row, b_attn[:, 0:2 * E]).then_inc(rows_in, 16)
            sp.dma_start(x1[:, :, :], w_proj.rearrange("(c p) n -> p c n", p=PARTS)).then_inc(wp_in, 16)
            sp.wait_ge(w_ready, EC + 1)
            sp.dma_start(stage.rearrange("p (u d) -> p u d", u=FC),
                         w_fc.rearrange("(u p) d -> p u d", p=PARTS)).then_inc(wfc_in, 16)
            sp.wait_ge(w_ready, 8)
            sp.dma_start(qk[96:98, 1, :, :], t16[96:98, 0, :].unsqueeze(1).to_broadcast([2, HEADS, T])
                         ).then_inc(k_rows, 16)

            def iteration(j, prev, here, nxt, setup):
                G, g0 = general_plan(prev, here, nxt, setup), general_base(j)
                if nxt and here:
                    row = TB * (j + 1) if isinstance(j, int) else sp.snap(TB * (j + 1))
                    need(sp, xn_ready, TB * (j + 1))
                    need(sp, g_full, g0)
                    sp.dma_start(xo[:, :, :], x_v[:, bass.ds(row, TB), :]).then_inc(x_in, 16)
                if setup:
                    sp.wait_ge(tern_ready, FC)
                    sp.dma_start(stage.rearrange("p (c f) -> p c f", c=EC),
                                 w_down.rearrange("(c p) f -> p c f", p=PARTS)).then_inc(wdown_in, 16)
                if here:
                    sp.wait_ge(g_drained, g0 + G["shift", 0] + 1)
                    for half in (HI, LO):
                        sp.dma_start(qk[96 + half:97 + half, 0, :, :].rearrange("o h (b t) -> o (h b) t", b=TB),
                                     m_half[:, half, :]).then_inc(shift_rows, 16)

                def store(tb):
                    row = TB * (j - 1) + tb if isinstance(j, int) else sp.snap(TB * (j - 1) + tb)
                    sp.wait_ge(out_ready, TB * (j - 1) + tb + 1)
                    sp.dma_start(out_v[bass.ds(row, 1), :, :].rearrange("r p e -> p (r e)"), z[:, :]
                                 ).then_inc(stored, 16)

                def stack(g):
                    if here:
                        n = max(4 * g + 3, max(h for h, what in QK_AT.items() if what[0] == g) + 2)
                        sp.wait_ge(s_full, 96 * j + 48 + 3 * n + 3)
                    else:
                        sp.wait_ge(g_drained, g0 + G["qk", (g, 1)] + 1)
                    for i in range(4):
                        src = qkn[HD * i:HD * (i + 1), g % 2, :, :]
                        head = qk[:, :, 4 * g + i, :]
                        sp.dma_start(head[0:32, :, :], src[:, 1:3, :]).then_inc(stacked[g], 16)
                        sp.dma_start(head[32:64, :, :], src[:, 0:3:2, :]).then_inc(stacked[g], 16)
                        sp.dma_start(head[64:96, :, :], src[:, 1:4:2, :]).then_inc(stacked[g], 16)

                if prev:
                    store(0)
                for g in range(4):
                    if g == 3 and here:
                        if prev:
                            sp.wait_ge(down_full, TB * j)
                        if setup:
                            sp.wait_ge(tern_ready, 2 * FC)
                        row = TB * j if isinstance(j, int) else sp.snap(TB * j)
                        sp.dma_start(xres, x_v[:, bass.ds(row, TB), :]).then_inc(xres_in, 16)
                    if nxt:
                        stack(g)
                    if prev:
                        if g in (0, 1):
                            store(g + 1)
                        if g == 3:
                            store(3)

            run(sp, iteration)
            sp.wait_ge(stored, 16 * TB * BATCHES)

        @block.tensor
        def _(pe):
            pe.wait_ge(consts, CONSTS)
            pe.wait_ge(ident_copy, 3)
            pe.wait_ge(bias_step, 4)
            for i in range(2 * EC):
                mm = nc.tensor.matmul(down[:, i:i + 1], b_r1[:, PARTS * i:PARTS * (i + 1)], ones32[0:1, 0:1],
                                      start=True, stop=True)
            mm.then_inc(bias_cols, 1)

            def gamma_total(m):
                pe.wait_ge(g_step, 6 * m + 2)
                nc.tensor.matmul(down[:, 16 + m:17 + m], ones32[:, :], gt[:, m:m + 1], start=True, stop=True
                                 ).then_inc(g_total, 1)

            def iteration(j, prev, here, nxt, setup):
                G, g0 = general_plan(prev, here, nxt, setup), general_base(j)

                def claim(name, n):
                    k = G[name, n]
                    need(pe, g_drained, g0 + k - 2)
                    return gen[general_bank(j, k)]

                def drained(name, n):
                    pe.wait_ge(g_drained, g0 + G[name, n] + 1)

                def claim_score(k):
                    need(pe, s_drained, 96 * j + k - 2)
                    return score[k % 3]

                def turn(bank, block, n=EC):
                    for c in range(n):
                        mm = nc.tensor.transpose(bank[:, PARTS * c:PARTS * (c + 1)], block(c), ident32[:, :])
                    return mm

                def turn16(bank, block):
                    for c in range(EC):
                        mm = nc.tensor.transpose(bank16(bank)[:, PARTS * c:PARTS * (c + 1)], block(c), ident16[:, :])
                    return mm

                def products(bank, pairs, stop=True):
                    for n, (a, b) in enumerate(pairs):
                        mm = nc.tensor.matmul(bank[:, :], a, b, start=(n == 0), stop=(n == len(pairs) - 1))
                    return mm

                def up(u):
                    bank = claim("up", u)
                    cols = slice(PARTS * u, PARTS * (u + 1))
                    products(bank, [(t1T[:, c, cols], x2T[:, half, c, :]) for c in range(EC) for half in (HI, LO)]
                             ).then_inc(g_full, 1)

                def hidden_sums(u):
                    drained("up", u)
                    for half in (HI, LO):
                        for tb in range(TB):
                            first, final = u == 0 and half == HI, u == FC - 1 and half == LO
                            mm = nc.tensor.matmul(pv[:, H_SUM + tb:H_SUM + tb + 1],
                                                  hT[:, half, u, PARTS * tb:PARTS * (tb + 1)], ones16[:, 0:1],
                                                  start=first and tb == 0, stop=final, skip_group_check=True)
                    if u == FC - 1:
                        mm.then_inc(hsum_full, 1)

                def square_sums():
                    pe.wait_ge(sq_step, 31 * j)
                    for tb in range(TB):
                        mm = nc.tensor.matmul(pv[:, H_SQ + tb:H_SQ + tb + 1], acc[:, PARTS * tb:PARTS * (tb + 1)],
                                              ones32[:, 0:1], start=True, stop=True)
                    mm.then_inc(hsq_full, 1)

                def ffn_down(tb, part):
                    if part == 0:
                        need(pe, down_drained, TB * (j - 1) + tb)
                    for u in range(4 * part, 4 * part + 4):
                        for half in (HI, LO):
                            mm = nc.tensor.matmul(down[:, :], hT[:, half, u, PARTS * tb:PARTS * (tb + 1)], t2T[:, u, :],
                                                  start=(u == 0 and half == HI), stop=(u == FC - 1 and half == LO))
                    if part == 3:
                        mm.then_inc(down_full, 1)

                def max_pass(u):
                    if u % 4 == 0:
                        pe.wait_ge(stacked[u // 4], 192 * (j + 1))
                    for i, tbs in enumerate(((3,), (0, 2), (1,))):
                        bank = claim_score(3 * u + i)
                        at = 0
                        for tb in tbs:
                            n = PARTS * (tb + 1)
                            mm = nc.tensor.matmul(bank[:, at:at + n], qk[0:96, 0, u, PARTS * tb:PARTS * (tb + 1)],
                                                  qk[0:96, 1, u, 0:n], start=(at == 0), stop=True,
                                                  skip_group_check=True)
                            at += n
                        mm.then_inc(s_full, 1)

                def scores(h):
                    def part(bank, at, s, t0, t1, start):
                        return nc.tensor.matmul(bank[:, at:at + t1 - t0], qk[0:98, 1, h, PARTS * s:PARTS * (s + 1)],
                                                qk[0:98, 0, h, t0:t1], start=start, stop=True, skip_group_check=True)
                    if h == 0:
                        pe.wait_ge(k_rows, 16)
                        pe.wait_ge(shift_rows, 32 * (j + 1))
                    bank = claim_score(48 + 3 * h)
                    nc.tensor.matmul(bank[:, :].rearrange("p (b t) -> p b t", b=TB), identb[:, :],
                                     mask_b[:, :].unsqueeze(1).to_broadcast([PARTS, TB, PARTS]),
                                     start=True, stop=False, skip_group_check=True)
                    for s in range(TB):
                        mm = part(bank, PARTS * s, s, PARTS * s, PARTS * (s + 1), False)
                    mm.then_inc(s_full, 1)
                    bank = claim_score(48 + 3 * h + 1)
                    part(bank, 0, 0, PARTS, T, True)
                    part(bank, 384, 2, 3 * PARTS, T, False).then_inc(s_full, 1)
                    bank = claim_score(48 + 3 * h + 2)
                    part(bank, 0, 1, 2 * PARTS, T, True).then_inc(s_full, 1)

                def weigh(h):
                    pe.wait_ge(s_drained, 96 * j + 48 + 3 * h + 3)
                    need(pe, pv_drained, HEADS * j + h)
                    for tb in range(TB):
                        for s in range(tb + 1):
                            for half in (HI, LO):
                                at = block_at(s, tb)
                                mm = nc.tensor.matmul(pv[:, VW * tb:VW * (tb + 1)],
                                                      probs[:, h % 2, half, at:at + PARTS], v_sb[:, s, h, :],
                                                      start=(s == 0 and half == HI), stop=(s == tb and half == LO))
                    mm.then_inc(pv_full, 1)

                def x_turn(tb):
                    pe.wait_ge(xn_ready, TB * (j + 1) + tb + 1)
                    bank = claim("xT", tb)
                    turn(bank, lambda c: xn[:, tb % 2, PARTS * c:PARTS * (c + 1)]).then_inc(g_full, 1)

                def values(tb):
                    if not here and tb == 0:
                        drained("xT", 3)
                    bank = claim("v", tb)
                    rows = slice(PARTS * tb, PARTS * (tb + 1))
                    cols = slice(2 * E, 3 * E)
                    products(bank, [(xT[:, a, c, rows], wa[:, b, c, cols]) for c in range(EC)
                                    for a, b in ((HI, HI), (HI, LO), (LO, HI))] + [(lift[:, :], v_bias[:, :])]
                             ).then_inc(g_full, 1)

                def queries_keys(g, which):
                    if (g, which) == (0, 0) and here:
                        drained("xT", 3)
                    bank = claim("qk", (g, which))
                    cols = slice(E * which + PARTS * g, E * which + PARTS * (g + 1))
                    products(bank, [(wa[:, a, c, cols], xT[:, b, c, :]) for c in range(EC)
                                    for a, b in ((HI, HI), (HI, LO), (LO, HI))]).then_inc(g_full, 1)

                def o_turn(tb):
                    if tb == 0:
                        pe.wait_ge(o_ready, HEADS * (j + 1))
                    bank = claim("oT", tb)
                    turn(bank, lambda c: xo[:, tb, PARTS * c:PARTS * (c + 1)]).then_inc(g_full, 1)

                def project(tb):
                    drained("oT", tb)
                    bank = claim("proj", tb)
                    products(bank, [(oT[:, tb % 2, a, c, :], wp[:, b, c, :]) for c in range(EC)
                                    for a, b in ((HI, HI), (HI, LO), (LO, HI))] + [(lift[:, :], p_bias[:, :])]
                             ).then_inc(g_full, 1)

                def x2_turn(tb):
                    pe.wait_ge(xn2_ready, TB * j + tb + 1)
                    bank = claim("x2T", tb)
                    turn(bank, lambda c: xn[:, tb % 2, PARTS * c:PARTS * (c + 1)]).then_inc(g_full, 1)

                if setup:
                    pe.wait_ge(w_ready, 9)
                    gamma_total(0)
                if prev:
                    pe.wait_ge(g_drained, g0)
                for u in range(FC):
                    if prev:
                        up(u)
                    if setup:
                        pe.wait_ge(tern_ready, u + 1)
                        turn16(claim("fc", u), lambda c: t16[:, u % 2, PARTS * c:PARTS * (c + 1)]).then_inc(g_full, 1)
                    if here:
                        max_pass(u)
                    if prev and u >= 2:
                        hidden_sums(u - 2)
                if prev:
                    hidden_sums(FC - 2)
                    hidden_sums(FC - 1)
                    ffn_down(0, 0)
                    ffn_down(0, 1)
                if here:
                    pe.wait_ge(s_drained, 96 * j + 48)
                    bank = claim("shift", 0)
                    nc.tensor.transpose(bank[:, 0:PARTS], mx[:, :], ident32[:, :]).then_inc(g_full, 1)
                if prev:
                    ffn_down(0, 2)
                    ffn_down(0, 3)
                    square_sums()
                if nxt:
                    x_turn(0)
                    x_turn(1)
                if here:
                    scores(0)
                if nxt:
                    x_turn(2)
                    x_turn(3)
                if nxt and not here:
                    pe.wait_ge(w_ready, 6)
                    for tb in range(TB):
                        values(tb)
                    pe.wait_ge(w_ready, 7)
                for h in range(HEADS):
                    if nxt and h in QK_AT:
                        queries_keys(*QK_AT[h])
                    if setup and h == W2_FROM - 1:
                        gamma_total(1)
                    if setup and h >= W2_FROM:
                        for u in (2 * (h - W2_FROM), 2 * (h - W2_FROM) + 1):
                            pe.wait_ge(tern_ready, FC + u + 1)
                            turn16(claim("w2", u), lambda c: t16[:, u % 2, PARTS * c:PARTS * (c + 1)]
                                   ).then_inc(g_full, 1)
                    if prev:
                        for tb, part in DOWN_AT.get(h, ()):
                            ffn_down(tb, part)
                    if here:
                        if h + 1 < HEADS:
                            scores(h + 1)
                        weigh(h)
                if here:
                    if nxt:
                        values(0)
                    o_turn(0)
                    o_turn(1)
                    project(0)
                    o_turn(2)
                    project(1)
                    o_turn(3)
                    project(2)
                    project(3)
                    if nxt:
                        values(1)
                    x2_turn(0)
                    if nxt:
                        values(2)
                    x2_turn(1)
                    if nxt:
                        values(3)
                    x2_turn(2)
                    x2_turn(3)
                if setup:
                    pe.wait_ge(g_drained, g0 + G["w2", FC - 1] + 1)
                    for u in range(FC):
                        mm = nc.tensor.matmul(down[:, :], ones16[:, :], t2T[:, u, :], start=(u == 0), stop=(u == FC - 1))
                    mm.then_inc(c_full, 1)

            run(pe, iteration)

        @block.scalar
        def _(act):
            def high(out, in_, bias=None, scale=1.0):
                if bias is None:
                    return nc.scalar.activation(out, in_, ACT.Copy, scale=scale)
                return nc.scalar.activation(out, in_, ACT.Identity, bias=bias, scale=scale)

            act.wait_ge(wv_in, 16)
            high(wa[:, HI, :, 2 * E:3 * E], wa_in[:, :, 2 * E:3 * E], scale=W_UP).then_inc(wv_hi, 1)
            for c in range(EC):
                act.wait_ge(rot_done, c + 1)
                high(wa[:, HI, c, 0:2 * E], rot1[:, c % 2, :], scale=W_UP).then_inc(wqk_hi, 1)
            act.wait_ge(wp_in, 16)
            high(wp[:, HI, :, :], x1[:, :, :], scale=W_UP).then_inc(wp_hi, 1)

            def iteration(j, prev, here, nxt, setup):
                G, g0 = general_plan(prev, here, nxt, setup), general_base(j)

                def filled(name, n):
                    k = G[name, n]
                    act.wait_ge(g_full, g0 + k + 1)
                    return gen[general_bank(j, k)]

                def blocks(bank, n=PARTS):
                    return bank[:, :].rearrange("p (c t) -> p c t", t=n)

                def hidden(u):
                    bank = filled("up", u)
                    nc.scalar.activation(hT[:, HI, u, :], bank[:, :], ACT.Gelu, scale=gam[:, 0:1])
                    nc.scalar.activation(bank[:, :], bank[:, :], ACT.Gelu, scale=gam[:, 0:1]).then_inc(h_full, 1)

                def normalise(tb):
                    nc.scalar.activation(xn[:, tb % 2, :], xo[:, tb, :], ACT.Identity, bias=shift[:, LX, tb:tb + 1],
                                         scale=rstd[:, LX, tb:tb + 1]).then_inc(xn_ready, 1)

                def x_turned(tb):
                    high(xT[:, HI, :, PARTS * tb:PARTS * (tb + 1)], blocks(filled("xT", tb))).then_inc(xT_hi, 1)

                def values(tb):
                    high(v_sb[:, tb, :, 0:HD], blocks(filled("v", tb), HD)).then_inc(v_hi, 1)

                def queries_keys(g, which):
                    bank = filled("qk", (g, which))
                    if which == 0:
                        need(act, stacked[(g - 2) % 4], 192 * (j + 1 + (1 if g >= 2 else 0)))
                    high(qkn[:, g % 2, 1 + which, :], bank[:, :], bias=qk_bias[:, EC * which + g:EC * which + g + 1]
                         ).then_inc(qk_hi, 1)

                def exponents(h):
                    for i, n in enumerate(SCORE_W):
                        act.wait_ge(s_full, 96 * j + 48 + 3 * h + i + 1)
                        nc.scalar.activation(probs[:, h % 2, HI, 512 * i:512 * i + n], score[i][:, 0:n], ACT.Exp,
                                             scale=1.0 / S_UP)
                        nc.scalar.activation(score[i][:, 0:n], score[i][:, 0:n], ACT.Exp, scale=1.0 / S_UP
                                             ).then_inc(exp_full, 1)

                def final(tb):
                    act.wait_ge(ln_ready[LF], TB * (j - 1) + tb + 1)
                    nc.scalar.activation(z[:, :], z[:, :], ACT.Identity, bias=shift[:, LF, tb:tb + 1],
                                         scale=rstd[:, LF, tb:tb + 1]).then_inc(fin_ready, 1)

                def o_turned(tb):
                    high(oT[:, tb % 2, HI, :, :], blocks(filled("oT", tb))).then_inc(oT_hi, 1)

                def copy_y(tb):
                    bank = filled("proj", tb)
                    need(act, x1_ready, TB * j + tb - 1)
                    nc.scalar.activation(y_sb[:, tb % 2, :], bank[:, :], ACT.Copy).then_inc(y_copied, 1)

                def residual(tb):
                    if tb == 0:
                        act.wait_ge(xres_in, 16 * (j + 1))
                    act.wait_ge(ln_ready[LP], TB * j + tb + 1)
                    nc.scalar.activation(xres[:, tb, :], xres[:, tb, :], ACT.Identity, bias=shift[:, LP, tb:tb + 1]
                                         ).then_inc(xb_ready, 1)

                def normalise2(tb):
                    act.wait_ge(ln_ready[L1], TB * j + tb + 1)
                    nc.scalar.activation(xn[:, tb % 2, :], x1[:, tb, :], ACT.Identity, bias=shift[:, L1, tb:tb + 1],
                                         scale=rstd[:, L1, tb:tb + 1]).then_inc(xn2_ready, 1)

                def x2_turned(tb):
                    high(x2T[:, HI, :, PARTS * tb:PARTS * (tb + 1)], blocks(filled("x2T", tb))).then_inc(x2T_hi, 1)

                if prev:
                    act.wait_ge(g_step, 14)
                    for u in range(FC):
                        hidden(u)
                if nxt:
                    act.wait_ge(ln_ready[LX], j + 2)
                    normalise(0)
                    normalise(1)
                    x_turned(0)
                    x_turned(1)
                    normalise(2)
                    normalise(3)
                if here:
                    exponents(0)
                if nxt:
                    x_turned(2)
                    x_turned(3)
                if nxt and not here:
                    for tb in range(TB):
                        values(tb)
                for h in range(HEADS):
                    if nxt and h in QK_AT:
                        queries_keys(*QK_AT[h])
                    if prev and h in FINISH_AT:
                        final(FINISH_AT[h])
                    if here and h + 1 < HEADS:
                        exponents(h + 1)
                if here:
                    if nxt:
                        values(0)
                    o_turned(0)
                    o_turned(1)
                    copy_y(0)
                    o_turned(2)
                    copy_y(1)
                    residual(0)
                    o_turned(3)
                    copy_y(2)
                    residual(1)
                    copy_y(3)
                    residual(2)
                    normalise2(0)
                    if nxt:
                        values(1)
                    residual(3)
                    normalise2(1)
                    x2_turned(0)
                    if nxt:
                        values(2)
                    x2_turned(1)
                    normalise2(2)
                    if nxt:
                        values(3)
                    normalise2(3)
                    x2_turned(2)
                    x2_turned(3)

            run(act, iteration)

        @block.vector
        def _(dve):
            V = nc.vector

            def low(out, whole, hi):
                return V.tensor_tensor(out, whole, hi, ALU.subtract)

            dve.wait_ge(consts, CONSTS)
            V.tensor_copy(ident16[:, :], ident32[:, :]).then_inc(ident_copy, 1)
            V.tensor_copy(identb[:, :], ident32[:, :]).then_inc(ident_copy, 1)
            V.tensor_copy(mask_b[:, :], m_stage).then_inc(ident_copy, 1)
            dve.wait_ge(wv_hi, 1)
            for c in range(EC):
                last_op = V.scalar_tensor_tensor(out=wa[:, LO, c, 2 * E:3 * E], in0=wa_in[:, c, 2 * E:3 * E],
                                                 scalar=W_UP, in1=wa[:, HI, c, 2 * E:3 * E],
                                                 op0=ALU.mult, op1=ALU.subtract)
            last_op.then_inc(w_ready, 1)
            cos2 = rope_sb[:, 0:E].unsqueeze(1).to_broadcast([PARTS, 2, E])
            dve.wait_ge(rope_in, 16)
            for c in range(EC):
                dve.wait_ge(wqk_in[c], 16)
                if c >= 2:
                    dve.wait_ge(wqk_hi, c - 1)
                    dve.wait_ge(w_ready, c)
                V.tensor_tensor(rot1[:, c % 2, :].rearrange("p (a e) -> p a e", a=2),
                                wa_in[:, c, 0:2 * E].rearrange("p (a e) -> p a e", a=2), cos2, ALU.mult
                                ).then_inc(rot_step, 1)
                dve.wait_ge(rot_step, c + 1)
                dve.wait_ge(rot_cross, 2 * c + 2)
                V.tensor_tensor(rot1[:, c % 2, :], rot1[:, c % 2, :], rot2[:, c % 2, :], ALU.add).then_inc(rot_done, 1)
                dve.wait_ge(wqk_hi, c + 1)
                V.scalar_tensor_tensor(out=wa[:, LO, c, 0:2 * E], in0=rot1[:, c % 2, :], scalar=W_UP,
                                       in1=wa[:, HI, c, 0:2 * E], op0=ALU.mult, op1=ALU.subtract).then_inc(w_ready, 1)
            dve.wait_ge(rows_in, 80)
            p_up = 1.0 / (PROJ_K * BIAS_UP)
            V.tensor_copy(v_bias[:, :], vb_in).then_inc(bias_step, 1)
            V.tensor_scalar(p_bias[:, :], pb_in, p_up, None, ALU.mult).then_inc(bias_step, 1)
            dve.wait_ge(bias_step, 2)
            low(v_bias[32:33, :], vb_in[32:33, :], v_bias[32:33, :]).then_inc(w_ready, 1)
            c_row = rope_sb[0:1, 0:E].unsqueeze(1).to_broadcast([1, 2, E])
            V.tensor_tensor(b_r1.rearrange("p (a e) -> p a e", a=2), b_row.rearrange("p (a e) -> p a e", a=2), c_row,
                            ALU.mult).then_inc(bias_step, 1)
            dve.wait_ge(bias_step, 3)
            dve.wait_ge(rot_cross, 2 * EC + 2)
            V.tensor_tensor(b_r1, b_r1, b_r2, ALU.add).then_inc(bias_step, 1)
            dve.wait_ge(bias_cols, 1)
            V.tensor_scalar(qk_bias[:, :], down[:, 0:2 * EC], W_UP, None, ALU.mult).then_inc(w_ready, 1)
            V.scalar_tensor_tensor(out=p_bias[32:33, :], in0=pb_in[32:33, :], scalar=p_up, in1=p_bias[32:33, :],
                                   op0=ALU.mult, op1=ALU.subtract).then_inc(w_ready, 1)
            dve.wait_ge(wp_hi, 1)
            for c in range(EC):
                last_op = V.scalar_tensor_tensor(out=wp[:, LO, c, :], in0=x1[:, c, :], scalar=W_UP,
                                                 in1=wp[:, HI, c, :], op0=ALU.mult, op1=ALU.subtract)
            last_op.then_inc(w_ready, 1)

            def magnitude(m, loaded):
                dve.wait_ge(loaded, 16)
                V.tensor_reduce(gs[:, :], stage.rearrange("p (u d) -> p u d", u=FC), AX.X, ALU.add,
                                apply_absolute_value=True).then_inc(g_step, 1)
                dve.wait_ge(g_step, 6 * m + 1)
                V.tensor_reduce(gt[:, m:m + 1], gs[:, :], AX.X, ALU.add).then_inc(g_step, 1)

            def iteration(j, prev, here, nxt, setup):
                G, g0 = general_plan(prev, here, nxt, setup), general_base(j)

                def bank_of(name, n):
                    return gen[general_bank(j, G[name, n])]

                def blocks(bank, n=PARTS):
                    return bank[:, :].rearrange("p (c t) -> p c t", t=n)

                def thresholds(m):
                    dve.wait_ge(g_total, m + 1)
                    s0 = 2 + 6 * m
                    V.tensor_scalar(gam[:, m:m + 1], down[:, 16 + m:17 + m], 1.0 / (F * E), None, ALU.mult
                                    ).then_inc(g_step, 1)
                    dve.wait_ge(g_step, s0 + 1)
                    V.tensor_scalar(theta[:, m, 0:1], gam[:, m:m + 1], EPS_BIT, 0.5, ALU.add, ALU.mult
                                    ).then_inc(g_step, 1)
                    V.tensor_scalar(theta[:, m, 1:2], gam[:, m:m + 1], EPS_BIT, -0.5, ALU.add, ALU.mult
                                    ).then_inc(g_step, 1)
                    V.tensor_tensor(g_sq[:, m:m + 1], gam[:, m:m + 1], gam[:, m:m + 1], ALU.mult).then_inc(g_step, 1)
                    dve.wait_ge(g_step, s0 + 4)
                    if m == 1:
                        V.reciprocal(g_sq[:, 0:1], g_sq[:, 1:2]).then_inc(g_step, 1)
                        dve.wait_ge(g_step, s0 + 5)
                        V.tensor_scalar(c_fin[:, :], g_sq[:, 0:1], EPS_LN, None, ALU.mult).then_inc(g_step, 1)
                        dve.wait_ge(g_step, s0 + 6)

                def ternary(m, u):
                    w = stage[:, E * u:E * (u + 1)]
                    n = FC * m + u
                    V.tensor_scalar(below[:, u % 2, :], w, theta[:, m, 1:2], None, ALU.is_lt).then_inc(tern_half, 1)
                    dve.wait_ge(tern_half, n + 1)
                    V.scalar_tensor_tensor(out=t16[:, u % 2, :], in0=w, scalar=theta[:, m, 0:1],
                                           in1=below[:, u % 2, :], op0=ALU.is_gt, op1=ALU.subtract
                                           ).then_inc(tern_ready, 1)

                def turned16(name, u):
                    dve.wait_ge(g_full, g0 + G[name, u] + 1)
                    if name == "fc":
                        dst = t1T[:, :, PARTS * u:PARTS * (u + 1)]
                    else:
                        dst = t2T[:, 4 * (u % 4):4 * (u % 4) + 4, PARTS * (u // 4):PARTS * (u // 4 + 1)]
                    src = bank16(bank_of(name, u)).rearrange("p (c t) -> p c t", t=PARTS)
                    V.tensor_copy(dst, src).then_inc(g_drained, 1)

                def hidden_low(u):
                    dve.wait_ge(h_full, FC * (j - 1) + u + 1)
                    low(hT[:, LO, u, :], bank_of("up", u)[:, :], hT[:, HI, u, :]).then_inc(g_drained, 1)

                def maxima(u):
                    for i, tbs in enumerate(((3,), (0, 2), (1,))):
                        at = 0
                        for tb in tbs:
                            n = PARTS * (tb + 1)
                            part = score[i][:, at:at + n]
                            op = V.tensor_tensor_reduce(part, part, mask_rows[:, T - n:T], 1.0, -3.0e38, ALU.add,
                                                        ALU.max, mx[:, TB * u + tb:TB * u + tb + 1])
                            at += n
                        op.then_inc(s_drained, 1)

                def halve_maxima():
                    bank = bank_of("shift", 0)
                    dve.wait_ge(g_full, g0 + G["shift", 0] + 1)
                    V.tensor_scalar(m_f[:, :], bank[0:HEADS * TB, 0:PARTS], -1.0 / ROW_UP, P_LIFT * S_UP / ROW_UP,
                                    ALU.mult, ALU.add).then_inc(m_neg, 1)
                    dve.wait_ge(m_neg, j + 1)
                    V.tensor_copy(m_half[:, HI, :], m_f[:, :]).then_inc(m_hi, 1)
                    dve.wait_ge(m_hi, j + 1)
                    low(m_half[:, LO, :], m_f[:, :], m_half[:, HI, :]).then_inc(g_drained, 1)

                def moments(ln, tb):
                    V.tensor_scalar(negm[:, ln, tb:tb + 1], bn[:, ln, tb, 1:2], bn[:, ln, tb, 4:5], -0.5,
                                    ALU.add, ALU.mult)
                    V.bn_aggr(mv[:, ln, tb, :], bn[:, ln, tb, :]).then_inc(mv_done[ln], 1)

                def terms(ln, tbs, var_ops, n):
                    V.tensor_scalar(veps[:, ln, tbs], mv[:, ln, tbs, 1], *var_ops).then_inc(ln_terms[ln], 1)

                def x_moments():
                    dve.wait_ge(x_in, 16 * (j + 2))
                    for tb in range(TB):
                        V.bn_stats(bn[:, LX, tb, :], xo[:, tb, :]).then_inc(bn_done[LX], 1)
                    dve.wait_ge(bn_done[LX], TB * (j + 2))
                    for tb in range(TB):
                        moments(LX, tb)
                    dve.wait_ge(mv_done[LX], TB * (j + 2))
                    terms(LX, slice(0, TB), (EPS_LN, None, ALU.add), 0)

                def hidden_moments():
                    dve.wait_ge(hsum_full, j)
                    dve.wait_ge(hsq_full, j)
                    V.tensor_scalar(h_negm[:, :], pv[:, H_SUM:H_SUM + TB], -1.0 / F, None, ALU.mult
                                    ).then_inc(h_step, 1)
                    dve.wait_ge(h_step, 3 * (j - 1) + 1)
                    V.tensor_tensor(h_msq[:, :], h_negm[:, :], h_negm[:, :], ALU.mult).then_inc(h_step, 1)
                    dve.wait_ge(h_step, 3 * (j - 1) + 2)
                    V.scalar_tensor_tensor(out=h_var[:, :], in0=pv[:, H_SQ:H_SQ + TB], scalar=1.0 / F,
                                           in1=h_msq[:, :], op0=ALU.mult, op1=ALU.subtract).then_inc(h_step, 1)
                    dve.wait_ge(h_step, 3 * (j - 1) + 3)
                    V.tensor_scalar(e_fin[:, :], h_var[:, :], EPS_BIT, c_fin[:, 0:1], ALU.add, ALU.mult
                                    ).then_inc(h_terms, 1)

                def final(tb):
                    n = TB * (j - 1) + tb
                    dve.wait_ge(down_full, n + 1)
                    need(dve, stored, 16 * n)
                    V.scalar_tensor_tensor(out=z[:, :], in0=c_sum[:, :], scalar=h_negm[:, tb:tb + 1],
                                           in1=down[:, :], op0=ALU.mult, op1=ALU.add).then_inc(down_drained, 1)
                    dve.wait_ge(down_drained, n + 1)
                    V.bn_stats(bn[:, LF, tb, :], z[:, :]).then_inc(bn_done[LF], 1)
                    dve.wait_ge(bn_done[LF], n + 1)
                    moments(LF, tb)
                    if tb == 0:
                        dve.wait_ge(h_terms, j)
                    dve.wait_ge(mv_done[LF], n + 1)
                    V.tensor_tensor(veps[:, LF, tb:tb + 1], mv[:, LF, tb, 1:2], e_fin[:, tb:tb + 1], ALU.add
                                    ).then_inc(ln_terms[LF], 1)

                def x_low(tb):
                    dve.wait_ge(xT_hi, TB * (j + 1) + tb + 1)
                    cols = slice(PARTS * tb, PARTS * (tb + 1))
                    low(xT[:, LO, :, cols], blocks(bank_of("xT", tb)), xT[:, HI, :, cols]).then_inc(g_drained, 1)

                def v_low(tb):
                    dve.wait_ge(v_hi, TB * (j + 1) + tb + 1)
                    low(v_sb[:, tb, :, HD + 1:VW], blocks(bank_of("v", tb), HD), v_sb[:, tb, :, 0:HD]
                        ).then_inc(g_drained, 1)

                def qk_low(g, which):
                    dve.wait_ge(qk_hi, 8 * (j + 1) + 2 * g + which + 1)
                    V.scalar_tensor_tensor(out=qkn[:, g % 2, 3 * which, :], in0=bank_of("qk", (g, which))[:, :],
                                           scalar=qk_bias[:, EC * which + g:EC * which + g + 1],
                                           in1=qkn[:, g % 2, 1 + which, :], op0=ALU.add, op1=ALU.subtract
                                           ).then_inc(g_drained, 1)

                def probs_low(h):
                    for i, n in enumerate(SCORE_W):
                        dve.wait_ge(exp_full, 48 * j + 3 * h + i + 1)
                        at = 512 * i
                        low(probs[:, h % 2, LO, at:at + n], score[i][:, 0:n], probs[:, h % 2, HI, at:at + n]
                            ).then_inc(s_drained, 1)

                def head_output(h):
                    n = HEADS * j + h
                    dve.wait_ge(pv_full, n + 1)
                    res = pv[:, 0:VW * TB].rearrange("p (b w) -> p b w", b=TB)
                    V.reciprocal(r_sum[:, :], res[:, :, HD]).then_inc(o_recip, 1)
                    pairs = bass.AP(pv, 0, [[512, PARTS], [VW, TB], [1, HD], [HD + 1, 2]])
                    V.tensor_reduce(oA[:, :, :], pairs, AX.X, ALU.add).then_inc(pv_drained, 1)
                    if h == 0 and nxt:
                        dve.wait_ge(xn_ready, TB * (j + 2))
                    dve.wait_ge(o_recip, n + 1)
                    dve.wait_ge(pv_drained, n + 1)
                    V.tensor_tensor(xo[:, :, HD * h:HD * (h + 1)], oA[:, :, :],
                                    r_sum[:, :].unsqueeze(2).to_broadcast([PARTS, TB, HD]), ALU.mult
                                    ).then_inc(o_ready, 1)

                def o_low(tb):
                    dve.wait_ge(oT_hi, TB * j + tb + 1)
                    low(oT[:, tb % 2, LO, :, :], blocks(bank_of("oT", tb)), oT[:, tb % 2, HI, :, :]
                        ).then_inc(g_drained, 1)

                def y_moments(tb):
                    n = TB * j + tb
                    dve.wait_ge(y_copied, n + 1)
                    V.bn_stats(bn[:, LP, tb, :], bank_of("proj", tb)[:, :]).then_inc(g_drained, 1)
                    dve.wait_ge(g_drained, g0 + G["proj", tb] + 1)
                    moments(LP, tb)
                    dve.wait_ge(mv_done[LP], n + 1)
                    terms(LP, slice(tb, tb + 1), (EPS_LN / PROJ_K ** 2, None, ALU.add), n)

                def first_sum(tb):
                    n = TB * j + tb
                    dve.wait_ge(xb_ready, n + 1)
                    V.scalar_tensor_tensor(out=x1[:, tb, :], in0=y_sb[:, tb % 2, :], scalar=rstd[:, LP, tb:tb + 1],
                                           in1=xres[:, tb, :], op0=ALU.mult, op1=ALU.add).then_inc(x1_ready, 1)
                    dve.wait_ge(x1_ready, n + 1)
                    V.bn_stats(bn[:, L1, tb, :], x1[:, tb, :]).then_inc(bn_done[L1], 1)
                    dve.wait_ge(bn_done[L1], n + 1)
                    moments(L1, tb)
                    dve.wait_ge(mv_done[L1], n + 1)
                    terms(L1, slice(tb, tb + 1), (1.0 + EPS_BIT, EPS_LN * EPS_BIT, ALU.mult, ALU.add), n)

                def x2_low(tb):
                    dve.wait_ge(x2T_hi, TB * j + tb + 1)
                    cols = slice(PARTS * tb, PARTS * (tb + 1))
                    low(x2T[:, LO, :, cols], blocks(bank_of("x2T", tb)), x2T[:, HI, :, cols]).then_inc(g_drained, 1)

                if setup:
                    magnitude(0, wfc_in)
                    thresholds(0)
                    dve.wait_ge(k_rows, 16)
                    ternary(0, 0)
                    ternary(0, 1)
                for u in range(FC):
                    if here:
                        dve.wait_ge(s_full, 96 * j + 3 * u + 3)
                    if prev:
                        hidden_low(u)
                    if setup:
                        turned16("fc", u)
                    if here:
                        maxima(u)
                    if setup and u + 2 < FC:
                        ternary(0, u + 2)
                if here:
                    halve_maxima()
                if nxt:
                    x_moments()
                if prev:
                    hidden_moments()
                    final(0)
                if nxt:
                    x_low(0)
                    x_low(1)
                if here:
                    probs_low(0)
                if nxt:
                    x_low(2)
                    x_low(3)
                if nxt and not here:
                    for tb in range(TB):
                        v_low(tb)
                for h in range(HEADS):
                    if nxt and h in QK_AT:
                        qk_low(*QK_AT[h])
                    if setup and h == W2_FROM - 1:
                        magnitude(1, wdown_in)
                        thresholds(1)
                        ternary(1, 0)
                        ternary(1, 1)
                    if setup and h >= W2_FROM:
                        for u in (2 * (h - W2_FROM), 2 * (h - W2_FROM) + 1):
                            turned16("w2", u)
                            if u + 2 < FC:
                                ternary(1, u + 2)
                    if prev and h in FINAL_AT:
                        final(FINAL_AT[h])
                    if here:
                        head_output(h)
                        if h + 1 < HEADS:
                            probs_low(h + 1)
                if here:
                    if nxt:
                        v_low(0)
                    o_low(0)
                    o_low(1)
                    y_moments(0)
                    o_low(2)
                    y_moments(1)
                    first_sum(0)
                    o_low(3)
                    y_moments(2)
                    first_sum(1)
                    y_moments(3)
                    first_sum(2)
                    if nxt:
                        v_low(1)
                    first_sum(3)
                    x2_low(0)
                    if nxt:
                        v_low(2)
                    x2_low(1)
                    if nxt:
                        v_low(3)
                    x2_low(2)
                    x2_low(3)
                if setup:
                    dve.wait_ge(c_full, 1)
                    V.tensor_copy(c_sum[:, :], down[:, :]).then_inc(c_ready, 1)

            run(dve, iteration)

        @block.gpsimd
        def _(pool):
            P = nc.gpsimd
            n_const = [0]

            def const(op):
                op.then_inc(consts, 1)
                n_const[0] += 1

            const(P.memset(ident32[:, :], 0.0))
            const(P.memset(mask_rows[:, :], 0.0))
            const(P.memset(m_stage, 0.0))
            const(P.memset(ones16[:, :], 1.0))
            const(P.memset(ones32[:, :], 1.0))
            const(P.memset(lift[:, :], BIAS_UP))
            const(P.memset(mhalf[:, :], -0.5))
            const(P.memset(mx[:, :], 0.0))
            const(P.memset(t16[:, 0, :], ROW_UP))
            const(P.memset(v_sb[:, :, :, HD:HD + 1], 1.0))
            P.memset(temp[:, 7168:8192], 0.0).then_inc(rows_zero, 1)
            pool.wait_ge(consts, 3)
            const(P.affine_select(out=ident32[:, :], in_=ident32[:, :], compare_op=ALU.not_equal, fill=1.0, base=0,
                                  pattern=[[-1, PARTS]], channel_multiplier=1))
            const(P.affine_select(out=mask_rows[:, 3 * PARTS:T], in_=mask_rows[:, 3 * PARTS:T], compare_op=ALU.is_ge,
                                  fill=NEG, base=0, pattern=[[-1, PARTS]], channel_multiplier=1))
            const(P.affine_select(out=m_stage, in_=m_stage, compare_op=ALU.is_ge, fill=NEG, base=0,
                                  pattern=[[1, PARTS]], channel_multiplier=-1))
            assert n_const[0] == CONSTS
            pool.wait_ge(rope_in, 16)

            def crossed(out, w, n):
                o2 = out.rearrange("p (a e two) -> p a e two", a=2, two=2)
                w2 = w.rearrange("p (a e two) -> p a e two", a=2, two=2)
                s2 = rope_sb[0:n, E:2 * E].rearrange("p (e two) -> p e two", two=2)
                for k in range(2):
                    sin = s2[:, :, k].unsqueeze(1).to_broadcast([n, 2, E // 2])
                    P.tensor_tensor(o2[:, :, :, k], w2[:, :, :, 1 - k], sin, ALU.mult).then_inc(rot_cross, 1)

            for c in range(EC):
                pool.wait_ge(wqk_in[c], 16)
                if c >= 2:
                    pool.wait_ge(rot_done, c - 1)
                crossed(rot2[:, c % 2, :], wa_in[:, c, 0:2 * E], PARTS)
            pool.wait_ge(rows_in, 80)
            crossed(b_r2, b_row, 1)

            def iteration(j, prev, here, nxt, setup):
                def power(ln, tbs, terms_n, n):
                    pool.wait_ge(ln_terms[ln], terms_n)
                    width = tbs.stop - tbs.start
                    P.tensor_tensor(rstd[:, ln, tbs], veps[:, ln, tbs], mhalf[:, 0:width], ALU.pow
                                    ).then_inc(ln_pow[ln], 1)
                    pool.wait_ge(ln_pow[ln], n)
                    P.tensor_tensor(shift[:, ln, tbs], negm[:, ln, tbs], rstd[:, ln, tbs], ALU.mult
                                    ).then_inc(ln_ready[ln], 1)

                def power1(ln, b, tb):
                    n = TB * b + tb + 1
                    power(ln, slice(tb, tb + 1), n, n)

                def squares(u):
                    pool.wait_ge(h_full, FC * (j - 1) + u + 1)
                    n = 31 * (j - 1) + 2 * u
                    if u:
                        pool.wait_ge(sq_step, n - 1)
                    P.tensor_tensor(acc_add if u else acc, hT[:, HI, u, :], hT[:, HI, u, :], ALU.mult
                                    ).then_inc(sq_step, 1)
                    if u:
                        pool.wait_ge(sq_step, n)
                        P.tensor_tensor(acc, acc, acc_add, ALU.add).then_inc(sq_step, 1)

                def finish(tb):
                    n = TB * (j - 1) + tb
                    pool.wait_ge(fin_ready, n + 1)
                    P.tensor_tensor(z[:, :], z[:, :], x1[:, tb, :], ALU.add).then_inc(out_ready, 1)

                if prev:
                    for u in range(FC):
                        squares(u)
                if nxt:
                    power(LX, slice(0, TB), j + 2, j + 2)
                if prev:
                    for tb in range(TB):
                        power1(LF, j - 1, tb)
                        finish(tb)
                if here:
                    power1(LP, j, 0)
                    power1(LP, j, 1)
                    power1(L1, j, 0)
                    power1(LP, j, 2)
                    power1(L1, j, 1)
                    power1(LP, j, 3)
                    power1(L1, j, 2)
                    power1(L1, j, 3)

            run(pool, iteration)


def rope_table():
    freqs = (np.float32(THETA) ** (-(np.arange(0, HD, 2, dtype=np.float32) / np.float32(HD)))).astype(np.float32)
    angle = np.outer(np.arange(HEADS, dtype=np.float32), freqs).astype(np.float32)
    cos = np.repeat(np.cos(angle), 2, axis=1).reshape(1, E)
    sin = np.stack([-np.sin(angle), np.sin(angle)], axis=-1).reshape(1, E)
    return np.concatenate([cos, sin], axis=1).astype(np.float32)


def kernel(L0_attn_x, L0_attn_w_attn, L0_attn_b_attn, L0_attn_w_proj, L0_attn_b_proj, L0_ffn_w_fc, L0_ffn_w_proj):
    import concourse.bacc as bacc
    from concourse.bass_utils import run_bass_kernel_spmd

    arrays = {
        "x": np.ascontiguousarray(L0_attn_x).reshape(BATCHES * T, E),
        "w_attn": np.ascontiguousarray(L0_attn_w_attn),
        "b_attn": np.ascontiguousarray(L0_attn_b_attn).reshape(1, 3 * E),
        "w_proj": np.ascontiguousarray(L0_attn_w_proj),
        "b_proj": np.ascontiguousarray(L0_attn_b_proj).reshape(1, E),
        "w_fc": np.ascontiguousarray(L0_ffn_w_fc),
        "w_down": np.ascontiguousarray(L0_ffn_w_proj),
        "rope": rope_table(),
    }
    nc = bacc.Bacc("TRN2", target_bir_lowering=False, num_devices=1)
    args = [nc.dram_tensor(n, a.shape, mybir.dt.float32, kind="ExternalInput").ap() for n, a in arrays.items()]
    out = nc.dram_tensor("out", (BATCHES * T, E), mybir.dt.float32, kind="ExternalOutput").ap()
    build(nc, *args, out)
    result = run_bass_kernel_spmd(nc, [arrays], core_ids=[0])
    return result.results[0]["out"].reshape(BATCHES, T, E)
```

```python
import numpy as np
from contextlib import ExitStack

import concourse.bass as bass
from concourse import mybir

BATCHES, T, E, HEADS = 8, 512, 512, 16
HD = E // HEADS
F = 4 * E
PARTS = 128
TB = T // PARTS
EC = E // PARTS
FC = F // PARTS
VW = 2 * HD + 1
THETA = 10000.0

W_UP = 16.0
S_UP = W_UP * W_UP
ROW_UP = 2.0 ** 15
P_LIFT = 12 * float(np.log(2.0))
BIAS_UP = 16.0
ATTN_SCALE = float(E) ** -0.5
PROJ_K = ATTN_SCALE / S_UP
P_UP = 1.0 / (PROJ_K * BIAS_UP)
EPS_LN, EPS_BIT = 1e-5, 1e-6
NEG = -1.0e30

QK_AT = {1: (0, 0), 2: (0, 1), 3: (1, 0), 4: (1, 1), 7: (2, 0), 8: (2, 1), 11: (3, 0), 12: (3, 1)}
DOWN_AT = {0: [(1, 0)], 5: [(1, 1), (1, 2)], 6: [(1, 3)], 9: [(2, 0), (2, 1)], 10: [(2, 2), (2, 3)],
           13: [(3, 0), (3, 1)], 14: [(3, 2), (3, 3)]}
FINAL_AT = {7: 1, 11: 2, 15: 3}
SQUARES_AT = 6
FINISH_AT = {6: 0, 8: 1, 12: 2}
W2_FROM = 5
STEP_MAX = {9: 0, 10: 1, 13: 2, 14: 3}
LATE_MAX = (4, 5, 6)
EARLY = len(STEP_MAX) + len(LATE_MAX)
MAX_AT = {0: 7, 2: 8, 4: 9, 6: 10, 8: 11, 9: 12, 10: 13, 11: 14, 12: 15}
SHIFT_AT = 13
X_AT = {7: 0, 9: 1, 11: 2, 14: 3}
X_NORM_AT = 5
CONSTS = 13


def general_plan(prev, here, nxt, setup):
    uses = []
    for u in range(FC):
        uses += [("up", u)] if prev else []
        uses += [("shift", 0)] if here and u == SHIFT_AT else []
        uses += [("xT", X_AT[u])] if nxt and u in X_AT else []
    if nxt and not here:
        uses += [("v", tb) for tb in range(TB)]
    for h in range(HEADS):
        uses += [("qk", QK_AT[h])] if nxt and h in QK_AT else []
    if here:
        for name, n in (("v", 0), ("v", 1), ("oT", 0), ("oT", 1), ("proj", 0), ("oT", 2), ("proj", 1),
                        ("oT", 3), ("proj", 2), ("proj", 3), ("v", 2), ("x2T", 0), ("v", 3), ("x2T", 1),
                        ("x2T", 2), ("x2T", 3)):
            if name != "v" or nxt:
                uses.append((name, n))
    return {name: k for k, name in enumerate(uses)}


N_FIRST = len(general_plan(False, False, True, False))
N_SETUP = len(general_plan(False, True, True, True))
N_USUAL = len(general_plan(True, True, True, False))
N_NO_NEXT = len(general_plan(True, True, False, False))
AFTER_O = N_USUAL - 1 - general_plan(True, True, True, False)["oT", 3]


def score_plan(here, nxt):
    uses = [("max", h) for h in range(EARLY, HEADS)] + [("scores", 0)] if here else []
    for h in range(HEADS):
        if nxt and here and h in STEP_MAX:
            uses.append(("next max", STEP_MAX[h]))
        if here and h + 1 < HEADS:
            uses.append(("scores", h + 1))
    if nxt:
        uses += [("next max", h) for h in (LATE_MAX if here else range(EARLY))]
    return {use: 3 * k for k, use in enumerate(uses)}


def score_base(j):
    return 0 if isinstance(j, int) and j < 0 else 6 * HEADS * j + 3 * EARLY


def general_base(j):
    if isinstance(j, int) and j <= 0:
        return 0 if j < 0 else N_FIRST
    if isinstance(j, int) and j == BATCHES:
        return N_FIRST + N_SETUP + N_USUAL * (BATCHES - 2) + N_NO_NEXT
    return N_USUAL * j + (N_FIRST + N_SETUP - N_USUAL)


def general_bank(j, k):
    at = general_base(j) if isinstance(j, int) else N_FIRST + N_SETUP
    return (at + k) % 3


assert N_USUAL % 3 == 0


def need(eng, semaphore, count):
    if not isinstance(count, int) or count > 0:
        eng.wait_ge(semaphore, count)


def build(nc, x, w_attn, b_attn, w_proj, b_proj, w_fc, w_down, rope, out):
    f32, f16, bf16 = mybir.dt.float32, mybir.dt.float16, mybir.dt.bfloat16
    ALU = mybir.AluOpType
    ACT = mybir.ActivationFunctionType
    AX = mybir.AxisListType
    HI, LO = 0, 1

    x_v = x.rearrange("(r p) e -> p r e", p=PARTS)
    out_v = out.rearrange("(r p) e -> r p e", p=PARTS)

    with ExitStack() as ctx:
        def sb(name, shape, dt):
            return ctx.enter_context(nc.sbuf_tensor(name, shape, dt))

        def sem(name):
            return ctx.enter_context(nc.semaphore(name))

        wa = sb("wa", [PARTS, 2, EC, 3 * E], f16)
        wp = sb("wp", [PARTS, 2, EC, E], f16)
        t1T = sb("t1T", [PARTS, EC, F], f16)
        t2T = sb("t2T", [PARTS, FC, E], f16)
        c_sum = sb("c_sum", [PARTS, E], f32)
        qk_bias = sb("qk_bias", [PARTS, 2 * EC], f32)
        v_bias = sb("v_bias", [PARTS, E], f16)
        p_bias = sb("p_bias", [PARTS, E], f16)
        lift = sb("lift", [PARTS, PARTS], f16)
        ones16 = sb("ones16", [PARTS, PARTS], f16)
        ones32 = sb("ones32", [PARTS, PARTS], f32)
        ident32 = sb("ident32", [PARTS, PARTS], f32)
        ident16 = sb("ident16", [PARTS, PARTS], f16)
        identb = sb("identb", [PARTS, PARTS], bf16)
        mask_b = sb("mask_b", [PARTS, PARTS], bf16)
        mask_rows = sb("mask_rows", [PARTS, T], f32)
        mhalf = sb("mhalf", [PARTS, TB], f32)
        qk = sb("qk", [PARTS, 2, HEADS, T], f16)
        v_sb = sb("v_sb", [PARTS, TB, HEADS, VW], f16)
        qkn = sb("qkn", [PARTS, 2, 4, T], f16)
        hT = sb("hT", [PARTS, 2, FC, T], f16)
        xT = sb("xT", [PARTS, 2, EC, T], f16)
        x2T = sb("x2T", [PARTS, 2, EC, T], f16)
        xo = sb("xo", [PARTS, TB, E], f32)
        xn = sb("xn", [PARTS, 2, E], f32)
        x1 = sb("x1", [PARTS, TB, E], f32)
        probs = sb("probs", [PARTS, 2, 2, 1280], f16)
        acc = sb("acc", [PARTS, T], f32)
        acc_add = sb("acc_add", [PARTS, T], f32)
        oA = sb("oA", [PARTS, TB, HD], f32)
        r_sum = sb("r_sum", [PARTS, TB], f32)
        mx = sb("mx", [PARTS, PARTS], f32)
        m_f = sb("m_f", [HEADS * TB, PARTS], f32)
        m_half = sb("m_half", [HEADS * TB, 2, PARTS], f16)
        bn = sb("bn", [PARTS, 4, TB, 6], f32)
        mv = sb("mv", [PARTS, 4, TB, 2], f32)
        veps = sb("veps", [PARTS, 4, TB], f32)
        negm = sb("negm", [PARTS, 4, TB], f32)
        rstd = sb("rstd", [PARTS, 4, TB], f32)
        shift = sb("shift", [PARTS, 4, TB], f32)
        h_negm = sb("h_negm", [PARTS, TB], f32)
        h_msq = sb("h_msq", [PARTS, TB], f32)
        h_var = sb("h_var", [PARTS, TB], f32)
        e_fin = sb("e_fin", [PARTS, TB], f32)
        spare = sb("spare", [PARTS, 1], f32)
        gs = sb("gs", [PARTS, 2 * EC], f32)
        gt = sb("gt", [PARTS, 2], f32)
        gam = sb("gam", [PARTS, 2], f32)
        theta = sb("theta", [PARTS, 2, 2], f32)
        g_sq = sb("g_sq", [PARTS, 2], f32)
        c_fin = sb("c_fin", [PARTS, 1], f32)
        LX, LP, L1, LF = range(4)
        PIECES = EC
        len_piece = FC * E // PIECES
        stage = hT[:, :, :, :].rearrange("p a c t -> p (a c t)").bitcast(f32)
        wa_in = stage[:, 0:EC * 3 * E].rearrange("p (c n) -> p c n", c=EC)
        y_sb = stage[:, 0:2 * E].rearrange("p (r e) -> p r e", r=2)
        xres = stage[:, 2 * E:6 * E].rearrange("p (b e) -> p b e", b=TB)
        oT = hT[:, 1, 8:12, :].rearrange("p c t -> p (c t)").rearrange(
            "p (r a c t) -> p r a c t", r=2, a=2, c=EC)
        temp = qk[:, :, :, :].rearrange("p a h t -> p (a h t)").bitcast(f32)
        rot1 = temp[:, 0:2048].rearrange("p (r n) -> p r n", r=2)
        rot2 = temp[:, 2048:4096].rearrange("p (r n) -> p r n", r=2)
        b_row, b_r1, b_r2 = (temp[0:1, 4096 + 1024 * i:5120 + 1024 * i] for i in range(3))
        vb_in, pb_in = temp[:, 7168:7680], temp[:, 7680:8192]
        rope_sb = probs[:, 0, :, :].rearrange("p a n -> p (a n)").bitcast(f32)[:, 0:2 * E]
        m_stage = acc[:, 0:PARTS]
        t16 = acc_add[:, :].bitcast(f16).rearrange("p (r e) -> p r e", r=2)
        below = acc[:, :].bitcast(f16).rearrange("p (r e) -> p r e", r=2)
        x2T_junk = x2T[:, 0, :, :].rearrange("p c t -> p (c t)")
        score = [ctx.enter_context(nc.psum_tensor(f"score{i}", [PARTS, 512], f32)) for i in range(3)]
        gen = [ctx.enter_context(nc.psum_tensor(f"gen{i}", [PARTS, 512], f32)) for i in range(3)]
        pv = ctx.enter_context(nc.psum_tensor("pv", [PARTS, 512], f32))
        down = ctx.enter_context(nc.psum_tensor("down", [PARTS, 512], f32))
        SQ_STEPS = 3 * FC
        H_SUM, H_SQ = 264, 268

        x_in, xres_in = sem("x_in"), sem("xres_in")
        wv_in, wp_in, rope_in, rows_in = sem("wv_in"), sem("wp_in"), sem("rope_in"), sem("rows_in")
        wqk_in = [sem(f"wqk_in{c}") for c in range(EC)]
        wfc_in, wdown_in = ([sem(f"{n}{i}") for i in range(PIECES)] for n in ("wfc_in", "wdown_in"))
        stacked = [sem(f"stacked{g}") for g in range(4)]
        shift_rows = sem("shift_rows")
        stored = [sem(f"stored{i}") for i in range(2)]
        consts, rows_zero, ident_copy, k_rows = (
            sem(n) for n in ("consts", "rows_zero", "ident_copy", "k_rows"))
        wv_hi, wp_hi, rot_cross, rot_step, rot_done, wqk_hi = (
            sem(n) for n in ("wv_hi", "wp_hi", "rot_cross", "rot_step", "rot_done", "wqk_hi"))
        w_low, w_ready, bias_step, bias_cols = (sem(n) for n in ("w_low", "w_ready", "bias_step", "bias_cols"))
        g_sums, g_step, g_total, tern_half, tern_ready, sign_full, sign_drained = (
            sem(n) for n in ("g_sums", "g_step", "g_total", "tern_half", "tern_ready", "sign_full", "sign_drained"))
        c_full, c_ready = sem("c_full"), sem("c_ready")
        g_full, g_drained = sem("g_full"), sem("g_drained")
        s_full, s_drained = sem("s_full"), sem("s_drained")
        pv_full, pv_drained = sem("pv_full"), sem("pv_drained")
        down_full, down_drained = sem("down_full"), sem("down_drained")
        hsum_full, hsq_full = sem("hsum_full"), sem("hsq_full")
        xn_ready, xT_hi, v_hi, qk_hi, h_full, exp_full = (
            sem(n) for n in ("xn_ready", "xT_hi", "v_hi", "qk_hi", "h_full", "exp_full"))
        gelu_done = sem("gelu_done")
        oT_hi, y_copied, xb_ready, xn2_ready, x2T_hi, fin_ready = (
            sem(n) for n in ("oT_hi", "y_copied", "xb_ready", "xn2_ready", "x2T_hi", "fin_ready"))
        m_neg, m_hi, o_sums, o_recip, o_ready, x1_ready = (
            sem(n) for n in ("m_neg", "m_hi", "o_sums", "o_recip", "o_ready", "x1_ready"))
        bn_done = [sem(f"bn_done{i}") for i in range(4)]
        mv_done = [sem(f"mv_done{i}") for i in range(4)]
        ln_terms = [sem(f"ln_terms{i}") for i in range(4)]
        h_step, h_terms = sem("h_step"), sem("h_terms")
        ln_pow = [sem(f"ln_pow{i}") for i in range(4)]
        ln_ready = [sem(f"ln_ready{i}") for i in range(4)]
        sq_step, out_ready = sem("sq_step"), sem("out_ready")

        signs = down[:, :].bitcast(f16)[:, 0:512]

        def w2_chunks(setup, h):
            at = 2 * (h - W2_FROM)
            return (at, at + 1) if setup and 0 <= at < FC else ()

        def block_at(s, tb):
            if s == tb:
                return PARTS * s
            return 512 + (PARTS * (tb - 1) if s == 0 else 384 if s == 2 else 512 + PARTS * (tb - 2))

        SCORE_W = (512, 512, 256)
        usual = (True, True, True, False)
        first = [(-1, False, False, True, False), (0, False, True, True, True), (1, *usual)]
        last = [(BATCHES - 1, True, True, False, False), (BATCHES, True, False, False, False)]

        def run(eng, iteration):
            for j, *what in first:
                iteration(j, *what)
            with eng.Fori(2, BATCHES - 1) as j:
                iteration(j, *usual)
            for j, *what in last:
                iteration(j, *what)

        block = ctx.enter_context(nc.Block())

        @block.sync
        def _(sp):
            sp.dma_start(xo[:, :, :], x_v[:, 0:TB, :]).then_inc(x_in, 16)
            wa_v = w_attn.rearrange("(c p) n -> p c n", p=PARTS)
            sp.dma_start(rope_sb.unsqueeze(1), rope.partition_broadcast(PARTS)).then_inc(rope_in, 16)
            sp.dma_start(wa_in[:, :, 2 * E:3 * E], wa_v[:, :, 2 * E:3 * E]).then_inc(wv_in, 16)
            for c in range(EC):
                sp.dma_start(wa_in[:, c, 0:2 * E], wa_v[:, c, 0:2 * E]).then_inc(wqk_in[c], 16)
            sp.wait_ge(rows_zero, 1)
            for p in (0, 32):
                sp.dma_start(vb_in[p:p + 1, :], b_attn[:, 2 * E:3 * E]).then_inc(rows_in, 16)
                sp.dma_start(pb_in[p:p + 1, :], b_proj[:, :]).then_inc(rows_in, 16)
            sp.dma_start(b_row, b_attn[:, 0:2 * E]).then_inc(rows_in, 16)
            sp.dma_start(x1[:, :, :], w_proj.rearrange("(c p) n -> p c n", p=PARTS)).then_inc(wp_in, 16)
            sp.wait_ge(w_low, 2 + EC)
            for i in range(PIECES):
                per = FC // PIECES
                sp.dma_start(stage[:, len_piece * i:len_piece * (i + 1)].rearrange("p (u d) -> p u d", u=per),
                             w_fc.rearrange("(u p) d -> p u d", p=PARTS)[:, per * i:per * (i + 1), :]
                             ).then_inc(wfc_in[i], 16)
            sp.wait_ge(w_ready, 2)
            sp.dma_start(qk[96:98, 1, :, :], t16[96:98, 0, :].unsqueeze(1).to_broadcast([2, HEADS, T])
                         ).then_inc(k_rows, 16)

            def iteration(j, prev, here, nxt, setup):
                G, g0 = general_plan(prev, here, nxt, setup), general_base(j)
                S, s0 = score_plan(here, nxt), score_base(j)
                if nxt and here:
                    row = TB * (j + 1) if isinstance(j, int) else sp.snap(TB * (j + 1))
                    need(sp, xn_ready, TB * (j + 1))
                    if not setup:
                        sp.wait_ge(g_full, g0 - AFTER_O)
                    sp.dma_start(xo[:, :, :], x_v[:, bass.ds(row, TB), :]).then_inc(x_in, 16)
                if here:
                    sp.wait_ge(g_drained, g0 + G["shift", 0] + 1)
                    for half in (HI, LO):
                        sp.dma_start(qk[96 + half:97 + half, 0, :, :].rearrange("o h (b t) -> o (h b) t", b=TB),
                                     m_half[:, half, :]).then_inc(shift_rows, 16)
                if setup:
                    sp.wait_ge(tern_ready, FC)
                    for i in range(PIECES):
                        sp.dma_start(stage[:, len_piece * i:len_piece * (i + 1)], w_down[PARTS * i:PARTS * (i + 1), :]
                                     ).then_inc(wdown_in[i], 16)

                def store(tb):
                    row = TB * (j - 1) + tb if isinstance(j, int) else sp.snap(TB * (j - 1) + tb)
                    sp.wait_ge(out_ready, TB * (j - 1) + tb + 1)
                    sp.dma_start(out_v[bass.ds(row, 1), :, :].rearrange("r p e -> p (r e)"), xn[:, tb % 2, :]
                                 ).then_inc(stored[tb % 2], 16)

                def stack(g):
                    if here:
                        n = max(4 * g + 3, max(h for h, what in QK_AT.items() if what[0] == g) + 2)
                        sp.wait_ge(s_full, s0 + S["scores", n] + 3)
                    else:
                        sp.wait_ge(g_drained, g0 + G["qk", (g, 1)] + 1)
                    for i in range(4):
                        src = qkn[HD * i:HD * (i + 1), g % 2, :, :]
                        head = qk[:, :, 4 * g + i, :]
                        sp.dma_start(head[0:32, :, :], src[:, 1:3, :]).then_inc(stacked[g], 16)
                        sp.dma_start(head[32:64, :, :], src[:, 0:3:2, :]).then_inc(stacked[g], 16)
                        sp.dma_start(head[64:96, :, :], src[:, 1:4:2, :]).then_inc(stacked[g], 16)

                for g in range(4):
                    if g == 3 and here:
                        if prev:
                            sp.wait_ge(down_full, TB * j)
                        if setup:
                            sp.wait_ge(tern_ready, 2 * FC)
                        row = TB * j if isinstance(j, int) else sp.snap(TB * j)
                        sp.dma_start(xres, x_v[:, bass.ds(row, TB), :]).then_inc(xres_in, 16)
                    if nxt:
                        stack(g)
                    if prev:
                        for tb in ((), (0, 1), (2,), (3,))[g]:
                            store(tb)

            run(sp, iteration)
            for half in stored:
                sp.wait_ge(half, 16 * 2 * BATCHES)

        @block.tensor
        def _(pe):
            pe.wait_ge(consts, CONSTS)
            pe.wait_ge(ident_copy, 3)

            def bias_columns():
                pe.wait_ge(bias_step, 4)
                for i in range(2 * EC):
                    mm = nc.tensor.matmul(down[:, i:i + 1], b_r1[:, PARTS * i:PARTS * (i + 1)], ones32[0:1, 0:1],
                                          start=True, stop=True)
                mm.then_inc(bias_cols, 1)

            def gamma_total(m):
                pe.wait_ge(g_step, 5 * m + 1)
                if m:
                    pe.wait_ge(sign_drained, FC)
                nc.tensor.matmul(down[:, m:m + 1], ones32[:, :], gt[:, m:m + 1], start=True, stop=True
                                 ).then_inc(g_total, 1)

            def sign_turn(n):
                pe.wait_ge(tern_ready, n + 1)
                if n:
                    pe.wait_ge(sign_drained, n)
                for c in range(EC):
                    mm = nc.tensor.transpose(signs[:, PARTS * c:PARTS * (c + 1)],
                                             t16[:, n % 2, PARTS * c:PARTS * (c + 1)], ident16[:, :])
                mm.then_inc(sign_full, 1)

            def iteration(j, prev, here, nxt, setup):
                G, g0 = general_plan(prev, here, nxt, setup), general_base(j)
                S, s0 = score_plan(here, nxt), score_base(j)

                def claim(name, n):
                    k = G[name, n]
                    need(pe, g_drained, g0 + k - 2)
                    return gen[general_bank(j, k)]

                def drained(name, n):
                    pe.wait_ge(g_drained, g0 + G[name, n] + 1)

                def claim_score(use, i):
                    need(pe, s_drained, s0 + S[use] + i - 2)
                    return score[i]

                def turn(bank, block, n=EC):
                    for c in range(n):
                        mm = nc.tensor.transpose(bank[:, PARTS * c:PARTS * (c + 1)], block(c), ident32[:, :])
                    return mm

                def products(bank, pairs, stop=True):
                    for n, (a, b) in enumerate(pairs):
                        mm = nc.tensor.matmul(bank[:, :], a, b, start=(n == 0), stop=(n == len(pairs) - 1))
                    return mm

                def up(u):
                    bank = claim("up", u)
                    cols = slice(PARTS * u, PARTS * (u + 1))
                    products(bank, [(t1T[:, c, cols], x2T[:, half, c, :]) for c in range(EC) for half in (HI, LO)]
                             ).then_inc(g_full, 1)

                def hidden_sums(u):
                    drained("up", u)
                    for half in (HI, LO):
                        for tb in range(TB):
                            first, final = u == 0 and half == HI, u == FC - 1 and half == LO
                            mm = nc.tensor.matmul(pv[:, H_SUM + tb:H_SUM + tb + 1],
                                                  hT[:, half, u, PARTS * tb:PARTS * (tb + 1)], ones16[:, 0:1],
                                                  start=first and tb == 0, stop=final, skip_group_check=True)
                    if u == FC - 1:
                        mm.then_inc(hsum_full, 1)

                def square_sums():
                    pe.wait_ge(sq_step, SQ_STEPS * j if here else SQ_STEPS * (j - 1) + FC - 1)
                    for tb in range(TB):
                        mm = nc.tensor.matmul(pv[:, H_SQ + tb:H_SQ + tb + 1], acc[:, PARTS * tb:PARTS * (tb + 1)],
                                              ones32[:, 0:1], start=True, stop=True)
                    mm.then_inc(hsq_full, 1)

                def ffn_down(tb, part):
                    if part == 0:
                        need(pe, down_drained, TB * (j - 1) + tb)
                    for u in range(4 * part, 4 * part + 4):
                        for half in (HI, LO):
                            mm = nc.tensor.matmul(down[:, :], hT[:, half, u, PARTS * tb:PARTS * (tb + 1)], t2T[:, u, :],
                                                  start=(u == 0 and half == HI), stop=(u == FC - 1 and half == LO))
                    if part == 3:
                        mm.then_inc(down_full, 1)

                def max_pass(u, ahead=0):
                    if u % 4 == 0:
                        pe.wait_ge(stacked[u // 4], 192 * (j + ahead + 1))
                    for i, tbs in enumerate(((3,), (0, 2), (1,))):
                        bank = claim_score(("next max" if ahead else "max", u), i)
                        at = 0
                        for tb in tbs:
                            n = PARTS * (tb + 1)
                            mm = nc.tensor.matmul(bank[:, at:at + n], qk[0:96, 0, u, PARTS * tb:PARTS * (tb + 1)],
                                                  qk[0:96, 1, u, 0:n], start=(at == 0), stop=True,
                                                  skip_group_check=True)
                            at += n
                        mm.then_inc(s_full, 1)

                def scores(h):
                    def part(bank, at, s, t0, t1, start):
                        return nc.tensor.matmul(bank[:, at:at + t1 - t0], qk[0:98, 1, h, PARTS * s:PARTS * (s + 1)],
                                                qk[0:98, 0, h, t0:t1], start=start, stop=True, skip_group_check=True)
                    if h == 0:
                        pe.wait_ge(k_rows, 16)
                        pe.wait_ge(shift_rows, 32 * (j + 1))
                    bank = claim_score(("scores", h), 0)
                    nc.tensor.matmul(bank[:, :].rearrange("p (b t) -> p b t", b=TB), identb[:, :],
                                     mask_b[:, :].unsqueeze(1).to_broadcast([PARTS, TB, PARTS]),
                                     start=True, stop=False, skip_group_check=True)
                    for s in range(TB):
                        mm = part(bank, PARTS * s, s, PARTS * s, PARTS * (s + 1), False)
                    mm.then_inc(s_full, 1)
                    bank = claim_score(("scores", h), 1)
                    part(bank, 0, 0, PARTS, T, True)
                    part(bank, 384, 2, 3 * PARTS, T, False).then_inc(s_full, 1)
                    bank = claim_score(("scores", h), 2)
                    part(bank, 0, 1, 2 * PARTS, T, True).then_inc(s_full, 1)

                def weigh(h):
                    pe.wait_ge(s_drained, s0 + S["scores", h] + 3)
                    need(pe, pv_drained, HEADS * j + h)
                    if prev and here and h == SQUARES_AT:
                        square_sums()
                    for tb in range(TB):
                        for s in range(tb + 1):
                            for half in (HI, LO):
                                at = block_at(s, tb)
                                mm = nc.tensor.matmul(pv[:, VW * tb:VW * (tb + 1)],
                                                      probs[:, h % 2, half, at:at + PARTS], v_sb[:, s, h, :],
                                                      start=(s == 0 and half == HI), stop=(s == tb and half == LO))
                    mm.then_inc(pv_full, 1)

                def x_turn(tb):
                    pe.wait_ge(xn_ready, TB * (j + 1) + tb + 1)
                    bank = claim("xT", tb)
                    turn(bank, lambda c: xn[:, tb % 2, PARTS * c:PARTS * (c + 1)]).then_inc(g_full, 1)

                def values(tb):
                    if not here and tb == 0:
                        drained("xT", 3)
                    bank = claim("v", tb)
                    rows = slice(PARTS * tb, PARTS * (tb + 1))
                    cols = slice(2 * E, 3 * E)
                    products(bank, [(xT[:, a, c, rows], wa[:, b, c, cols]) for c in range(EC)
                                    for a, b in ((HI, HI), (HI, LO), (LO, HI))] + [(lift[:, :], v_bias[:, :])]
                             ).then_inc(g_full, 1)

                def queries_keys(g, which):
                    if (g, which) == (0, 0) and here:
                        drained("xT", 3)
                    bank = claim("qk", (g, which))
                    cols = slice(E * which + PARTS * g, E * which + PARTS * (g + 1))
                    products(bank, [(wa[:, a, c, cols], xT[:, b, c, :]) for c in range(EC)
                                    for a, b in ((HI, HI), (HI, LO), (LO, HI))]).then_inc(g_full, 1)

                def o_turn(tb):
                    if tb == 0:
                        pe.wait_ge(o_ready, HEADS * (j + 1))
                    bank = claim("oT", tb)
                    turn(bank, lambda c: xo[:, tb, PARTS * c:PARTS * (c + 1)]).then_inc(g_full, 1)

                def project(tb):
                    if setup and tb == 0:
                        pe.wait_ge(w_ready, 3)
                    drained("oT", tb)
                    bank = claim("proj", tb)
                    products(bank, [(oT[:, tb % 2, a, c, :], wp[:, b, c, :]) for c in range(EC)
                                    for a, b in ((HI, HI), (HI, LO), (LO, HI))] + [(lift[:, :], p_bias[:, :])]
                             ).then_inc(g_full, 1)

                def x2_turn(tb):
                    pe.wait_ge(xn2_ready, TB * j + tb + 1)
                    bank = claim("x2T", tb)
                    turn(bank, lambda c: xn[:, tb % 2, PARTS * c:PARTS * (c + 1)]).then_inc(g_full, 1)

                if setup:
                    gamma_total(0)
                for u in range(FC):
                    if prev:
                        if u == 0:
                            pe.wait_ge(g_drained, g0)
                        up(u)
                        if u >= 2:
                            hidden_sums(u - 2)
                    if here and u in MAX_AT:
                        max_pass(MAX_AT[u])
                    if setup:
                        sign_turn(u)
                    if here and u == SHIFT_AT:
                        pe.wait_ge(s_drained, s0 + S["max", HEADS - 1] + 3)
                        bank = claim("shift", 0)
                        nc.tensor.transpose(bank[:, 0:PARTS], mx[:, :], ident32[:, :]).then_inc(g_full, 1)
                    if nxt and u in X_AT:
                        x_turn(X_AT[u])
                if prev:
                    ffn_down(0, 0)
                    ffn_down(0, 1)
                    hidden_sums(FC - 2)
                    hidden_sums(FC - 1)
                if here:
                    scores(0)
                if prev:
                    ffn_down(0, 2)
                    ffn_down(0, 3)
                    if not here:
                        square_sums()
                if nxt and not here:
                    pe.wait_ge(w_low, 2)
                    for tb in range(TB):
                        values(tb)
                    bias_columns()
                    pe.wait_ge(w_low, 2 + EC)
                for h in range(HEADS):
                    if nxt and h in QK_AT:
                        queries_keys(*QK_AT[h])
                    if setup and h == W2_FROM - 1:
                        gamma_total(1)
                    for u in w2_chunks(setup, h):
                        sign_turn(FC + u)
                    pieces = DOWN_AT.get(h, ()) if prev else ()
                    if h and pieces:
                        ffn_down(*pieces[0])
                    if here and nxt and h in STEP_MAX:
                        max_pass(STEP_MAX[h], 1)
                    for tb, part in pieces[1:]:
                        ffn_down(tb, part)
                    if here:
                        if h + 1 < HEADS:
                            scores(h + 1)
                        elif nxt:
                            values(0)
                        weigh(h)
                    if h == 0 and pieces:
                        ffn_down(*pieces[0])
                if nxt and not here:
                    for u in range(EARLY):
                        max_pass(u, 1)
                if here:
                    if nxt:
                        values(1)
                    o_turn(0)
                    o_turn(1)
                    if nxt:
                        max_pass(LATE_MAX[0], 1)
                    project(0)
                    o_turn(2)
                    project(1)
                    o_turn(3)
                    project(2)
                    project(3)
                    if nxt:
                        values(2)
                    x2_turn(0)
                    if nxt:
                        max_pass(LATE_MAX[1], 1)
                        values(3)
                    x2_turn(1)
                    x2_turn(2)
                    if nxt:
                        max_pass(LATE_MAX[2], 1)
                    x2_turn(3)
                if setup:
                    pe.wait_ge(sign_drained, 2 * FC)
                    for u in range(FC):
                        mm = nc.tensor.matmul(down[:, :], ones16[:, :], t2T[:, u, :], start=(u == 0), stop=(u == FC - 1))
                    mm.then_inc(c_full, 1)

            run(pe, iteration)

        @block.scalar
        def _(act):
            def high(out, in_, bias=None, scale=1.0):
                if bias is None:
                    return nc.scalar.activation(out, in_, ACT.Copy, scale=scale)
                return nc.scalar.activation(out, in_, ACT.Identity, bias=bias, scale=scale)

            def iteration(j, prev, here, nxt, setup):
                G, g0 = general_plan(prev, here, nxt, setup), general_base(j)
                S, s0 = score_plan(here, nxt), score_base(j)

                def filled(name, n):
                    k = G[name, n]
                    act.wait_ge(g_full, g0 + k + 1)
                    return gen[general_bank(j, k)]

                def blocks(bank, n=PARTS):
                    return bank[:, :].rearrange("p (c t) -> p c t", t=n)

                def hidden(u):
                    bank = filled("up", u)
                    nc.scalar.activation(hT[:, HI, u, :], bank[:, :], ACT.Gelu, scale=gam[:, 0:1])
                    whole = nc.scalar.activation(bank[:, :], bank[:, :], ACT.Gelu, scale=gam[:, 0:1])
                    if not here:
                        whole.then_inc(gelu_done, 1)
                        if u >= 3:
                            act.wait_ge(sq_step, SQ_STEPS * (j - 1) + u - 2)
                        act.wait_ge(gelu_done, u + 1)
                        whole = nc.scalar.activation(xn[:, u % 2, :] if u else acc[:, :], bank[:, :], ACT.Square)
                    whole.then_inc(h_full, 1)

                def normalise(tb):
                    nc.scalar.activation(xn[:, tb % 2, :], xo[:, tb, :], ACT.Identity, bias=shift[:, LX, tb:tb + 1],
                                         scale=rstd[:, LX, tb:tb + 1]).then_inc(xn_ready, 1)

                def x_turned(tb):
                    high(xT[:, HI, :, PARTS * tb:PARTS * (tb + 1)], blocks(filled("xT", tb))).then_inc(xT_hi, 1)

                def values(tb):
                    bank = filled("v", tb)
                    if here and tb == 0:
                        act.wait_ge(pv_full, HEADS * (j + 1))
                    high(v_sb[:, tb, :, 0:HD], blocks(bank, HD)).then_inc(v_hi, 1)

                def queries_keys(g, which):
                    bank = filled("qk", (g, which))
                    if not here and (g, which) == (0, 0):
                        act.wait_ge(w_ready, 2)
                    if which == 0:
                        need(act, stacked[(g - 2) % 4], 192 * (j + 1 + (1 if g >= 2 else 0)))
                    high(qkn[:, g % 2, 1 + which, :], bank[:, :], bias=qk_bias[:, EC * which + g:EC * which + g + 1]
                         ).then_inc(qk_hi, 1)

                def exponents(h):
                    for i, n in enumerate(SCORE_W):
                        act.wait_ge(s_full, s0 + S["scores", h] + i + 1)
                        nc.scalar.activation(probs[:, h % 2, HI, 512 * i:512 * i + n], score[i][:, 0:n], ACT.Exp,
                                             scale=1.0 / S_UP)
                        nc.scalar.activation(score[i][:, 0:n], score[i][:, 0:n], ACT.Exp, scale=1.0 / S_UP
                                             ).then_inc(exp_full, 1)

                def final(tb):
                    act.wait_ge(ln_ready[LF], TB * (j - 1) + tb + 1)
                    nc.scalar.activation(xn[:, tb % 2, :], xn[:, tb % 2, :], ACT.Identity, bias=shift[:, LF, tb:tb + 1],
                                         scale=rstd[:, LF, tb:tb + 1]).then_inc(fin_ready, 1)

                def o_turned(tb):
                    high(oT[:, tb % 2, HI, :, :], blocks(filled("oT", tb))).then_inc(oT_hi, 1)

                def copy_y(tb):
                    bank = filled("proj", tb)
                    need(act, x1_ready, TB * j + tb - 1)
                    nc.scalar.activation(y_sb[:, tb % 2, :], bank[:, :], ACT.Copy).then_inc(y_copied, 1)

                def residual(tb):
                    if tb == 0:
                        act.wait_ge(xres_in, 16 * (j + 1))
                    act.wait_ge(ln_ready[LP], TB * j + tb + 1)
                    nc.scalar.activation(xres[:, tb, :], xres[:, tb, :], ACT.Identity, bias=shift[:, LP, tb:tb + 1]
                                         ).then_inc(xb_ready, 1)

                def normalise2(tb):
                    if tb < 2 and prev:
                        act.wait_ge(stored[tb], 16 * 2 * j)
                    act.wait_ge(ln_ready[L1], TB * j + tb + 1)
                    nc.scalar.activation(xn[:, tb % 2, :], x1[:, tb, :], ACT.Identity, bias=shift[:, L1, tb:tb + 1],
                                         scale=rstd[:, L1, tb:tb + 1]).then_inc(xn2_ready, 1)

                def x2_turned(tb):
                    high(x2T[:, HI, :, PARTS * tb:PARTS * (tb + 1)], blocks(filled("x2T", tb))).then_inc(x2T_hi, 1)

                def magnitudes(m, loaded):
                    for i in range(PIECES):
                        act.wait_ge(loaded[i], 16)
                        at = slice(len_piece * i, len_piece * (i + 1))
                        op = nc.scalar.activation(x2T_junk, stage[:, at], ACT.Abs,
                                                  accum_out=gs[:, PIECES * m + i:PIECES * m + i + 1])
                        op.then_inc(g_sums, 1)
                        act.wait_ge(g_sums, PIECES * m + i + 1)

                def sign_turned(n):
                    act.wait_ge(sign_full, n + 1)
                    u = n % FC
                    if n < FC:
                        dst = t1T[:, :, PARTS * u:PARTS * (u + 1)]
                    else:
                        dst = t2T[:, 4 * (u % 4):4 * (u % 4) + 4, PARTS * (u // 4):PARTS * (u // 4 + 1)]
                    nc.scalar.activation(dst, signs.rearrange("p (c t) -> p c t", t=PARTS), ACT.Copy
                                         ).then_inc(sign_drained, 1)

                if prev:
                    act.wait_ge(g_step, 12)
                if setup:
                    magnitudes(0, wfc_in)
                for u in range(FC):
                    if prev:
                        hidden(u)
                    if setup:
                        sign_turned(u)
                    if nxt and u == X_NORM_AT:
                        act.wait_ge(ln_ready[LX], j + 2)
                        normalise(0)
                        normalise(1)
                    if nxt and u in X_AT:
                        if X_AT[u] == 0:
                            if not here:
                                act.wait_ge(wv_in, 16)
                                high(wa[:, HI, :, 2 * E:3 * E], wa_in[:, :, 2 * E:3 * E], scale=W_UP
                                     ).then_inc(wv_hi, 1)
                        x_turned(X_AT[u])
                        if X_AT[u] + 2 < TB:
                            normalise(X_AT[u] + 2)
                if here:
                    exponents(0)
                if nxt and not here:
                    for c in range(EC):
                        act.wait_ge(rot_done, c + 1)
                        high(wa[:, HI, c, 0:2 * E], rot1[:, c % 2, :], scale=W_UP).then_inc(wqk_hi, 1)
                        values(c)
                for h in range(HEADS):
                    if nxt and h in QK_AT:
                        queries_keys(*QK_AT[h])
                    if setup and h == W2_FROM - 1:
                        magnitudes(1, wdown_in)
                    for u in w2_chunks(setup, h):
                        sign_turned(FC + u)
                    if prev and h in FINISH_AT:
                        final(FINISH_AT[h])
                    if here and h + 1 < HEADS:
                        exponents(h + 1)
                if nxt and not here:
                    act.wait_ge(wp_in, 16)
                    high(wp[:, HI, :, :], x1[:, :, :], scale=W_UP).then_inc(wp_hi, 1)
                if prev:
                    final(3)
                if here:
                    if nxt:
                        values(0)
                        values(1)
                    o_turned(0)
                    o_turned(1)
                    copy_y(0)
                    o_turned(2)
                    copy_y(1)
                    residual(0)
                    o_turned(3)
                    copy_y(2)
                    residual(1)
                    copy_y(3)
                    residual(2)
                    normalise2(0)
                    if nxt:
                        values(2)
                    residual(3)
                    normalise2(1)
                    x2_turned(0)
                    if nxt:
                        values(3)
                    normalise2(2)
                    x2_turned(1)
                    normalise2(3)
                    x2_turned(2)
                    x2_turned(3)

            run(act, iteration)

        @block.vector
        def _(dve):
            V = nc.vector

            def low(out, whole, hi):
                return V.tensor_tensor(out, whole, hi, ALU.subtract)

            dve.wait_ge(consts, CONSTS)
            V.tensor_copy(ident16[:, :], ident32[:, :]).then_inc(ident_copy, 1)
            V.tensor_copy(identb[:, :], ident32[:, :]).then_inc(ident_copy, 1)
            V.tensor_copy(mask_b[:, :], m_stage).then_inc(ident_copy, 1)

            def rotation(c):
                cos2 = rope_sb[:, 0:E].unsqueeze(1).to_broadcast([PARTS, 2, E])
                dve.wait_ge(wqk_in[c], 16)
                if c >= 2:
                    dve.wait_ge(w_low, 2 + c - 1)
                V.tensor_tensor(rot1[:, c % 2, :].rearrange("p (a e) -> p a e", a=2),
                                wa_in[:, c, 0:2 * E].rearrange("p (a e) -> p a e", a=2), cos2, ALU.mult
                                ).then_inc(rot_step, 1)

            def rotated_low(c):
                dve.wait_ge(wqk_hi, c + 1)
                V.scalar_tensor_tensor(out=wa[:, LO, c, 0:2 * E], in0=rot1[:, c % 2, :], scalar=W_UP,
                                       in1=wa[:, HI, c, 0:2 * E], op0=ALU.mult, op1=ALU.subtract).then_inc(w_low, 1)

            def value_weights():
                dve.wait_ge(wv_hi, 1)
                for c in range(EC):
                    last_op = V.scalar_tensor_tensor(out=wa[:, LO, c, 2 * E:3 * E], in0=wa_in[:, c, 2 * E:3 * E],
                                                     scalar=W_UP, in1=wa[:, HI, c, 2 * E:3 * E],
                                                     op0=ALU.mult, op1=ALU.subtract)
                last_op.then_inc(w_low, 1)
                dve.wait_ge(rows_in, 80)
                V.tensor_copy(v_bias[:, :], vb_in).then_inc(bias_step, 1)
                V.tensor_scalar(p_bias[:, :], pb_in, P_UP, None, ALU.mult).then_inc(bias_step, 1)
                dve.wait_ge(bias_step, 2)
                low(v_bias[32:33, :], vb_in[32:33, :], v_bias[32:33, :]).then_inc(w_low, 1)
                c_row = rope_sb[0:1, 0:E].unsqueeze(1).to_broadcast([1, 2, E])
                V.tensor_tensor(b_r1.rearrange("p (a e) -> p a e", a=2), b_row.rearrange("p (a e) -> p a e", a=2),
                                c_row, ALU.mult).then_inc(bias_step, 1)
                V.scalar_tensor_tensor(out=p_bias[32:33, :], in0=pb_in[32:33, :], scalar=P_UP,
                                       in1=p_bias[32:33, :], op0=ALU.mult, op1=ALU.subtract).then_inc(w_ready, 1)

            def biases():
                dve.wait_ge(bias_step, 3)
                dve.wait_ge(rot_cross, 2 * EC + 2)
                V.tensor_tensor(b_r1, b_r1, b_r2, ALU.add).then_inc(bias_step, 1)
                dve.wait_ge(bias_cols, 1)
                V.tensor_scalar(qk_bias[:, :], down[:, 0:2 * EC], W_UP, None, ALU.mult).then_inc(w_ready, 1)

            def projection_weights():
                dve.wait_ge(wp_hi, 1)
                for c in range(EC):
                    last_op = V.scalar_tensor_tensor(out=wp[:, LO, c, :], in0=x1[:, c, :], scalar=W_UP,
                                                     in1=wp[:, HI, c, :], op0=ALU.mult, op1=ALU.subtract)
                last_op.then_inc(w_ready, 1)

            def iteration(j, prev, here, nxt, setup):
                G, g0 = general_plan(prev, here, nxt, setup), general_base(j)
                S, s0 = score_plan(here, nxt), score_base(j)

                def bank_of(name, n):
                    return gen[general_bank(j, G[name, n])]

                def blocks(bank, n=PARTS):
                    return bank[:, :].rearrange("p (c t) -> p c t", t=n)

                def thresholds(m):
                    dve.wait_ge(g_sums, PIECES * (m + 1))
                    V.tensor_reduce(gt[:, m:m + 1], gs[:, PIECES * m:PIECES * (m + 1)], AX.X, ALU.add
                                    ).then_inc(g_step, 1)
                    dve.wait_ge(g_total, m + 1)
                    s0 = 1 + 5 * m
                    V.tensor_scalar(gam[:, m:m + 1], down[:, m:m + 1], 1.0 / (F * E), None, ALU.mult
                                    ).then_inc(g_step, 1)
                    dve.wait_ge(g_step, s0 + 1)
                    V.tensor_scalar(theta[:, m, 0:1], gam[:, m:m + 1], EPS_BIT, 0.5, ALU.add, ALU.mult
                                    ).then_inc(g_step, 1)
                    V.tensor_scalar(theta[:, m, 1:2], gam[:, m:m + 1], EPS_BIT, -0.5, ALU.add, ALU.mult
                                    ).then_inc(g_step, 1)
                    V.tensor_tensor(g_sq[:, m:m + 1], gam[:, m:m + 1], gam[:, m:m + 1], ALU.mult).then_inc(g_step, 1)
                    dve.wait_ge(g_step, s0 + 4)
                    if m == 1:
                        V.reciprocal(g_sq[:, 0:1], g_sq[:, 1:2]).then_inc(g_step, 1)
                        dve.wait_ge(g_step, s0 + 5)
                        V.tensor_scalar(c_fin[:, :], g_sq[:, 0:1], EPS_LN, None, ALU.mult).then_inc(g_step, 1)
                        dve.wait_ge(g_step, s0 + 6)

                def ternary(n):
                    m, u = divmod(n, FC)
                    dve.wait_ge(tern_half, n + 1)
                    if n >= 2:
                        dve.wait_ge(sign_full, n - 1)
                    V.scalar_tensor_tensor(out=t16[:, n % 2, :], in0=stage[:, E * u:E * (u + 1)],
                                           scalar=theta[:, m, 0:1], in1=below[:, n % 2, :], op0=ALU.is_gt,
                                           op1=ALU.subtract).then_inc(tern_ready, 1)

                def hidden_low(u):
                    dve.wait_ge(h_full, FC * (j - 1) + u + 1)
                    low(hT[:, LO, u, :], bank_of("up", u)[:, :], hT[:, HI, u, :]).then_inc(g_drained, 1)

                def maxima(u, ahead=0):
                    dve.wait_ge(s_full, s0 + S["next max" if ahead else "max", u] + 3)
                    V.tensor_copy(spare[:, :], mhalf[:, 0:1])
                    for i, tbs in enumerate(((3,), (0, 2), (1,))):
                        at = 0
                        for tb in tbs:
                            n = PARTS * (tb + 1)
                            part = score[i][:, at:at + n]
                            op = V.tensor_tensor_reduce(part, part, mask_rows[:, T - n:T], 1.0, -3.0e38, ALU.add,
                                                        ALU.max, mx[:, TB * u + tb:TB * u + tb + 1])
                            at += n
                        op.then_inc(s_drained, 1)

                def halve_maxima():
                    bank = bank_of("shift", 0)
                    dve.wait_ge(g_full, g0 + G["shift", 0] + 1)
                    V.tensor_scalar(m_f[:, :], bank[0:HEADS * TB, 0:PARTS], -1.0 / ROW_UP, P_LIFT * S_UP / ROW_UP,
                                    ALU.mult, ALU.add).then_inc(m_neg, 1)
                    dve.wait_ge(m_neg, j + 1)
                    V.tensor_copy(m_half[:, HI, :], m_f[:, :]).then_inc(m_hi, 1)
                    dve.wait_ge(m_hi, j + 1)
                    low(m_half[:, LO, :], m_f[:, :], m_half[:, HI, :]).then_inc(g_drained, 1)

                def moments(ln, tb):
                    V.tensor_scalar(negm[:, ln, tb:tb + 1], bn[:, ln, tb, 1:2], bn[:, ln, tb, 4:5], -0.5,
                                    ALU.add, ALU.mult)
                    V.bn_aggr(mv[:, ln, tb, :], bn[:, ln, tb, :]).then_inc(mv_done[ln], 1)

                def terms(ln, tbs, *var_ops):
                    V.tensor_scalar(veps[:, ln, tbs], mv[:, ln, tbs, 1], *var_ops).then_inc(ln_terms[ln], 1)

                def x_moments(tb):
                    if tb == 0:
                        dve.wait_ge(x_in, 16 * (j + 2))
                    V.bn_stats(bn[:, LX, tb, :], xo[:, tb, :]).then_inc(bn_done[LX], 1)
                    dve.wait_ge(bn_done[LX], TB * (j + 1) + tb + 1)
                    moments(LX, tb)
                    if tb == TB - 1:
                        dve.wait_ge(mv_done[LX], TB * (j + 2))
                        terms(LX, slice(0, TB), EPS_LN, None, ALU.add)

                def hidden_mean():
                    dve.wait_ge(hsum_full, j)
                    if not here:
                        dve.wait_ge(hsq_full, j)
                    V.tensor_scalar(h_negm[:, :], pv[:, H_SUM:H_SUM + TB], -1.0 / F, None, ALU.mult
                                    ).then_inc(h_step, 1)
                    dve.wait_ge(h_step, 3 * (j - 1) + 1)

                def hidden_variance():
                    if here:
                        dve.wait_ge(pv_full, HEADS * j + SQUARES_AT + 1)
                    dve.wait_ge(hsq_full, j)
                    V.tensor_tensor(h_msq[:, :], h_negm[:, :], h_negm[:, :], ALU.mult).then_inc(h_step, 1)
                    dve.wait_ge(h_step, 3 * (j - 1) + 2)
                    V.scalar_tensor_tensor(out=h_var[:, :], in0=pv[:, H_SQ:H_SQ + TB], scalar=1.0 / F,
                                           in1=h_msq[:, :], op0=ALU.mult, op1=ALU.subtract).then_inc(h_step, 1)
                    dve.wait_ge(h_step, 3 * (j - 1) + 3)
                    V.tensor_scalar(e_fin[:, :], h_var[:, :], EPS_BIT, c_fin[:, 0:1], ALU.add, ALU.mult
                                    ).then_inc(h_terms, 1)

                def final(tb):
                    n = TB * (j - 1) + tb
                    dve.wait_ge(down_full, n + 1)
                    need(dve, stored[tb % 2], 16 * (2 * (j - 1) + tb // 2))
                    V.scalar_tensor_tensor(out=xn[:, tb % 2, :], in0=c_sum[:, :], scalar=h_negm[:, tb:tb + 1],
                                           in1=down[:, :], op0=ALU.mult, op1=ALU.add).then_inc(down_drained, 1)
                    dve.wait_ge(down_drained, n + 1)
                    V.bn_stats(bn[:, LF, tb, :], xn[:, tb % 2, :]).then_inc(bn_done[LF], 1)
                    dve.wait_ge(bn_done[LF], n + 1)
                    moments(LF, tb)

                def final_terms(tb):
                    n = TB * (j - 1) + tb
                    if tb == 0:
                        dve.wait_ge(h_terms, j)
                    dve.wait_ge(mv_done[LF], n + 1)
                    V.tensor_tensor(veps[:, LF, tb:tb + 1], mv[:, LF, tb, 1:2], e_fin[:, tb:tb + 1], ALU.add
                                    ).then_inc(ln_terms[LF], 1)

                def x_low(tb):
                    dve.wait_ge(xT_hi, TB * (j + 1) + tb + 1)
                    cols = slice(PARTS * tb, PARTS * (tb + 1))
                    low(xT[:, LO, :, cols], blocks(bank_of("xT", tb)), xT[:, HI, :, cols]).then_inc(g_drained, 1)

                def v_low(tb):
                    dve.wait_ge(v_hi, TB * (j + 1) + tb + 1)
                    low(v_sb[:, tb, :, HD + 1:VW], blocks(bank_of("v", tb), HD), v_sb[:, tb, :, 0:HD]
                        ).then_inc(g_drained, 1)

                def qk_low(g, which):
                    dve.wait_ge(qk_hi, 8 * (j + 1) + 2 * g + which + 1)
                    V.scalar_tensor_tensor(out=qkn[:, g % 2, 3 * which, :], in0=bank_of("qk", (g, which))[:, :],
                                           scalar=qk_bias[:, EC * which + g:EC * which + g + 1],
                                           in1=qkn[:, g % 2, 1 + which, :], op0=ALU.add, op1=ALU.subtract
                                           ).then_inc(g_drained, 1)

                def probs_low(h):
                    for i, n in enumerate(SCORE_W):
                        dve.wait_ge(exp_full, 48 * j + 3 * h + i + 1)
                        at = 512 * i
                        low(probs[:, h % 2, LO, at:at + n], score[i][:, 0:n], probs[:, h % 2, HI, at:at + n]
                            ).then_inc(s_drained, 1)

                def head_output(h):
                    n = HEADS * j + h
                    dve.wait_ge(pv_full, n + 1)
                    res = pv[:, 0:VW * TB].rearrange("p (b w) -> p b w", b=TB)
                    V.reciprocal(r_sum[:, :], res[:, :, HD]).then_inc(o_recip, 1)
                    pairs = bass.AP(pv, 0, [[512, PARTS], [VW, TB], [1, HD], [HD + 1, 2]])
                    V.tensor_reduce(oA[:, :, :], pairs, AX.X, ALU.add).then_inc(pv_drained, 1)
                    if h == 0 and nxt:
                        dve.wait_ge(xn_ready, TB * (j + 2))
                    dve.wait_ge(o_recip, n + 1)
                    dve.wait_ge(pv_drained, n + 1)
                    V.tensor_tensor(xo[:, :, HD * h:HD * (h + 1)], oA[:, :, :],
                                    r_sum[:, :].unsqueeze(2).to_broadcast([PARTS, TB, HD]), ALU.mult
                                    ).then_inc(o_ready, 1)

                def o_low(tb):
                    dve.wait_ge(oT_hi, TB * j + tb + 1)
                    low(oT[:, tb % 2, LO, :, :], blocks(bank_of("oT", tb)), oT[:, tb % 2, HI, :, :]
                        ).then_inc(g_drained, 1)

                def y_moments(tb):
                    n = TB * j + tb
                    dve.wait_ge(y_copied, n + 1)
                    V.bn_stats(bn[:, LP, tb, :], bank_of("proj", tb)[:, :]).then_inc(g_drained, 1)
                    dve.wait_ge(g_drained, g0 + G["proj", tb] + 1)
                    moments(LP, tb)
                    dve.wait_ge(mv_done[LP], n + 1)
                    terms(LP, slice(tb, tb + 1), EPS_LN / PROJ_K ** 2, None, ALU.add)

                def first_sum(tb):
                    n = TB * j + tb
                    dve.wait_ge(xb_ready, n + 1)
                    V.scalar_tensor_tensor(out=x1[:, tb, :], in0=y_sb[:, tb % 2, :], scalar=rstd[:, LP, tb:tb + 1],
                                           in1=xres[:, tb, :], op0=ALU.mult, op1=ALU.add).then_inc(x1_ready, 1)
                    dve.wait_ge(x1_ready, n + 1)
                    V.bn_stats(bn[:, L1, tb, :], x1[:, tb, :]).then_inc(bn_done[L1], 1)
                    dve.wait_ge(bn_done[L1], n + 1)
                    moments(L1, tb)
                    dve.wait_ge(mv_done[L1], n + 1)
                    terms(L1, slice(tb, tb + 1), 1.0 + EPS_BIT, EPS_LN * EPS_BIT, ALU.mult, ALU.add)

                def x2_low(tb):
                    dve.wait_ge(x2T_hi, TB * j + tb + 1)
                    cols = slice(PARTS * tb, PARTS * (tb + 1))
                    low(x2T[:, LO, :, cols], blocks(bank_of("x2T", tb)), x2T[:, HI, :, cols]).then_inc(g_drained, 1)

                if setup:
                    thresholds(0)
                    dve.wait_ge(k_rows, 16)
                    ternary(0)
                    ternary(1)
                for u in range(FC):
                    if here and u in MAX_AT:
                        maxima(MAX_AT[u])
                    if prev:
                        hidden_low(u)
                    if here and u == SHIFT_AT:
                        halve_maxima()
                    if nxt and u < TB:
                        x_moments(u)
                    if nxt and not here and u == X_NORM_AT:
                        rotation(0)
                        rotation(1)
                    if nxt and u in X_AT:
                        x_low(X_AT[u])
                    if setup and u + 2 < FC:
                        ternary(u + 2)
                if prev:
                    hidden_mean()
                    if not here:
                        hidden_variance()
                    final(0)
                    if not here:
                        final_terms(0)
                if here:
                    probs_low(0)
                if nxt and not here:
                    value_weights()
                    for c in range(EC):
                        dve.wait_ge(rot_step, c + 1)
                        dve.wait_ge(rot_cross, 2 * c + 2)
                        V.tensor_tensor(rot1[:, c % 2, :], rot1[:, c % 2, :], rot2[:, c % 2, :], ALU.add
                                        ).then_inc(rot_done, 1)
                        if c >= 1:
                            rotated_low(c - 1)
                            if c + 1 < EC:
                                rotation(c + 1)
                            v_low(c - 1)
                    rotated_low(EC - 1)
                    v_low(TB - 1)
                    biases()
                for h in range(HEADS):
                    if nxt and h in QK_AT:
                        qk_low(*QK_AT[h])
                    if setup and h == W2_FROM - 1:
                        thresholds(1)
                        ternary(FC)
                        ternary(FC + 1)
                    if prev and here and h == SQUARES_AT:
                        hidden_variance()
                        final_terms(0)
                    if prev and h in FINAL_AT:
                        final(FINAL_AT[h])
                        final_terms(FINAL_AT[h])
                    if here:
                        if nxt and h in STEP_MAX:
                            maxima(STEP_MAX[h], 1)
                        head_output(h)
                        if h + 1 < HEADS:
                            probs_low(h + 1)
                    for u in w2_chunks(setup, h):
                        if u + 2 < FC:
                            ternary(FC + u + 2)
                if nxt and not here:
                    projection_weights()
                    for u in range(EARLY):
                        maxima(u, 1)
                if here:
                    if nxt:
                        v_low(0)
                        v_low(1)
                    o_low(0)
                    o_low(1)
                    if nxt:
                        maxima(LATE_MAX[0], 1)
                    y_moments(0)
                    o_low(2)
                    y_moments(1)
                    o_low(3)
                    first_sum(0)
                    y_moments(2)
                    first_sum(1)
                    y_moments(3)
                    first_sum(2)
                    if nxt:
                        v_low(2)
                    first_sum(3)
                    x2_low(0)
                    if nxt:
                        maxima(LATE_MAX[1], 1)
                        v_low(3)
                    x2_low(1)
                    x2_low(2)
                    x2_low(3)
                    if nxt:
                        maxima(LATE_MAX[2], 1)
                if setup:
                    dve.wait_ge(c_full, 1)
                    V.tensor_copy(c_sum[:, :], down[:, :]).then_inc(c_ready, 1)

            run(dve, iteration)

        @block.gpsimd
        def _(pool):
            P = nc.gpsimd
            n_const = [0]

            def const(op):
                op.then_inc(consts, 1)
                n_const[0] += 1

            const(P.memset(ident32[:, :], 0.0))
            const(P.memset(mask_rows[:, :], 0.0))
            const(P.memset(m_stage, 0.0))
            const(P.memset(ones16[:, :], 1.0))
            const(P.memset(ones32[:, :], 1.0))
            const(P.memset(lift[:, :], BIAS_UP))
            const(P.memset(mhalf[:, :], -0.5))
            const(P.memset(mx[:, :], 0.0))
            const(P.memset(t16[:, 0, :], ROW_UP))
            const(P.memset(v_sb[:, :, :, HD:HD + 1], 1.0))
            P.memset(temp[:, 7168:8192], 0.0).then_inc(rows_zero, 1)
            pool.wait_ge(consts, 3)
            const(P.affine_select(out=ident32[:, :], in_=ident32[:, :], compare_op=ALU.not_equal, fill=1.0, base=0,
                                  pattern=[[-1, PARTS]], channel_multiplier=1))
            const(P.affine_select(out=mask_rows[:, 3 * PARTS:T], in_=mask_rows[:, 3 * PARTS:T], compare_op=ALU.is_ge,
                                  fill=NEG, base=0, pattern=[[-1, PARTS]], channel_multiplier=1))
            const(P.affine_select(out=m_stage, in_=m_stage, compare_op=ALU.is_ge, fill=NEG, base=0,
                                  pattern=[[1, PARTS]], channel_multiplier=-1))
            assert n_const[0] == CONSTS
            def crossed(out, w, n):
                o2 = out.rearrange("p (a e two) -> p a e two", a=2, two=2)
                w2 = w.rearrange("p (a e two) -> p a e two", a=2, two=2)
                s2 = rope_sb[0:n, E:2 * E].rearrange("p (e two) -> p e two", two=2)
                for k in range(2):
                    sin = s2[:, :, k].unsqueeze(1).to_broadcast([n, 2, E // 2])
                    P.tensor_tensor(o2[:, :, :, k], w2[:, :, :, 1 - k], sin, ALU.mult).then_inc(rot_cross, 1)

            def crossed_weights():
                pool.wait_ge(rope_in, 16)
                for c in range(EC):
                    pool.wait_ge(wqk_in[c], 16)
                    if c >= 2:
                        pool.wait_ge(rot_done, c - 1)
                    crossed(rot2[:, c % 2, :], wa_in[:, c, 0:2 * E], PARTS)
                pool.wait_ge(rows_in, 80)
                crossed(b_r2, b_row, 1)

            def iteration(j, prev, here, nxt, setup):
                G, g0 = general_plan(prev, here, nxt, setup), general_base(j)
                S, s0 = score_plan(here, nxt), score_base(j)

                def power(ln, tbs, terms_n, n):
                    pool.wait_ge(ln_terms[ln], terms_n)
                    width = tbs.stop - tbs.start
                    P.tensor_tensor(rstd[:, ln, tbs], veps[:, ln, tbs], mhalf[:, 0:width], ALU.pow
                                    ).then_inc(ln_pow[ln], 1)
                    pool.wait_ge(ln_pow[ln], n)
                    P.tensor_tensor(shift[:, ln, tbs], negm[:, ln, tbs], rstd[:, ln, tbs], ALU.mult
                                    ).then_inc(ln_ready[ln], 1)

                def power1(ln, b, tb):
                    n = TB * b + tb + 1
                    power(ln, slice(tb, tb + 1), n, n)

                def squares(u):
                    if not here:
                        if u:
                            pool.wait_ge(h_full, FC * (j - 1) + u + 1)
                            if u >= 2:
                                pool.wait_ge(sq_step, SQ_STEPS * (j - 1) + u - 1)
                            P.tensor_tensor(acc[:, :], acc[:, :], xn[:, u % 2, :], ALU.add).then_inc(sq_step, 1)
                        return
                    pool.wait_ge(g_drained, g0 + G["up", u] + 1)
                    n = SQ_STEPS * (j - 1) + 3 * u
                    if u:
                        pool.wait_ge(sq_step, n)
                    whole = acc_add if u else acc
                    P.tensor_tensor(whole[:, :], hT[:, HI, u, :], hT[:, LO, u, :], ALU.add).then_inc(sq_step, 1)
                    pool.wait_ge(sq_step, n + 1)
                    P.tensor_tensor(whole[:, :], whole[:, :], whole[:, :], ALU.mult).then_inc(sq_step, 1 if u else 2)
                    if u:
                        pool.wait_ge(sq_step, n + 2)
                        P.tensor_tensor(acc[:, :], acc[:, :], acc_add[:, :], ALU.add).then_inc(sq_step, 1)

                def under(n):
                    m, u = divmod(n, FC)
                    if u == 0:
                        pool.wait_ge(g_step, 5 * m + 4)
                    if n >= 2:
                        pool.wait_ge(tern_ready, n - 1)
                    P.tensor_scalar(below[:, n % 2, :], stage[:, E * u:E * (u + 1)], theta[:, m, 1:2], None,
                                    ALU.is_lt).then_inc(tern_half, 1)

                def finish(tb):
                    n = TB * (j - 1) + tb
                    pool.wait_ge(fin_ready, n + 1)
                    P.tensor_tensor(xn[:, tb % 2, :], xn[:, tb % 2, :], x1[:, tb, :], ALU.add).then_inc(out_ready, 1)

                for u in range(FC):
                    if prev:
                        squares(u)
                    if setup:
                        under(u)
                    if nxt and u == (5 if setup else 2):
                        power(LX, slice(0, TB), j + 2, j + 2)
                if nxt and not here:
                    crossed_weights()
                if setup:
                    for u in range(FC):
                        under(FC + u)
                if prev:
                    for tb in range(TB):
                        power1(LF, j - 1, tb)
                        finish(tb)
                if here:
                    power1(LP, j, 0)
                    power1(LP, j, 1)
                    power1(L1, j, 0)
                    power1(LP, j, 2)
                    power1(L1, j, 1)
                    power1(LP, j, 3)
                    power1(L1, j, 2)
                    power1(L1, j, 3)

            run(pool, iteration)


def rope_table():
    freqs = (np.float32(THETA) ** (-(np.arange(0, HD, 2, dtype=np.float32) / np.float32(HD)))).astype(np.float32)
    angle = np.outer(np.arange(HEADS, dtype=np.float32), freqs).astype(np.float32)
    cos = np.repeat(np.cos(angle), 2, axis=1).reshape(1, E)
    sin = np.stack([-np.sin(angle), np.sin(angle)], axis=-1).reshape(1, E)
    return np.concatenate([cos, sin], axis=1).astype(np.float32)


def kernel(L0_attn_x, L0_attn_w_attn, L0_attn_b_attn, L0_attn_w_proj, L0_attn_b_proj, L0_ffn_w_fc, L0_ffn_w_proj):
    import concourse.bacc as bacc
    from concourse.bass_utils import run_bass_kernel_spmd

    arrays = {
        "x": np.ascontiguousarray(L0_attn_x).reshape(BATCHES * T, E),
        "w_attn": np.ascontiguousarray(L0_attn_w_attn),
        "b_attn": np.ascontiguousarray(L0_attn_b_attn).reshape(1, 3 * E),
        "w_proj": np.ascontiguousarray(L0_attn_w_proj),
        "b_proj": np.ascontiguousarray(L0_attn_b_proj).reshape(1, E),
        "w_fc": np.ascontiguousarray(L0_ffn_w_fc),
        "w_down": np.ascontiguousarray(L0_ffn_w_proj),
        "rope": rope_table(),
    }
    nc = bacc.Bacc("TRN2", target_bir_lowering=False, num_devices=1)
    args = [nc.dram_tensor(n, a.shape, mybir.dt.float32, kind="ExternalInput").ap() for n, a in arrays.items()]
    out = nc.dram_tensor("out", (BATCHES * T, E), mybir.dt.float32, kind="ExternalOutput").ap()
    build(nc, *args, out)
    result = run_bass_kernel_spmd(nc, [arrays], core_ids=[0])
    return result.results[0]["out"].reshape(BATCHES, T, E)
```

```python
import numpy as np
from contextlib import ExitStack

import concourse.bass as bass
from concourse import mybir

BATCHES, T, E, HEADS = 8, 512, 512, 16
HD = E // HEADS
F = 4 * E
PARTS = 128
TB = T // PARTS
EC = E // PARTS
FC = F // PARTS
VW = 2 * HD + 1
THETA = 10000.0

W_UP = 16.0
S_UP = W_UP * W_UP
ROW_UP = 2.0 ** 15
P_LIFT = 12 * float(np.log(2.0))
BIAS_UP = 16.0
ATTN_SCALE = float(E) ** -0.5
PROJ_K = ATTN_SCALE / S_UP
P_UP = 1.0 / (PROJ_K * BIAS_UP)
EPS_LN, EPS_BIT = 1e-5, 1e-6
NEG = -1.0e30

QK_AT = {1: (0, 0), 2: (0, 1), 3: (1, 0), 4: (1, 1), 7: (2, 0), 8: (2, 1), 11: (3, 0), 12: (3, 1)}
DOWN_AT = {0: [(1, 0)], 5: [(1, 1), (1, 2)], 6: [(1, 3)], 9: [(2, 0), (2, 1)], 10: [(2, 2), (2, 3)],
           13: [(3, 0), (3, 1)], 14: [(3, 2), (3, 3)]}
FINAL_AT = {8: 1, 12: 2}
SQUARES_AT = 6
FINISH_AT = {6: 0, 9: 1, 13: 2}
FIRST_MAX = {8: 0, 11: 1, 12: 2}
PAIRS = FC // 2
PAIRS_BEFORE = PAIRS // 2
MAGNITUDE_AT = {4: 3, 7: 0, 8: 1, 11: 2}
PIECE_ORDER = tuple(MAGNITUDE_AT.values())
PAIR_AT = {0: 4, 2: 5, 5: 6, 7: 7}
PAIR2_AT = {h: PAIRS + h - 4 for h in range(4, 4 + PAIRS)}
STEP_MAX = {8: 0, 9: 1, 10: 2, 11: 3, 12: 4, 13: 5}
LATE_MAX = len(STEP_MAX)
EARLY = LATE_MAX + 1
MAX_AT = {0: 7, 2: 8, 3: 9, 5: 10, 7: 11, 8: 12, 9: 13, 11: 14, 12: 15}
SHIFT_AT = 15
X_AT = {8: 0, 10: 1, 12: 2, 15: 3}
X_NORM_AT = 6
CONSTS = 13


def general_plan(prev, here, nxt, setup):
    uses = []
    for u in range(FC):
        uses += [("shift", 0)] if here and u == SHIFT_AT else []
        uses += [("up", u)] if prev else []
        uses += [("xT", X_AT[u])] if nxt and u in X_AT else []
    if nxt and not here:
        uses += [("v", tb) for tb in range(TB)]
    for h in range(HEADS):
        uses += [("qk", QK_AT[h])] if nxt and h in QK_AT else []
        uses += [("next max", 3 * STEP_MAX[h] + i) for i in range(3)] if here and nxt and h in STEP_MAX else []
    if here:
        for name, n in (("v", 0), ("oT", 0), ("oT", 1), ("proj", 0), ("oT", 2), ("proj", 1), ("oT", 3),
                        ("proj", 2), ("proj", 3), ("v", 1), ("x2T", 0), ("v", 2), ("x2T", 1), ("v", 3),
                        ("x2T", 2), ("x2T", 3)):
            if name != "v" or nxt:
                uses.append((name, n))
    return {name: k for k, name in enumerate(uses)}


N_FIRST = len(general_plan(False, False, True, False))
N_SETUP = len(general_plan(False, True, True, True))
N_USUAL = len(general_plan(True, True, True, False))
N_NO_NEXT = len(general_plan(True, True, False, False))
AFTER_O = N_USUAL - 1 - general_plan(True, True, True, False)["oT", 3]


def score_plan(here, nxt):
    uses = [("max", h) for h in range(EARLY, HEADS)] + [("scores", 0)] if here else []
    for h in range(HEADS):
        if here and h + 1 < HEADS:
            uses.append(("scores", h + 1))
    if nxt:
        uses += [("next max", h) for h in ([LATE_MAX] if here else range(EARLY))]
    return {use: 3 * k for k, use in enumerate(uses)}


def score_base(j):
    return 0 if isinstance(j, int) and j < 0 else 3 * EARLY + 3 * (2 * HEADS - len(STEP_MAX)) * j


def general_base(j):
    if isinstance(j, int) and j <= 0:
        return 0 if j < 0 else N_FIRST
    if isinstance(j, int) and j == BATCHES:
        return N_FIRST + N_SETUP + N_USUAL * (BATCHES - 2) + N_NO_NEXT
    return N_USUAL * j + (N_FIRST + N_SETUP - N_USUAL)


def general_bank(j, k):
    at = general_base(j) if isinstance(j, int) else N_FIRST + N_SETUP
    return (at + k) % 3


assert N_USUAL % 3 == 0 and len(FIRST_MAX) + PAIRS_BEFORE == EARLY


def need(eng, semaphore, count):
    if not isinstance(count, int) or count > 0:
        eng.wait_ge(semaphore, count)


def build(nc, x, w_attn, b_attn, w_proj, b_proj, w_fc, w_down, rope, out):
    f32, f16, bf16 = mybir.dt.float32, mybir.dt.float16, mybir.dt.bfloat16
    ALU = mybir.AluOpType
    ACT = mybir.ActivationFunctionType
    AX = mybir.AxisListType
    HI, LO = 0, 1

    x_v = x.rearrange("(r p) e -> p r e", p=PARTS)
    out_v = out.rearrange("(r p) e -> r p e", p=PARTS)

    with ExitStack() as ctx:
        def sb(name, shape, dt):
            return ctx.enter_context(nc.sbuf_tensor(name, shape, dt))

        def sem(name):
            return ctx.enter_context(nc.semaphore(name))

        wa = sb("wa", [PARTS, 2, EC, 3 * E], f16)
        wp = sb("wp", [PARTS, 2, EC, E], f16)
        t1T = sb("t1T", [PARTS, EC, F], f16)
        t2T = sb("t2T", [PARTS, FC, E], f16)
        c_sum = sb("c_sum", [PARTS, E], f32)
        qk_bias = sb("qk_bias", [PARTS, 2 * EC], f32)
        v_bias = sb("v_bias", [PARTS, E], f16)
        p_bias = sb("p_bias", [PARTS, E], f16)
        lift = sb("lift", [PARTS, PARTS], f16)
        ones16 = sb("ones16", [PARTS, PARTS], f16)
        ones32 = sb("ones32", [PARTS, PARTS], f32)
        ident32 = sb("ident32", [PARTS, PARTS], f32)
        ident16 = sb("ident16", [PARTS, PARTS], f16)
        identb = sb("identb", [PARTS, PARTS], bf16)
        mask_b = sb("mask_b", [PARTS, PARTS], bf16)
        mask_rows = sb("mask_rows", [PARTS, T], f32)
        mhalf = sb("mhalf", [PARTS, TB], f32)
        qk = sb("qk", [PARTS, 2, HEADS, T], f16)
        v_sb = sb("v_sb", [PARTS, TB, HEADS, VW], f16)
        qkn = sb("qkn", [PARTS, 2, 4, T], f16)
        hT = sb("hT", [PARTS, 2, FC, T], f16)
        xT = sb("xT", [PARTS, 2, EC, T], f16)
        x2T = sb("x2T", [PARTS, 2, EC, T], f16)
        xo = sb("xo", [PARTS, TB, E], f32)
        xn = sb("xn", [PARTS, 2, E], f32)
        x1 = sb("x1", [PARTS, TB, E], f32)
        probs = sb("probs", [PARTS, 2, 2, 1280], f16)
        acc = sb("acc", [PARTS, T], f32)
        acc_add = sb("acc_add", [PARTS, T], f32)
        oA = sb("oA", [PARTS, TB, HD], f32)
        r_sum = sb("r_sum", [PARTS, TB], f32)
        mx = sb("mx", [PARTS, PARTS], f32)
        m_f = sb("m_f", [HEADS * TB, PARTS], f32)
        m_half = sb("m_half", [HEADS * TB, 2, PARTS], f16)
        bn = sb("bn", [PARTS, 4, TB, 6], f32)
        mv = sb("mv", [PARTS, 4, TB, 2], f32)
        veps = sb("veps", [PARTS, 4, TB], f32)
        negm = sb("negm", [PARTS, 4, TB], f32)
        rstd = sb("rstd", [PARTS, 4, TB], f32)
        shift = sb("shift", [PARTS, 4, TB], f32)
        h_negm = sb("h_negm", [PARTS, TB], f32)
        h_msq = sb("h_msq", [PARTS, TB], f32)
        h_var = sb("h_var", [PARTS, TB], f32)
        e_fin = sb("e_fin", [PARTS, TB], f32)
        wait_copy = sb("wait_copy", [PARTS, 1], f32)
        gs = sb("gs", [PARTS, 2 * EC], f32)
        gt = sb("gt", [PARTS, 2], f32)
        gam = sb("gam", [PARTS, 2], f32)
        theta = sb("theta", [PARTS, 2, 2], f32)
        g_sq = sb("g_sq", [PARTS, 2], f32)
        c_fin = sb("c_fin", [PARTS, 1], f32)
        LX, LP, L1, LF = range(4)
        PIECES = EC
        len_piece = FC * E // PIECES
        stage = hT[:, :, :, :].rearrange("p a c t -> p (a c t)").bitcast(f32)
        wa_in = stage[:, 0:EC * 3 * E].rearrange("p (c n) -> p c n", c=EC)
        y_sb = stage[:, 0:2 * E].rearrange("p (r e) -> p r e", r=2)
        xres = stage[:, 2 * E:6 * E].rearrange("p (b e) -> p b e", b=TB)
        oT = hT[:, 1, 8:12, :].rearrange("p c t -> p (c t)").rearrange(
            "p (r a c t) -> p r a c t", r=2, a=2, c=EC)
        temp = qk[:, :, :, :].rearrange("p a h t -> p (a h t)").bitcast(f32)
        rot1 = temp[:, 0:2048].rearrange("p (r n) -> p r n", r=2)
        rot2 = temp[:, 2048:4096].rearrange("p (r n) -> p r n", r=2)
        b_row, b_r1, b_r2 = (temp[0:1, 4096 + 1024 * i:5120 + 1024 * i] for i in range(3))
        vb_in, pb_in = temp[:, 7168:7680], temp[:, 7680:8192]
        rope_sb = probs[:, 0, :, :].rearrange("p a n -> p (a n)").bitcast(f32)[:, 0:2 * E]
        m_stage = acc[:, 0:PARTS]
        t16 = acc_add[:, :].bitcast(f16).rearrange("p (r e) -> p r e", r=2)
        below = acc[:, :].bitcast(f16).rearrange("p (r e) -> p r e", r=2)
        unused_out = x2T[:, 0, :, :].rearrange("p c t -> p (c t)")
        score = [ctx.enter_context(nc.psum_tensor(f"score{i}", [PARTS, 512], f32)) for i in range(3)]
        gen = [ctx.enter_context(nc.psum_tensor(f"gen{i}", [PARTS, 512], f32)) for i in range(3)]
        pv = ctx.enter_context(nc.psum_tensor("pv", [PARTS, 512], f32))
        down = ctx.enter_context(nc.psum_tensor("down", [PARTS, 512], f32))
        SQ_STEPS = 3 * FC
        H_SUM, H_SQ = 264, 268

        x_in, xres_in = sem("x_in"), sem("xres_in")
        wv_in, wp_in, rope_in, rows_in = sem("wv_in"), sem("wp_in"), sem("rope_in"), sem("rows_in")
        wqk_in = [sem(f"wqk_in{c}") for c in range(EC)]
        wfc_in, wdown_in = ([sem(f"{n}{i}") for i in range(PIECES)] for n in ("wfc_in", "wdown_in"))
        stacked = [sem(f"stacked{g}") for g in range(4)]
        shift_rows = sem("shift_rows")
        stored = [sem(f"stored{i}") for i in range(2)]
        consts, rows_zero, ident_copy, k_rows = (
            sem(n) for n in ("consts", "rows_zero", "ident_copy", "k_rows"))
        wv_hi, wp_hi, rot_cross, rot_step, rot_done, wqk_hi = (
            sem(n) for n in ("wv_hi", "wp_hi", "rot_cross", "rot_step", "rot_done", "wqk_hi"))
        w_low, w_ready, bias_step, bias_cols = (sem(n) for n in ("w_low", "w_ready", "bias_step", "bias_cols"))
        dve_half = sem("dve_half")
        g_sums, g_step, g_total, tern_half, tern_ready, sign_full, sign_drained = (
            sem(n) for n in ("g_sums", "g_step", "g_total", "tern_half", "tern_ready", "sign_full", "sign_drained"))
        c_full, c_ready = sem("c_full"), sem("c_ready")
        g_full, g_drained = sem("g_full"), sem("g_drained")
        s_full, s_drained = sem("s_full"), sem("s_drained")
        pv_full, pv_drained = sem("pv_full"), sem("pv_drained")
        down_full, down_drained = sem("down_full"), sem("down_drained")
        hsum_full, hsq_full = sem("hsum_full"), sem("hsq_full")
        xn_ready, xT_hi, v_hi, qk_hi, h_full, exp_full = (
            sem(n) for n in ("xn_ready", "xT_hi", "v_hi", "qk_hi", "h_full", "exp_full"))
        gelu_done = sem("gelu_done")
        oT_hi, y_copied, xb_ready, xn2_ready, x2T_hi, fin_ready = (
            sem(n) for n in ("oT_hi", "y_copied", "xb_ready", "xn2_ready", "x2T_hi", "fin_ready"))
        m_neg, m_hi, o_sums, o_recip, o_ready, x1_ready = (
            sem(n) for n in ("m_neg", "m_hi", "o_sums", "o_recip", "o_ready", "x1_ready"))
        bn_done = [sem(f"bn_done{i}") for i in range(4)]
        mv_done = [sem(f"mv_done{i}") for i in range(4)]
        ln_terms = [sem(f"ln_terms{i}") for i in range(4)]
        h_step, h_terms = sem("h_step"), sem("h_terms")
        ln_pow = [sem(f"ln_pow{i}") for i in range(4)]
        ln_ready = [sem(f"ln_ready{i}") for i in range(4)]
        sq_step, out_ready = sem("sq_step"), sem("out_ready")

        signs = down[:, :].bitcast(f16)

        def block_at(s, tb):
            if s == tb:
                return PARTS * s
            return 512 + (PARTS * (tb - 1) if s == 0 else 384 if s == 2 else 512 + PARTS * (tb - 2))

        SCORE_W = (512, 512, 256)
        usual = (True, True, True, False)
        first = [(-1, False, False, True, False), (0, False, True, True, True), (1, *usual)]
        last = [(BATCHES - 1, True, True, False, False), (BATCHES, True, False, False, False)]

        def run(eng, iteration):
            for j, *what in first:
                iteration(j, *what)
            with eng.Fori(2, BATCHES - 1) as j:
                iteration(j, *usual)
            for j, *what in last:
                iteration(j, *what)

        block = ctx.enter_context(nc.Block())

        @block.sync
        def _(sp):
            sp.dma_start(xo[:, :, :], x_v[:, 0:TB, :]).then_inc(x_in, 16)
            wa_v = w_attn.rearrange("(c p) n -> p c n", p=PARTS)
            sp.dma_start(rope_sb.unsqueeze(1), rope.partition_broadcast(PARTS)).then_inc(rope_in, 16)
            sp.dma_start(wa_in[:, :, 2 * E:3 * E], wa_v[:, :, 2 * E:3 * E]).then_inc(wv_in, 16)
            for c in range(EC):
                sp.dma_start(wa_in[:, c, 0:2 * E], wa_v[:, c, 0:2 * E]).then_inc(wqk_in[c], 16)
            sp.wait_ge(rows_zero, 1)
            for p in (0, 32):
                sp.dma_start(vb_in[p:p + 1, :], b_attn[:, 2 * E:3 * E]).then_inc(rows_in, 16)
                sp.dma_start(pb_in[p:p + 1, :], b_proj[:, :]).then_inc(rows_in, 16)
            sp.dma_start(b_row, b_attn[:, 0:2 * E]).then_inc(rows_in, 16)
            sp.dma_start(x1[:, :, :], w_proj.rearrange("(c p) n -> p c n", p=PARTS)).then_inc(wp_in, 16)
            for i in PIECE_ORDER:
                if i < PIECES - 1:
                    sp.wait_ge(w_low, 2 + i + 2)
                per = FC // PIECES
                sp.dma_start(stage[:, len_piece * i:len_piece * (i + 1)].rearrange("p (u d) -> p u d", u=per),
                             w_fc.rearrange("(u p) d -> p u d", p=PARTS)[:, per * i:per * (i + 1), :]
                             ).then_inc(wfc_in[i], 16)
            sp.wait_ge(w_ready, 2)
            sp.dma_start(qk[96:98, 1, :, :], t16[96:98, 0, :].unsqueeze(1).to_broadcast([2, HEADS, T])
                         ).then_inc(k_rows, 16)

            def iteration(j, prev, here, nxt, setup):
                G, g0 = general_plan(prev, here, nxt, setup), general_base(j)
                S, s0 = score_plan(here, nxt), score_base(j)
                if nxt and here:
                    row = TB * (j + 1) if isinstance(j, int) else sp.snap(TB * (j + 1))
                    need(sp, xn_ready, TB * (j + 1))
                    if not setup:
                        sp.wait_ge(g_full, g0 - AFTER_O)
                    sp.dma_start(xo[:, :, :], x_v[:, bass.ds(row, TB), :]).then_inc(x_in, 16)

                def load_down(i):
                    sp.wait_ge(tern_ready, FC // PIECES * (i + 1))
                    sp.dma_start(stage[:, len_piece * i:len_piece * (i + 1)], w_down[PARTS * i:PARTS * (i + 1), :]
                                 ).then_inc(wdown_in[i], 16)

                if setup:
                    for i in range(PIECES - 1):
                        load_down(i)
                if here:
                    sp.wait_ge(g_drained, g0 + G["shift", 0] + 1)
                    for half in (HI, LO):
                        sp.dma_start(qk[96 + half:97 + half, 0, :, :].rearrange("o h (b t) -> o (h b) t", b=TB),
                                     m_half[:, half, :]).then_inc(shift_rows, 16)
                if setup:
                    load_down(PIECES - 1)

                def store(tb):
                    row = TB * (j - 1) + tb if isinstance(j, int) else sp.snap(TB * (j - 1) + tb)
                    sp.wait_ge(out_ready, TB * (j - 1) + tb + 1)
                    sp.dma_start(out_v[bass.ds(row, 1), :, :].rearrange("r p e -> p (r e)"), xn[:, tb % 2, :]
                                 ).then_inc(stored[tb % 2], 16)

                def stack(g):
                    if here:
                        n = max(4 * g + 3, max(h for h, what in QK_AT.items() if what[0] == g) + 2)
                        sp.wait_ge(s_full, s0 + S["scores", n] + 3)
                    else:
                        sp.wait_ge(g_drained, g0 + G["qk", (g, 1)] + 1)
                    for i in range(4):
                        src = qkn[HD * i:HD * (i + 1), g % 2, :, :]
                        head = qk[:, :, 4 * g + i, :]
                        sp.dma_start(head[0:32, :, :], src[:, 1:3, :]).then_inc(stacked[g], 16)
                        sp.dma_start(head[32:64, :, :], src[:, 0:3:2, :]).then_inc(stacked[g], 16)
                        sp.dma_start(head[64:96, :, :], src[:, 1:4:2, :]).then_inc(stacked[g], 16)

                for g in range(4):
                    if g == 3 and here:
                        if prev:
                            sp.wait_ge(down_full, TB * j)
                        if setup:
                            sp.wait_ge(tern_ready, 2 * FC)
                        row = TB * j if isinstance(j, int) else sp.snap(TB * j)
                        sp.dma_start(xres, x_v[:, bass.ds(row, TB), :]).then_inc(xres_in, 16)
                    if nxt:
                        stack(g)
                    if prev:
                        for tb in ((), (0, 1), (2,), (3,))[g]:
                            store(tb)

            run(sp, iteration)
            for half in stored:
                sp.wait_ge(half, 16 * 2 * BATCHES)

        @block.tensor
        def _(pe):
            pe.wait_ge(consts, CONSTS)
            pe.wait_ge(ident_copy, 3)

            def bias_columns():
                pe.wait_ge(bias_step, 4)
                for i in range(2 * EC):
                    mm = nc.tensor.matmul(down[:, i:i + 1], b_r1[:, PARTS * i:PARTS * (i + 1)], ones32[0:1, 0:1],
                                          start=True, stop=True)
                mm.then_inc(bias_cols, 1)

            def gamma_total(m):
                pe.wait_ge(g_step, 5 * m + 1)
                if m:
                    pe.wait_ge(sign_drained, PAIRS)
                nc.tensor.matmul(down[:, m:m + 1], ones32[:, :], gt[:, m:m + 1], start=True, stop=True
                                 ).then_inc(g_total, 1)

            def sign_turn(pair):
                if pair:
                    pe.wait_ge(sign_drained, pair)
                pe.wait_ge(tern_ready, 2 * pair + 2)
                for k in range(2):
                    for c in range(EC):
                        at = E * k + PARTS * c
                        mm = nc.tensor.transpose(signs[:, at:at + PARTS], t16[:, k, PARTS * c:PARTS * (c + 1)],
                                                 ident16[:, :])
                mm.then_inc(sign_full, 1)

            def iteration(j, prev, here, nxt, setup):
                G, g0 = general_plan(prev, here, nxt, setup), general_base(j)
                S, s0 = score_plan(here, nxt), score_base(j)

                def claim(name, n):
                    k = G[name, n]
                    need(pe, g_drained, g0 + k - 2)
                    return gen[general_bank(j, k)]

                def drained(name, n):
                    pe.wait_ge(g_drained, g0 + G[name, n] + 1)

                def claim_score(use, i):
                    need(pe, s_drained, s0 + S[use] + i - 2)
                    return score[i]

                def turn(bank, block):
                    for c in range(EC):
                        mm = nc.tensor.transpose(bank[:, PARTS * c:PARTS * (c + 1)], block(c), ident32[:, :])
                    return mm

                def products(bank, pairs, start=True, stop=True):
                    for n, (a, b) in enumerate(pairs):
                        mm = nc.tensor.matmul(bank[:, :], a, b, start=(start and n == 0),
                                              stop=(stop and n == len(pairs) - 1))
                    return mm

                def up(u):
                    bank = claim("up", u)
                    cols = slice(PARTS * u, PARTS * (u + 1))
                    products(bank, [(t1T[:, c, cols], x2T[:, HI, c, :]) for c in range(EC)], stop=False)
                    if u == 0:
                        pe.wait_ge(g_drained, g0)
                    products(bank, [(t1T[:, c, cols], x2T[:, LO, c, :]) for c in range(EC)], start=False
                             ).then_inc(g_full, 1)

                def hidden_sums(u):
                    drained("up", u)
                    for half in (HI, LO):
                        for tb in range(TB):
                            first, final = u == 0 and half == HI, u == FC - 1 and half == LO
                            mm = nc.tensor.matmul(pv[:, H_SUM + tb:H_SUM + tb + 1],
                                                  hT[:, half, u, PARTS * tb:PARTS * (tb + 1)], ones16[:, 0:1],
                                                  start=first and tb == 0, stop=final, skip_group_check=True)
                    if u == FC - 1:
                        mm.then_inc(hsum_full, 1)

                def square_sums():
                    pe.wait_ge(sq_step, SQ_STEPS * j if here else SQ_STEPS * (j - 1) + FC - 1)
                    for tb in range(TB):
                        mm = nc.tensor.matmul(pv[:, H_SQ + tb:H_SQ + tb + 1], acc[:, PARTS * tb:PARTS * (tb + 1)],
                                              ones32[:, 0:1], start=True, stop=True)
                    mm.then_inc(hsq_full, 1)

                def ffn_down(tb, part):
                    if isinstance(j, int) and j == 1 and (tb, part) == (0, 0):
                        pe.wait_ge(c_ready, 1)
                    if part == 0:
                        need(pe, down_drained, TB * (j - 1) + tb)
                    for u in range(4 * part, 4 * part + 4):
                        for half in (HI, LO):
                            mm = nc.tensor.matmul(down[:, :], hT[:, half, u, PARTS * tb:PARTS * (tb + 1)], t2T[:, u, :],
                                                  start=(u == 0 and half == HI), stop=(u == FC - 1 and half == LO))
                    if part == 3:
                        mm.then_inc(down_full, 1)

                def max_pass(u, ahead=0, in_general=False):
                    if u % 4 == 0:
                        pe.wait_ge(stacked[u // 4], 192 * (j + ahead + 1))
                    for i, tbs in enumerate(((3,), (0, 2), (1,))):
                        if in_general:
                            bank = claim("next max", 3 * u + i)
                        else:
                            bank = claim_score(("next max" if ahead else "max", u), i)
                        at = 0
                        for tb in tbs:
                            n = PARTS * (tb + 1)
                            mm = nc.tensor.matmul(bank[:, at:at + n], qk[0:96, 0, u, PARTS * tb:PARTS * (tb + 1)],
                                                  qk[0:96, 1, u, 0:n], start=(at == 0), stop=True,
                                                  skip_group_check=True)
                            at += n
                        mm.then_inc(g_full if in_general else s_full, 1)

                def scores(h):
                    def part(bank, at, s, t0, t1, start):
                        return nc.tensor.matmul(bank[:, at:at + t1 - t0], qk[0:98, 1, h, PARTS * s:PARTS * (s + 1)],
                                                qk[0:98, 0, h, t0:t1], start=start, stop=True, skip_group_check=True)
                    if h == 0:
                        pe.wait_ge(k_rows, 16)
                        pe.wait_ge(shift_rows, 32 * (j + 1))
                    bank = claim_score(("scores", h), 0)
                    nc.tensor.matmul(bank[:, :].rearrange("p (b t) -> p b t", b=TB), identb[:, :],
                                     mask_b[:, :].unsqueeze(1).to_broadcast([PARTS, TB, PARTS]),
                                     start=True, stop=False, skip_group_check=True)
                    for s in range(TB):
                        mm = part(bank, PARTS * s, s, PARTS * s, PARTS * (s + 1), False)
                    mm.then_inc(s_full, 1)
                    bank = claim_score(("scores", h), 1)
                    part(bank, 0, 0, PARTS, T, True)
                    part(bank, 384, 2, 3 * PARTS, T, False).then_inc(s_full, 1)
                    bank = claim_score(("scores", h), 2)
                    part(bank, 0, 1, 2 * PARTS, T, True).then_inc(s_full, 1)

                def weigh(h):
                    pe.wait_ge(s_drained, s0 + S["scores", h] + 3)
                    need(pe, pv_drained, HEADS * j + h)
                    if prev and here and h == SQUARES_AT:
                        square_sums()
                    for tb in range(TB):
                        for s in range(tb + 1):
                            for half in (HI, LO):
                                at = block_at(s, tb)
                                mm = nc.tensor.matmul(pv[:, VW * tb:VW * (tb + 1)],
                                                      probs[:, h % 2, half, at:at + PARTS], v_sb[:, s, h, :],
                                                      start=(s == 0 and half == HI), stop=(s == tb and half == LO))
                    mm.then_inc(pv_full, 1)

                def x_turn(tb):
                    pe.wait_ge(xn_ready, TB * (j + 1) + tb + 1)
                    bank = claim("xT", tb)
                    turn(bank, lambda c: xn[:, tb % 2, PARTS * c:PARTS * (c + 1)]).then_inc(g_full, 1)

                def values(tb):
                    if not here and tb == 0:
                        drained("xT", 3)
                    bank = claim("v", tb)
                    rows = slice(PARTS * tb, PARTS * (tb + 1))
                    cols = slice(2 * E, 3 * E)
                    products(bank, [(xT[:, a, c, rows], wa[:, b, c, cols]) for c in range(EC)
                                    for a, b in ((HI, HI), (HI, LO), (LO, HI))] + [(lift[:, :], v_bias[:, :])]
                             ).then_inc(g_full, 1)

                def queries_keys(g, which):
                    if (g, which) == (0, 0) and here:
                        drained("xT", 3)
                    bank = claim("qk", (g, which))
                    cols = slice(E * which + PARTS * g, E * which + PARTS * (g + 1))
                    products(bank, [(wa[:, a, c, cols], xT[:, b, c, :]) for c in range(EC)
                                    for a, b in ((HI, HI), (HI, LO), (LO, HI))]).then_inc(g_full, 1)

                def o_turn(tb):
                    if tb == 0:
                        pe.wait_ge(o_ready, HEADS * (j + 1))
                    bank = claim("oT", tb)
                    turn(bank, lambda c: xo[:, tb, PARTS * c:PARTS * (c + 1)]).then_inc(g_full, 1)

                def project(tb):
                    if setup and tb == 0:
                        pe.wait_ge(w_ready, 3)
                    pe.wait_ge(oT_hi, TB * j + tb + 1)
                    bank = claim("proj", tb)
                    products(bank, [(lift[:, :], p_bias[:, :])] + [(oT[:, tb % 2, HI, c, :], wp[:, b, c, :])
                                                                  for c in range(EC) for b in (HI, LO)], stop=False)
                    drained("oT", tb)
                    products(bank, [(oT[:, tb % 2, LO, c, :], wp[:, HI, c, :]) for c in range(EC)], start=False
                             ).then_inc(g_full, 1)

                def x2_turn(tb):
                    pe.wait_ge(xn2_ready, TB * j + tb + 1)
                    bank = claim("x2T", tb)
                    turn(bank, lambda c: xn[:, tb % 2, PARTS * c:PARTS * (c + 1)]).then_inc(g_full, 1)

                for u in range(FC):
                    if here and u == SHIFT_AT:
                        pe.wait_ge(s_drained, s0 + S["max", HEADS - 1] + 3)
                        bank = claim("shift", 0)
                        nc.tensor.transpose(bank[:, 0:PARTS], mx[:, :], ident32[:, :]).then_inc(g_full, 1)
                    if here and u == 0:
                        max_pass(MAX_AT[0])
                    if prev:
                        if u == 0:
                            pe.wait_ge(x2T_hi, TB * j)
                        up(u)
                        if u >= 2:
                            hidden_sums(u - 2)
                    if here and u and u in MAX_AT:
                        max_pass(MAX_AT[u])
                    if setup and u in PAIR_AT:
                        sign_turn(PAIR_AT[u])
                    if nxt and u in X_AT:
                        x_turn(X_AT[u])
                if prev:
                    ffn_down(0, 0)
                    ffn_down(0, 1)
                    hidden_sums(FC - 2)
                    hidden_sums(FC - 1)
                if here:
                    scores(0)
                if prev:
                    ffn_down(0, 2)
                    ffn_down(0, 3)
                    if not here:
                        square_sums()
                if nxt and not here:
                    pe.wait_ge(w_low, 2)
                    for tb in range(TB):
                        values(tb)
                    pe.wait_ge(w_low, 2 + EC)
                for h in range(HEADS):
                    if nxt and h in QK_AT:
                        queries_keys(*QK_AT[h])
                        if not here and QK_AT[h] == (0, 0):
                            bias_columns()
                        if not here and h in FIRST_MAX:
                            max_pass(FIRST_MAX[h], 1)
                        if not here and QK_AT[h] == (3, 1):
                            gamma_total(0)
                    pieces = DOWN_AT.get(h, ()) if prev else ()
                    if h:
                        for tb, part in pieces:
                            ffn_down(tb, part)
                    if here:
                        if h + 1 < HEADS:
                            scores(h + 1)
                        elif nxt:
                            values(0)
                        if setup and h == 2:
                            gamma_total(1)
                        if nxt and h in STEP_MAX:
                            max_pass(STEP_MAX[h], 1, in_general=True)
                        weigh(h)
                        if setup and h in PAIR2_AT:
                            sign_turn(PAIR2_AT[h])
                    if h == 0 and pieces:
                        ffn_down(*pieces[0])
                if nxt and not here:
                    for pair in range(PAIRS_BEFORE):
                        max_pass(len(FIRST_MAX) + pair, 1)
                        sign_turn(pair)
                if here:
                    if nxt:
                        max_pass(LATE_MAX, 1)
                    o_turn(0)
                    o_turn(1)
                    project(0)
                    o_turn(2)
                    project(1)
                    o_turn(3)
                    project(2)
                    project(3)
                    if setup:
                        pe.wait_ge(sign_drained, 2 * PAIRS)
                        for u in range(FC):
                            mm = nc.tensor.matmul(down[:, :], ones16[:, :], t2T[:, u, :], start=(u == 0),
                                                  stop=(u == FC - 1))
                        mm.then_inc(c_full, 1)
                    if nxt:
                        values(1)
                    x2_turn(0)
                    if nxt:
                        values(2)
                    x2_turn(1)
                    if nxt:
                        values(3)
                    x2_turn(2)
                    x2_turn(3)

            run(pe, iteration)

        @block.scalar
        def _(act):
            def high(out, in_, bias=None, scale=1.0):
                if bias is None:
                    return nc.scalar.activation(out, in_, ACT.Copy, scale=scale)
                return nc.scalar.activation(out, in_, ACT.Identity, bias=bias, scale=scale)

            def iteration(j, prev, here, nxt, setup):
                G, g0 = general_plan(prev, here, nxt, setup), general_base(j)
                S, s0 = score_plan(here, nxt), score_base(j)

                def filled(name, n):
                    k = G[name, n]
                    act.wait_ge(g_full, g0 + k + 1)
                    return gen[general_bank(j, k)]

                def blocks(bank, n=PARTS):
                    return bank[:, :].rearrange("p (c t) -> p c t", t=n)

                def hidden(u):
                    bank = filled("up", u)
                    nc.scalar.activation(hT[:, HI, u, :], bank[:, :], ACT.Gelu, scale=gam[:, 0:1])
                    whole = nc.scalar.activation(bank[:, :], bank[:, :], ACT.Gelu, scale=gam[:, 0:1])
                    if not here:
                        whole.then_inc(gelu_done, 1)
                        if u >= 3:
                            act.wait_ge(sq_step, SQ_STEPS * (j - 1) + u - 2)
                        act.wait_ge(gelu_done, u + 1)
                        whole = nc.scalar.activation(xn[:, u % 2, :] if u else acc[:, :], bank[:, :], ACT.Square)
                    whole.then_inc(h_full, 1)

                def normalise(tb):
                    nc.scalar.activation(xn[:, tb % 2, :], xo[:, tb, :], ACT.Identity, bias=shift[:, LX, tb:tb + 1],
                                         scale=rstd[:, LX, tb:tb + 1]).then_inc(xn_ready, 1)

                def x_turned(tb):
                    high(xT[:, HI, :, PARTS * tb:PARTS * (tb + 1)], blocks(filled("xT", tb))).then_inc(xT_hi, 1)

                def values(tb):
                    bank = filled("v", tb)
                    if here and tb == 0:
                        act.wait_ge(pv_full, HEADS * (j + 1))
                    high(v_sb[:, tb, :, 0:HD], blocks(bank, HD)).then_inc(v_hi, 1)

                def queries_keys(g, which):
                    bank = filled("qk", (g, which))
                    if not here and (g, which) == (0, 0):
                        act.wait_ge(w_ready, 2)
                    if which == 0:
                        need(act, stacked[(g - 2) % 4], 192 * (j + 1 + (1 if g >= 2 else 0)))
                    high(qkn[:, g % 2, 1 + which, :], bank[:, :], bias=qk_bias[:, EC * which + g:EC * which + g + 1]
                         ).then_inc(qk_hi, 1)

                def exponents(h):
                    for i, n in enumerate(SCORE_W):
                        act.wait_ge(s_full, s0 + S["scores", h] + i + 1)
                        nc.scalar.activation(probs[:, h % 2, HI, 512 * i:512 * i + n], score[i][:, 0:n], ACT.Exp,
                                             scale=1.0 / S_UP)
                        nc.scalar.activation(score[i][:, 0:n], score[i][:, 0:n], ACT.Exp, scale=1.0 / S_UP
                                             ).then_inc(exp_full, 1)

                def final(tb):
                    act.wait_ge(ln_ready[LF], TB * (j - 1) + tb + 1)
                    nc.scalar.activation(xn[:, tb % 2, :], xn[:, tb % 2, :], ACT.Identity, bias=shift[:, LF, tb:tb + 1],
                                         scale=rstd[:, LF, tb:tb + 1]).then_inc(fin_ready, 1)

                def o_turned(tb):
                    high(oT[:, tb % 2, HI, :, :], blocks(filled("oT", tb))).then_inc(oT_hi, 1)

                def copy_y(tb):
                    bank = filled("proj", tb)
                    need(act, x1_ready, TB * j + tb - 1)
                    nc.scalar.activation(y_sb[:, tb % 2, :], bank[:, :], ACT.Copy).then_inc(y_copied, 1)

                def residual(tb):
                    if tb == 0:
                        act.wait_ge(xres_in, 16 * (j + 1))
                    act.wait_ge(ln_ready[LP], TB * j + tb + 1)
                    nc.scalar.activation(xres[:, tb, :], xres[:, tb, :], ACT.Identity, bias=shift[:, LP, tb:tb + 1]
                                         ).then_inc(xb_ready, 1)

                def normalise2(tb):
                    if tb < 2 and prev:
                        act.wait_ge(stored[tb], 16 * 2 * j)
                    act.wait_ge(ln_ready[L1], TB * j + tb + 1)
                    nc.scalar.activation(xn[:, tb % 2, :], x1[:, tb, :], ACT.Identity, bias=shift[:, L1, tb:tb + 1],
                                         scale=rstd[:, L1, tb:tb + 1]).then_inc(xn2_ready, 1)

                def x2_turned(tb):
                    high(x2T[:, HI, :, PARTS * tb:PARTS * (tb + 1)], blocks(filled("x2T", tb))).then_inc(x2T_hi, 1)

                def magnitudes(m, loaded, i):
                    act.wait_ge(loaded[i], 16)
                    done = PIECES + i if m else PIECE_ORDER.index(i)
                    n = PIECES * m + i
                    if done:
                        act.wait_ge(g_sums, done)
                    nc.scalar.activation(unused_out, stage[:, len_piece * i:len_piece * (i + 1)], ACT.Abs,
                                         accum_out=gs[:, n:n + 1]).then_inc(g_sums, 1)

                def sign_turned(pair):
                    act.wait_ge(sign_full, pair + 1)
                    if pair < PAIRS:
                        at = 2 * PARTS * pair
                        dst = t1T[:, :, at:at + 2 * PARTS].rearrange("p c (k t) -> p k c t", k=2)
                        src = signs.rearrange("p (k c t) -> p k c t", k=2, c=EC)
                    else:
                        c, half = divmod(pair - PAIRS, 2)
                        dst = t2T[:, 8 * half:8 * half + 8, PARTS * c:PARTS * (c + 1)]
                        src = signs.rearrange("p (c t) -> p c t", t=PARTS)
                    nc.scalar.activation(dst, src, ACT.Copy).then_inc(sign_drained, 1)

                if prev:
                    act.wait_ge(g_step, 12)
                for u in range(FC):
                    if prev:
                        hidden(u)
                    if setup and u in PAIR_AT:
                        sign_turned(PAIR_AT[u])
                    if setup and u >= FC - PIECES + 1:
                        magnitudes(1, wdown_in, u - (FC - PIECES + 1))
                    if nxt and u == X_NORM_AT:
                        act.wait_ge(ln_ready[LX], j + 2)
                        normalise(0)
                        normalise(1)
                    if nxt and u in X_AT:
                        if X_AT[u] == 0:
                            if not here:
                                act.wait_ge(wv_in, 16)
                                high(wa[:, HI, :, 2 * E:3 * E], wa_in[:, :, 2 * E:3 * E], scale=W_UP
                                     ).then_inc(wv_hi, 1)
                        x_turned(X_AT[u])
                        if X_AT[u] + 2 < TB:
                            normalise(X_AT[u] + 2)
                if here:
                    exponents(0)
                if nxt and not here:
                    for c in range(EC):
                        act.wait_ge(rot_done, c + 1)
                        high(wa[:, HI, c, 0:2 * E], rot1[:, c % 2, :], scale=W_UP).then_inc(wqk_hi, 1)
                        values(c)
                for h in range(HEADS):
                    if nxt and h in QK_AT:
                        queries_keys(*QK_AT[h])
                    if nxt and not here:
                        if h == 3:
                            act.wait_ge(wp_in, 16)
                            high(wp[:, HI, :, :], x1[:, :, :], scale=W_UP).then_inc(wp_hi, 1)
                        if h in MAGNITUDE_AT:
                            magnitudes(0, wfc_in, MAGNITUDE_AT[h])
                    if here and h + 1 < HEADS:
                        exponents(h + 1)
                    if setup and h == 0:
                        magnitudes(1, wdown_in, PIECES - 1)
                    if setup and h in PAIR2_AT:
                        sign_turned(PAIR2_AT[h])
                    if prev and h in FINISH_AT:
                        final(FINISH_AT[h])
                if nxt and not here:
                    for pair in range(PAIRS_BEFORE):
                        sign_turned(pair)
                if prev and not here:
                    final(3)
                if here:
                    if nxt:
                        values(0)
                    o_turned(0)
                    o_turned(1)
                    copy_y(0)
                    o_turned(2)
                    if prev:
                        final(3)
                    copy_y(1)
                    residual(0)
                    o_turned(3)
                    copy_y(2)
                    residual(1)
                    copy_y(3)
                    residual(2)
                    normalise2(0)
                    if nxt:
                        values(1)
                    residual(3)
                    normalise2(1)
                    x2_turned(0)
                    if nxt:
                        values(2)
                    normalise2(2)
                    x2_turned(1)
                    normalise2(3)
                    if nxt:
                        values(3)
                    x2_turned(2)
                    x2_turned(3)

            run(act, iteration)

        @block.vector
        def _(dve):
            V = nc.vector

            def low(out, whole, hi):
                return V.tensor_tensor(out, whole, hi, ALU.subtract)

            dve.wait_ge(consts, CONSTS)
            V.tensor_copy(ident16[:, :], ident32[:, :]).then_inc(ident_copy, 1)
            V.tensor_copy(identb[:, :], ident32[:, :]).then_inc(ident_copy, 1)
            V.tensor_copy(mask_b[:, :], m_stage).then_inc(ident_copy, 1)

            def rotation(c):
                cos2 = rope_sb[:, 0:E].unsqueeze(1).to_broadcast([PARTS, 2, E])
                dve.wait_ge(wqk_in[c], 16)
                if c >= 2:
                    dve.wait_ge(w_low, 2 + c - 1)
                V.tensor_tensor(rot1[:, c % 2, :].rearrange("p (a e) -> p a e", a=2),
                                wa_in[:, c, 0:2 * E].rearrange("p (a e) -> p a e", a=2), cos2, ALU.mult
                                ).then_inc(rot_step, 1)

            def rotated_low(c):
                dve.wait_ge(wqk_hi, c + 1)
                V.scalar_tensor_tensor(out=wa[:, LO, c, 0:2 * E], in0=rot1[:, c % 2, :], scalar=W_UP,
                                       in1=wa[:, HI, c, 0:2 * E], op0=ALU.mult, op1=ALU.subtract).then_inc(w_low, 1)

            def value_weights():
                dve.wait_ge(wv_hi, 1)
                for c in range(EC):
                    last_op = V.scalar_tensor_tensor(out=wa[:, LO, c, 2 * E:3 * E], in0=wa_in[:, c, 2 * E:3 * E],
                                                     scalar=W_UP, in1=wa[:, HI, c, 2 * E:3 * E],
                                                     op0=ALU.mult, op1=ALU.subtract)
                last_op.then_inc(w_low, 1)
                dve.wait_ge(rows_in, 80)
                V.tensor_copy(v_bias[:, :], vb_in).then_inc(bias_step, 1)
                V.tensor_scalar(p_bias[:, :], pb_in, P_UP, None, ALU.mult).then_inc(bias_step, 1)
                dve.wait_ge(bias_step, 2)
                low(v_bias[32:33, :], vb_in[32:33, :], v_bias[32:33, :]).then_inc(w_low, 1)
                c_row = rope_sb[0:1, 0:E].unsqueeze(1).to_broadcast([1, 2, E])
                V.tensor_tensor(b_r1.rearrange("p (a e) -> p a e", a=2), b_row.rearrange("p (a e) -> p a e", a=2),
                                c_row, ALU.mult).then_inc(bias_step, 1)
                V.scalar_tensor_tensor(out=p_bias[32:33, :], in0=pb_in[32:33, :], scalar=P_UP,
                                       in1=p_bias[32:33, :], op0=ALU.mult, op1=ALU.subtract).then_inc(w_ready, 1)

            def biases():
                dve.wait_ge(bias_step, 3)
                dve.wait_ge(rot_cross, 2 * EC + 2)
                V.tensor_tensor(b_r1, b_r1, b_r2, ALU.add).then_inc(bias_step, 1)

            def bias_ready():
                dve.wait_ge(bias_cols, 1)
                V.tensor_scalar(qk_bias[:, :], down[:, 0:2 * EC], W_UP, None, ALU.mult).then_inc(w_ready, 1)

            def projection_weights():
                dve.wait_ge(wp_hi, 1)
                for c in range(EC):
                    last_op = V.scalar_tensor_tensor(out=wp[:, LO, c, :], in0=x1[:, c, :], scalar=W_UP,
                                                     in1=wp[:, HI, c, :], op0=ALU.mult, op1=ALU.subtract)
                last_op.then_inc(w_ready, 1)

            def iteration(j, prev, here, nxt, setup):
                G, g0 = general_plan(prev, here, nxt, setup), general_base(j)
                S, s0 = score_plan(here, nxt), score_base(j)

                def bank_of(name, n):
                    return gen[general_bank(j, G[name, n])]

                def blocks(bank, n=PARTS):
                    return bank[:, :].rearrange("p (c t) -> p c t", t=n)

                def magnitude(m):
                    dve.wait_ge(g_sums, PIECES * (m + 1))
                    V.tensor_reduce(gt[:, m:m + 1], gs[:, PIECES * m:PIECES * (m + 1)], AX.X, ALU.add
                                    ).then_inc(g_step, 1)

                def thresholds(m):
                    s0 = 1 + 5 * m
                    dve.wait_ge(g_total, m + 1)
                    V.tensor_scalar(gam[:, m:m + 1], down[:, m:m + 1], 1.0 / (F * E), None, ALU.mult
                                    ).then_inc(g_step, 1)
                    dve.wait_ge(g_step, s0 + 1)
                    V.tensor_scalar(theta[:, m, 0:1], gam[:, m:m + 1], EPS_BIT, 0.5, ALU.add, ALU.mult
                                    ).then_inc(g_step, 1)
                    V.tensor_scalar(theta[:, m, 1:2], gam[:, m:m + 1], EPS_BIT, -0.5, ALU.add, ALU.mult
                                    ).then_inc(g_step, 1)
                    V.tensor_tensor(g_sq[:, m:m + 1], gam[:, m:m + 1], gam[:, m:m + 1], ALU.mult).then_inc(g_step, 1)
                    dve.wait_ge(g_step, s0 + 4)
                    if m == 1:
                        V.reciprocal(g_sq[:, 0:1], g_sq[:, 1:2]).then_inc(g_step, 1)
                        dve.wait_ge(g_step, s0 + 5)
                        V.tensor_scalar(c_fin[:, :], g_sq[:, 0:1], EPS_LN, None, ALU.mult).then_inc(g_step, 1)
                        dve.wait_ge(g_step, s0 + 6)

                def ternary(pair):
                    for k in range(2):
                        m, u = divmod(2 * pair + k, FC)
                        if m == 0 and k == 1:
                            if pair:
                                dve.wait_ge(tern_ready, 2 * pair)
                            V.tensor_scalar(below[:, 1, :], stage[:, E * u:E * (u + 1)], theta[:, 0, 1:2], None,
                                            ALU.is_lt).then_inc(dve_half, 1)
                            dve.wait_ge(dve_half, pair + 1)
                        else:
                            dve.wait_ge(tern_half, pair + 1 if m == 0 else 2 * pair + k + 1 - PAIRS)
                        if pair and k == 0:
                            dve.wait_ge(sign_full, pair)
                        V.scalar_tensor_tensor(out=t16[:, k, :], in0=stage[:, E * u:E * (u + 1)],
                                               scalar=theta[:, m, 0:1], in1=below[:, k, :], op0=ALU.is_gt,
                                               op1=ALU.subtract).then_inc(tern_ready, 1)

                def hidden_low(u):
                    dve.wait_ge(h_full, FC * (j - 1) + u + 1)
                    low(hT[:, LO, u, :], bank_of("up", u)[:, :], hT[:, HI, u, :]).then_inc(g_drained, 1)

                def maxima(u, ahead=0, in_general=False):
                    if in_general:
                        dve.wait_ge(g_full, g0 + G["next max", 3 * u + 2] + 1)
                    else:
                        dve.wait_ge(s_full, s0 + S["next max" if ahead else "max", u] + 3)
                    V.tensor_copy(wait_copy[:, :], mhalf[:, 0:1])
                    for i, tbs in enumerate(((3,), (0, 2), (1,))):
                        bank = bank_of("next max", 3 * u + i) if in_general else score[i]
                        at = 0
                        for tb in tbs:
                            n = PARTS * (tb + 1)
                            part = bank[:, at:at + n]
                            op = V.tensor_tensor_reduce(part, part, mask_rows[:, T - n:T], 1.0, -3.0e38, ALU.add,
                                                        ALU.max, mx[:, TB * u + tb:TB * u + tb + 1])
                            at += n
                        op.then_inc(g_drained if in_general else s_drained, 1)

                def halve_maxima():
                    bank = bank_of("shift", 0)
                    dve.wait_ge(g_full, g0 + G["shift", 0] + 1)
                    V.tensor_scalar(m_f[:, :], bank[0:HEADS * TB, 0:PARTS], -1.0 / ROW_UP, P_LIFT * S_UP / ROW_UP,
                                    ALU.mult, ALU.add).then_inc(m_neg, 1)
                    dve.wait_ge(m_neg, j + 1)
                    V.tensor_copy(m_half[:, HI, :], m_f[:, :]).then_inc(m_hi, 1)
                    dve.wait_ge(m_hi, j + 1)
                    low(m_half[:, LO, :], m_f[:, :], m_half[:, HI, :]).then_inc(g_drained, 1)

                def moments(ln, tb):
                    V.tensor_scalar(negm[:, ln, tb:tb + 1], bn[:, ln, tb, 1:2], bn[:, ln, tb, 4:5], -0.5,
                                    ALU.add, ALU.mult)
                    V.bn_aggr(mv[:, ln, tb, :], bn[:, ln, tb, :]).then_inc(mv_done[ln], 1)

                def terms(ln, tbs, *var_ops):
                    V.tensor_scalar(veps[:, ln, tbs], mv[:, ln, tbs, 1], *var_ops).then_inc(ln_terms[ln], 1)

                def x_moments(tb):
                    if tb == 0:
                        dve.wait_ge(x_in, 16 * (j + 2))
                    V.bn_stats(bn[:, LX, tb, :], xo[:, tb, :]).then_inc(bn_done[LX], 1)
                    dve.wait_ge(bn_done[LX], TB * (j + 1) + tb + 1)
                    moments(LX, tb)
                    if tb == TB - 1:
                        dve.wait_ge(mv_done[LX], TB * (j + 2))
                        terms(LX, slice(0, TB), EPS_LN, None, ALU.add)

                def hidden_mean():
                    dve.wait_ge(hsum_full, j)
                    if not here:
                        dve.wait_ge(hsq_full, j)
                    V.tensor_scalar(h_negm[:, :], pv[:, H_SUM:H_SUM + TB], -1.0 / F, None, ALU.mult
                                    ).then_inc(h_step, 1)
                    dve.wait_ge(h_step, 3 * (j - 1) + 1)

                def hidden_variance():
                    if here:
                        dve.wait_ge(pv_full, HEADS * j + SQUARES_AT + 1)
                    dve.wait_ge(hsq_full, j)
                    V.tensor_tensor(h_msq[:, :], h_negm[:, :], h_negm[:, :], ALU.mult).then_inc(h_step, 1)
                    dve.wait_ge(h_step, 3 * (j - 1) + 2)
                    V.scalar_tensor_tensor(out=h_var[:, :], in0=pv[:, H_SQ:H_SQ + TB], scalar=1.0 / F,
                                           in1=h_msq[:, :], op0=ALU.mult, op1=ALU.subtract).then_inc(h_step, 1)
                    dve.wait_ge(h_step, 3 * (j - 1) + 3)
                    V.tensor_scalar(e_fin[:, :], h_var[:, :], EPS_BIT, c_fin[:, 0:1], ALU.add, ALU.mult
                                    ).then_inc(h_terms, 1)

                def final(tb):
                    n = TB * (j - 1) + tb
                    dve.wait_ge(down_full, n + 1)
                    need(dve, stored[tb % 2], 16 * (2 * (j - 1) + tb // 2))
                    V.scalar_tensor_tensor(out=xn[:, tb % 2, :], in0=c_sum[:, :], scalar=h_negm[:, tb:tb + 1],
                                           in1=down[:, :], op0=ALU.mult, op1=ALU.add).then_inc(down_drained, 1)

                def final_moments(tb):
                    n = TB * (j - 1) + tb
                    dve.wait_ge(down_drained, n + 1)
                    V.bn_stats(bn[:, LF, tb, :], xn[:, tb % 2, :]).then_inc(bn_done[LF], 1)
                    dve.wait_ge(bn_done[LF], n + 1)
                    moments(LF, tb)

                def final_terms(tb):
                    n = TB * (j - 1) + tb
                    if tb == 0:
                        dve.wait_ge(h_terms, j)
                    dve.wait_ge(mv_done[LF], n + 1)
                    V.tensor_tensor(veps[:, LF, tb:tb + 1], mv[:, LF, tb, 1:2], e_fin[:, tb:tb + 1], ALU.add
                                    ).then_inc(ln_terms[LF], 1)

                def x_low(tb):
                    dve.wait_ge(xT_hi, TB * (j + 1) + tb + 1)
                    cols = slice(PARTS * tb, PARTS * (tb + 1))
                    low(xT[:, LO, :, cols], blocks(bank_of("xT", tb)), xT[:, HI, :, cols]).then_inc(g_drained, 1)

                def v_low(tb):
                    dve.wait_ge(v_hi, TB * (j + 1) + tb + 1)
                    low(v_sb[:, tb, :, HD + 1:VW], blocks(bank_of("v", tb), HD), v_sb[:, tb, :, 0:HD]
                        ).then_inc(g_drained, 1)

                def qk_low(g, which):
                    dve.wait_ge(qk_hi, 8 * (j + 1) + 2 * g + which + 1)
                    V.scalar_tensor_tensor(out=qkn[:, g % 2, 3 * which, :], in0=bank_of("qk", (g, which))[:, :],
                                           scalar=qk_bias[:, EC * which + g:EC * which + g + 1],
                                           in1=qkn[:, g % 2, 1 + which, :], op0=ALU.add, op1=ALU.subtract
                                           ).then_inc(g_drained, 1)

                def probs_low(h):
                    for i, n in enumerate(SCORE_W):
                        dve.wait_ge(exp_full, 48 * j + 3 * h + i + 1)
                        at = 512 * i
                        low(probs[:, h % 2, LO, at:at + n], score[i][:, 0:n], probs[:, h % 2, HI, at:at + n]
                            ).then_inc(s_drained, 1)

                def head_output(h):
                    n = HEADS * j + h
                    dve.wait_ge(pv_full, n + 1)
                    res = pv[:, 0:VW * TB].rearrange("p (b w) -> p b w", b=TB)
                    V.reciprocal(r_sum[:, :], res[:, :, HD]).then_inc(o_recip, 1)
                    pairs = bass.AP(pv, 0, [[512, PARTS], [VW, TB], [1, HD], [HD + 1, 2]])
                    V.tensor_reduce(oA[:, :, :], pairs, AX.X, ALU.add).then_inc(pv_drained, 1)
                    if h == 0 and nxt:
                        dve.wait_ge(xn_ready, TB * (j + 2))
                    dve.wait_ge(o_recip, n + 1)
                    dve.wait_ge(pv_drained, n + 1)
                    V.tensor_tensor(xo[:, :, HD * h:HD * (h + 1)], oA[:, :, :],
                                    r_sum[:, :].unsqueeze(2).to_broadcast([PARTS, TB, HD]), ALU.mult
                                    ).then_inc(o_ready, 1)

                def o_low(tb):
                    dve.wait_ge(oT_hi, TB * j + tb + 1)
                    low(oT[:, tb % 2, LO, :, :], blocks(bank_of("oT", tb)), oT[:, tb % 2, HI, :, :]
                        ).then_inc(g_drained, 1)

                def y_moments(tb):
                    n = TB * j + tb
                    dve.wait_ge(y_copied, n + 1)
                    V.bn_stats(bn[:, LP, tb, :], bank_of("proj", tb)[:, :]).then_inc(g_drained, 1)
                    dve.wait_ge(g_drained, g0 + G["proj", tb] + 1)
                    moments(LP, tb)
                    dve.wait_ge(mv_done[LP], n + 1)
                    terms(LP, slice(tb, tb + 1), EPS_LN / PROJ_K ** 2, None, ALU.add)

                def first_sum(tb):
                    n = TB * j + tb
                    dve.wait_ge(xb_ready, n + 1)
                    V.scalar_tensor_tensor(out=x1[:, tb, :], in0=y_sb[:, tb % 2, :], scalar=rstd[:, LP, tb:tb + 1],
                                           in1=xres[:, tb, :], op0=ALU.mult, op1=ALU.add).then_inc(x1_ready, 1)
                    dve.wait_ge(x1_ready, n + 1)
                    V.bn_stats(bn[:, L1, tb, :], x1[:, tb, :]).then_inc(bn_done[L1], 1)
                    dve.wait_ge(bn_done[L1], n + 1)
                    moments(L1, tb)
                    dve.wait_ge(mv_done[L1], n + 1)
                    terms(L1, slice(tb, tb + 1), 1.0 + EPS_BIT, EPS_LN * EPS_BIT, ALU.mult, ALU.add)

                def x2_low(tb):
                    dve.wait_ge(x2T_hi, TB * j + tb + 1)
                    cols = slice(PARTS * tb, PARTS * (tb + 1))
                    low(x2T[:, LO, :, cols], blocks(bank_of("x2T", tb)), x2T[:, HI, :, cols]).then_inc(g_drained, 1)

                for u in range(FC):
                    if setup and u in PAIR_AT:
                        ternary(PAIR_AT[u])
                    if here and u in MAX_AT:
                        maxima(MAX_AT[u])
                    if here and u == SHIFT_AT:
                        halve_maxima()
                    if prev:
                        hidden_low(u)
                    if nxt and u < TB:
                        x_moments(u)
                    if nxt and not here and u == X_NORM_AT:
                        rotation(0)
                        rotation(1)
                    if nxt and u in X_AT:
                        x_low(X_AT[u])
                if prev:
                    hidden_mean()
                    if not here:
                        hidden_variance()
                if here:
                    probs_low(0)
                if prev:
                    final(0)
                    final_moments(0)
                    if not here:
                        final_terms(0)
                if nxt and not here:
                    value_weights()
                    for c in range(EC):
                        dve.wait_ge(rot_step, c + 1)
                        dve.wait_ge(rot_cross, 2 * c + 2)
                        V.tensor_tensor(rot1[:, c % 2, :], rot1[:, c % 2, :], rot2[:, c % 2, :], ALU.add
                                        ).then_inc(rot_done, 1)
                        if c >= 1:
                            rotated_low(c - 1)
                            if c + 1 < EC:
                                rotation(c + 1)
                            v_low(c - 1)
                    rotated_low(EC - 1)
                    biases()
                    v_low(TB - 1)
                    bias_ready()
                for h in range(HEADS):
                    if setup and h == 2:
                        magnitude(1)
                    if nxt and h in QK_AT:
                        if not here and QK_AT[h] == (3, 1):
                            magnitude(0)
                        qk_low(*QK_AT[h])
                    if nxt and not here and h in FIRST_MAX:
                        maxima(FIRST_MAX[h], 1)
                    if nxt and not here and h == 3:
                        projection_weights()
                    if prev and h in FINAL_AT:
                        final(FINAL_AT[h])
                    if prev and here and h == SQUARES_AT:
                        hidden_variance()
                        final_terms(0)
                    if here:
                        if nxt and h in STEP_MAX:
                            maxima(STEP_MAX[h], 1, in_general=True)
                        head_output(h)
                        if h + 1 < HEADS:
                            probs_low(h + 1)
                    if prev and h in FINAL_AT:
                        final_moments(FINAL_AT[h])
                        final_terms(FINAL_AT[h])
                    if setup and h == 2:
                        thresholds(1)
                    if setup and h + 1 in PAIR2_AT:
                        ternary(PAIR2_AT[h + 1])
                if nxt and not here:
                    thresholds(0)
                    dve.wait_ge(k_rows, 16)
                    for pair in range(PAIRS_BEFORE):
                        ternary(pair)
                        maxima(len(FIRST_MAX) + pair, 1)
                if prev and not here:
                    final(3)
                    final_moments(3)
                    final_terms(3)
                if here:
                    if nxt:
                        v_low(0)
                    o_low(0)
                    o_low(1)
                    if nxt:
                        maxima(LATE_MAX, 1)
                    if prev:
                        final(3)
                        final_moments(3)
                        final_terms(3)
                    y_moments(0)
                    o_low(2)
                    y_moments(1)
                    o_low(3)
                    first_sum(0)
                    y_moments(2)
                    first_sum(1)
                    y_moments(3)
                    first_sum(2)
                    if nxt:
                        v_low(1)
                    x2_low(0)
                    first_sum(3)
                    if nxt:
                        v_low(2)
                    x2_low(1)
                    if nxt:
                        v_low(3)
                    x2_low(2)
                    x2_low(3)
                if setup:
                    dve.wait_ge(c_full, 1)
                    V.tensor_copy(c_sum[:, :], down[:, :]).then_inc(c_ready, 1)

            run(dve, iteration)

        @block.gpsimd
        def _(pool):
            P = nc.gpsimd
            n_const = [0]

            def const(op):
                op.then_inc(consts, 1)
                n_const[0] += 1

            const(P.memset(ident32[:, :], 0.0))
            const(P.memset(mask_rows[:, :], 0.0))
            const(P.memset(m_stage, 0.0))
            const(P.memset(ones16[:, :], 1.0))
            const(P.memset(ones32[:, :], 1.0))
            const(P.memset(lift[:, :], BIAS_UP))
            const(P.memset(mhalf[:, :], -0.5))
            const(P.memset(mx[:, :], 0.0))
            const(P.memset(t16[:, 0, :], ROW_UP))
            const(P.memset(v_sb[:, :, :, HD:HD + 1], 1.0))
            P.memset(temp[:, 7168:8192], 0.0).then_inc(rows_zero, 1)
            pool.wait_ge(consts, 3)
            const(P.affine_select(out=ident32[:, :], in_=ident32[:, :], compare_op=ALU.not_equal, fill=1.0, base=0,
                                  pattern=[[-1, PARTS]], channel_multiplier=1))
            const(P.affine_select(out=mask_rows[:, 3 * PARTS:T], in_=mask_rows[:, 3 * PARTS:T], compare_op=ALU.is_ge,
                                  fill=NEG, base=0, pattern=[[-1, PARTS]], channel_multiplier=1))
            const(P.affine_select(out=m_stage, in_=m_stage, compare_op=ALU.is_ge, fill=NEG, base=0,
                                  pattern=[[1, PARTS]], channel_multiplier=-1))
            assert n_const[0] == CONSTS
            def crossed(out, w, n):
                o2 = out.rearrange("p (a e two) -> p a e two", a=2, two=2)
                w2 = w.rearrange("p (a e two) -> p a e two", a=2, two=2)
                s2 = rope_sb[0:n, E:2 * E].rearrange("p (e two) -> p e two", two=2)
                for k in range(2):
                    sin = s2[:, :, k].unsqueeze(1).to_broadcast([n, 2, E // 2])
                    P.tensor_tensor(o2[:, :, :, k], w2[:, :, :, 1 - k], sin, ALU.mult).then_inc(rot_cross, 1)

            def crossed_weights():
                pool.wait_ge(rope_in, 16)
                for c in range(EC):
                    pool.wait_ge(wqk_in[c], 16)
                    if c >= 2:
                        pool.wait_ge(rot_done, c - 1)
                    crossed(rot2[:, c % 2, :], wa_in[:, c, 0:2 * E], PARTS)
                pool.wait_ge(rows_in, 80)
                crossed(b_r2, b_row, 1)

            def iteration(j, prev, here, nxt, setup):
                G, g0 = general_plan(prev, here, nxt, setup), general_base(j)
                S, s0 = score_plan(here, nxt), score_base(j)

                def power(ln, tbs, terms_n, n):
                    pool.wait_ge(ln_terms[ln], terms_n)
                    width = tbs.stop - tbs.start
                    P.tensor_tensor(rstd[:, ln, tbs], veps[:, ln, tbs], mhalf[:, 0:width], ALU.pow
                                    ).then_inc(ln_pow[ln], 1)
                    pool.wait_ge(ln_pow[ln], n)
                    P.tensor_tensor(shift[:, ln, tbs], negm[:, ln, tbs], rstd[:, ln, tbs], ALU.mult
                                    ).then_inc(ln_ready[ln], 1)

                def power1(ln, b, tb):
                    n = TB * b + tb + 1
                    power(ln, slice(tb, tb + 1), n, n)

                def squares(u):
                    if not here:
                        if u:
                            pool.wait_ge(h_full, FC * (j - 1) + u + 1)
                            if u >= 2:
                                pool.wait_ge(sq_step, SQ_STEPS * (j - 1) + u - 1)
                            P.tensor_tensor(acc[:, :], acc[:, :], xn[:, u % 2, :], ALU.add).then_inc(sq_step, 1)
                        return
                    pool.wait_ge(g_drained, g0 + G["up", u] + 1)
                    n = SQ_STEPS * (j - 1) + 3 * u
                    if u:
                        pool.wait_ge(sq_step, n)
                    whole = acc_add if u else acc
                    P.tensor_tensor(whole[:, :], hT[:, HI, u, :], hT[:, LO, u, :], ALU.add).then_inc(sq_step, 1)
                    pool.wait_ge(sq_step, n + 1)
                    P.tensor_tensor(whole[:, :], whole[:, :], whole[:, :], ALU.mult).then_inc(sq_step, 1 if u else 2)
                    if u:
                        pool.wait_ge(sq_step, n + 2)
                        P.tensor_tensor(acc[:, :], acc[:, :], acc_add[:, :], ALU.add).then_inc(sq_step, 1)

                def under(n):
                    m, u = divmod(n, FC)
                    if u == 0:
                        pool.wait_ge(g_step, 5 * m + 4)
                    if n >= 2:
                        pool.wait_ge(tern_ready, n - 1)
                    P.tensor_scalar(below[:, n % 2, :], stage[:, E * u:E * (u + 1)], theta[:, m, 1:2], None,
                                    ALU.is_lt).then_inc(tern_half, 1)

                def finish(tb):
                    n = TB * (j - 1) + tb
                    pool.wait_ge(fin_ready, n + 1)
                    P.tensor_tensor(xn[:, tb % 2, :], xn[:, tb % 2, :], x1[:, tb, :], ALU.add).then_inc(out_ready, 1)

                for u in range(FC):
                    if prev:
                        squares(u)
                    if setup and u in PAIR_AT:
                        under(2 * PAIR_AT[u])
                    if nxt and u == (5 if setup else 2):
                        power(LX, slice(0, TB), j + 2, j + 2)
                if nxt and not here:
                    crossed_weights()
                    for n in range(0, 2 * PAIRS_BEFORE, 2):
                        under(n)
                if setup:
                    for n in range(FC, 2 * FC):
                        under(n)
                if prev:
                    for tb in range(TB):
                        power1(LF, j - 1, tb)
                        finish(tb)
                if here:
                    power1(LP, j, 0)
                    power1(LP, j, 1)
                    power1(L1, j, 0)
                    power1(LP, j, 2)
                    power1(L1, j, 1)
                    power1(LP, j, 3)
                    power1(L1, j, 2)
                    power1(L1, j, 3)

            run(pool, iteration)


def rope_table():
    freqs = (np.float32(THETA) ** (-(np.arange(0, HD, 2, dtype=np.float32) / np.float32(HD)))).astype(np.float32)
    angle = np.outer(np.arange(HEADS, dtype=np.float32), freqs).astype(np.float32)
    cos = np.repeat(np.cos(angle), 2, axis=1).reshape(1, E)
    sin = np.stack([-np.sin(angle), np.sin(angle)], axis=-1).reshape(1, E)
    return np.concatenate([cos, sin], axis=1).astype(np.float32)


def kernel(L0_attn_x, L0_attn_w_attn, L0_attn_b_attn, L0_attn_w_proj, L0_attn_b_proj, L0_ffn_w_fc, L0_ffn_w_proj):
    import concourse.bacc as bacc
    from concourse.bass_utils import run_bass_kernel_spmd

    arrays = {
        "x": np.ascontiguousarray(L0_attn_x).reshape(BATCHES * T, E),
        "w_attn": np.ascontiguousarray(L0_attn_w_attn),
        "b_attn": np.ascontiguousarray(L0_attn_b_attn).reshape(1, 3 * E),
        "w_proj": np.ascontiguousarray(L0_attn_w_proj),
        "b_proj": np.ascontiguousarray(L0_attn_b_proj).reshape(1, E),
        "w_fc": np.ascontiguousarray(L0_ffn_w_fc),
        "w_down": np.ascontiguousarray(L0_ffn_w_proj),
        "rope": rope_table(),
    }
    nc = bacc.Bacc("TRN2", target_bir_lowering=False, num_devices=1)
    args = [nc.dram_tensor(n, a.shape, mybir.dt.float32, kind="ExternalInput").ap() for n, a in arrays.items()]
    out = nc.dram_tensor("out", (BATCHES * T, E), mybir.dt.float32, kind="ExternalOutput").ap()
    build(nc, *args, out)
    result = run_bass_kernel_spmd(nc, [arrays], core_ids=[0])
    return result.results[0]["out"].reshape(BATCHES, T, E)
```
